# Optimizing a Trainium2 kernel written in Bass

```python
import numpy as np
import jax
import jax.numpy as jnp

def _softmax(x, axis=-1):
    return jax.nn.softmax(x, axis=axis)

def _gelu(x):
    return jax.nn.gelu(x, approximate=True)

def _silu(x):
    return jax.nn.silu(x)

def _sigmoid(x):
    return jax.nn.sigmoid(x)

def _layernorm(x, axis=-1, eps=1e-05):
    m = jnp.mean(x, axis=axis, keepdims=True)
    v = jnp.var(x, axis=axis, keepdims=True)
    return (x - m) / jnp.sqrt(v + eps)

def _scatter_add(tgt, idx, src, axis=0):
    return tgt.at[idx].add(src)

def _segment_sum(src, seg, n):
    return jax.ops.segment_sum(src, seg, n)
kernel_name = 'mk_adj_preln_d2_adj_r2_f7a256'

def setup_inputs(seed: int=0):
    np.random.seed(seed)
    _w = jnp.asarray

    def _rec_inputs():
        import jax
        import jax.numpy as jnp
        _gk = jax.random.key(seed)
        x = 7.22e-05 + 1 * jax.random.normal(jax.random.fold_in(_gk, 1), (4096, 512), jnp.float32)
        _a = jax.random.bernoulli(jax.random.fold_in(_gk, 2), 0.00195312, (4096, 4096))
        _a = jnp.logical_or(_a, jnp.swapaxes(_a, -1, -2))
        _a = jnp.logical_or(_a, jnp.eye(4096, dtype=bool))
        _af = _a.astype(jnp.float32)
        adj = _af
        return (x, adj)
    x, adj = _rec_inputs()

    def _L0_gnn_setup():
        import jax, jax.numpy as jnp
        import numpy as np
        N = 4096
        D = 512
        key = jax.random.key(seed)
        ks = jax.random.split(key, 13)
        w_scale = 1.0 / np.sqrt(D)
        inp = {'query': jax.random.normal(ks[0], (N, D), dtype=jnp.float32), 'key': jax.random.normal(ks[1], (N, D), dtype=jnp.float32), 'value': jax.random.normal(ks[2], (N, D), dtype=jnp.float32), 'adj_matrix': jax.random.randint(ks[3], (N, N), 0, 2).astype(jnp.float32), 'Wq': jax.random.normal(ks[4], (D, D), dtype=jnp.float32) * w_scale, 'bq': jax.random.normal(ks[5], (D,), dtype=jnp.float32) * 0.01, 'Wk': jax.random.normal(ks[6], (D, D), dtype=jnp.float32) * w_scale, 'bk': jax.random.normal(ks[7], (D,), dtype=jnp.float32) * 0.01, 'Wv': jax.random.normal(ks[8], (D, D), dtype=jnp.float32) * w_scale, 'bv': jax.random.normal(ks[9], (D,), dtype=jnp.float32) * 0.01, 'Wm': jax.random.normal(ks[10], (D, D), dtype=jnp.float32) * w_scale, 'bm': jax.random.normal(ks[11], (D,), dtype=jnp.float32) * 0.01}
        return inp
    _L0_gnn_all = _L0_gnn_setup()
    _L0_gnn_in = {k: v for k, v in _L0_gnn_all.items() if k in ('key', 'value', 'Wq', 'bq', 'Wk', 'bk', 'Wv', 'bv', 'Wm', 'bm')}
    del _L0_gnn_all

    def _L1_gnn_setup():
        import jax, jax.numpy as jnp
        import numpy as np
        N = 4096
        IN_FEATURES = 512
        OUT_FEATURES = 512
        key = jax.random.key(seed)
        k_x, k_adj, k_w, k_b = jax.random.split(key, 4)
        x = jax.random.normal(k_x, (N, IN_FEATURES), dtype=jnp.float32)
        adj = jax.random.uniform(k_adj, (N, N), dtype=jnp.float32)
        stdv = 1.0 / np.sqrt(OUT_FEATURES)
        weight = jax.random.uniform(k_w, (IN_FEATURES, OUT_FEATURES), dtype=jnp.float32, minval=-stdv, maxval=stdv)
        bias = jax.random.uniform(k_b, (OUT_FEATURES,), dtype=jnp.float32, minval=-stdv, maxval=stdv)
        return {'x': x, 'adj': adj, 'weight': weight, 'bias': bias}
    _L1_gnn_all = _L1_gnn_setup()
    _L1_gnn_in = {k: v for k, v in _L1_gnn_all.items() if k in ('weight', 'bias')}
    del _L1_gnn_all
    return {'x': x, 'adj': adj, 'L0_gnn_key': _L0_gnn_in['key'], 'L0_gnn_value': _L0_gnn_in['value'], 'L0_gnn_Wq': _L0_gnn_in['Wq'], 'L0_gnn_bq': _L0_gnn_in['bq'], 'L0_gnn_Wk': _L0_gnn_in['Wk'], 'L0_gnn_bk': _L0_gnn_in['bk'], 'L0_gnn_Wv': _L0_gnn_in['Wv'], 'L0_gnn_bv': _L0_gnn_in['bv'], 'L0_gnn_Wm': _L0_gnn_in['Wm'], 'L0_gnn_bm': _L0_gnn_in['bm'], 'L1_gnn_weight': _L1_gnn_in['weight'], 'L1_gnn_bias': _L1_gnn_in['bias']}

def reference(x, adj, L0_gnn_key, L0_gnn_value, L0_gnn_Wq, L0_gnn_bq, L0_gnn_Wk, L0_gnn_bk, L0_gnn_Wv, L0_gnn_bv, L0_gnn_Wm, L0_gnn_bm, L1_gnn_weight, L1_gnn_bias):
    import jax
    import jax.numpy as jnp

    def _L0_gnn_ref(query, key, value, adj_matrix, Wq, bq, Wk, bk, Wv, bv, Wm, bm):
        import jax, jax.numpy as jnp
        import numpy as np
        N = 4096
        D = 512
        q = query @ Wq.T + bq
        k = key @ Wk.T + bk
        v = value @ Wv.T + bv
        scale = q.shape[0] ** 0.5
        scores = jnp.einsum('nd,md->nm', q, k) / scale
        adj_scores = scores * adj_matrix
        adj_scores = jnp.where(jnp.abs(adj_scores) < 1e-05, -1000000000.0, adj_scores)
        prob = jax.nn.softmax(adj_scores, axis=-1)
        x = jnp.einsum('nm,md->nd', prob, v)
        return x @ Wm.T + bm

    def _L1_gnn_ref(x, adj, weight, bias):
        import jax, jax.numpy as jnp
        import numpy as np
        N = 4096
        IN_FEATURES = 512
        OUT_FEATURES = 512
        support = jnp.matmul(x, weight)
        output = jnp.matmul(adj, support)
        return output + bias
    h = jnp.maximum(_layernorm(x, axis=-1), 0.0)
    x = x + _L0_gnn_ref(h, L0_gnn_key, L0_gnn_value, adj, L0_gnn_Wq, L0_gnn_bq, L0_gnn_Wk, L0_gnn_bk, L0_gnn_Wv, L0_gnn_bv, L0_gnn_Wm, L0_gnn_bm)
    h = jnp.maximum(_layernorm(x, axis=-1), 0.0)
    x = x + _L1_gnn_ref(h, adj, L1_gnn_weight, L1_gnn_bias)
    return x

_drawn_inputs = setup_inputs


def setup_inputs(seed=0):
    import zlib

    import numpy as np

    out = dict(_drawn_inputs(seed))
    spreads = {}
    factors = {'L0_gnn_bq': 64.0,
     'L0_gnn_bk': 64.0,
     'L0_gnn_bv': 5.008,
     'L0_gnn_bm': 4.352,
     'L1_gnn_bias': 8.0}
    for name, (base, spread) in spreads.items():
        noise = np.random.default_rng([zlib.crc32(name.encode()), seed]).standard_normal(out[name].shape)
        drawn = base * np.exp(spread * noise) if base else spread * noise
        out[name] = jnp.asarray(drawn.astype(out[name].dtype))
    for name, factor in factors.items():
        out[name] = (out[name] * factor).astype(out[name].dtype)
    return out
```

```python
import concourse.bass as bass
from concourse import mybir

F32 = mybir.dt.float32
F16 = mybir.dt.float16
BF16 = mybir.dt.bfloat16
I32 = mybir.dt.int32
ALU = mybir.AluOpType
ACT = mybir.ActivationFunctionType
AX_X = mybir.AxisListType.X
AX_XY = mybir.AxisListType.XY
RMAX = bass.bass_isa.ReduceOp.max
RADD = bass.bass_isa.ReduceOp.add

P = 128
N = 4096
D = 512
DB = D // P
NT = N // P
GT = 4
NG = NT // GT
CH = N // D
HC = CH // 2
SC = N // HC
TG = NT // 4
KB = 1024

EPS = 1e-5
NEAR_ZERO = 1e-5
MASKED = -1e9
H_SCALE = 256.0
P_SHIFT = 9.0
TOP = 2.0 ** 14
SCORE_DIV = float(N) ** 0.5
EXPONENT_BITS = 0x7F800000
SUPPORT_SCALE = 1.0 / (H_SCALE * D)


def wait_from(eng, sem, count):
    if not isinstance(count, int) or count > 0:
        eng.wait_ge(sem, count)


class Chain:

    def __init__(self, eng, sem):
        self.eng, self.sem, self.base, self.k = eng, sem, 0, 0

    def mark(self, ins):
        self.k += 1
        return ins.then_inc(self.sem, 1)

    def settle(self):
        self.eng.wait_ge(self.sem, self.base + self.k)

    def rebase(self, base):
        self.base, self.k = base, 0


def program(nc, x, adj, key, value, wq, bq, wk, bk, wv, bv, wm, bm, w1, b1, out):
    from contextlib import ExitStack
    ctx = ExitStack()
    with ctx:
        def sb(name, shape, dt):
            return ctx.enter_context(nc.sbuf_tensor(name, shape, dt))

        def sem(name):
            return ctx.enter_context(nc.semaphore(name))

        q_scr = nc.dram_tensor("q_scr", (NT, P, 2 * DB * P), F16, kind="Internal").ap()
        w2_scr = nc.dram_tensor("w2_scr", (P, DB * 2 * D), F16, kind="Internal").ap()
        w1_scr = nc.dram_tensor("w1_scr", (P, DB * 2 * D), F16, kind="Internal").ap()
        o_scr = nc.dram_tensor("o_scr", (N, D), F32, kind="Internal").ap()
        x1_scr = nc.dram_tensor("x1_scr", (N, D), F32, kind="Internal").ap()

        KR = sb("key_region", [P, 16 * KB], F32)
        VR = sb("value_region", [P, 16 * KB], F32)
        R = sb("work_region", [P, 18 * KB], F32)

        def view(region, kb, size_kb, dt):
            w = region[:, kb * KB // 4:(kb + size_kb) * KB // 4]
            return w if dt == F32 else w.bitcast(dt)

        KT = view(KR, 0, 64, F16).rearrange("p (h a n) -> p h a n", h=2, a=DB)
        VV = view(VR, 0, 64, F16).rearrange("p (t h d) -> p t h d", h=2, d=D)
        def wview(kb):
            return view(VR, kb, 8, F32).rearrange("p (a d) -> p a d", a=DB)
        wq_s, wk_s, wv_s, wm_s, wmT, m32, w232, w1_s = [wview(8 * n) for n in range(8)]
        bkb = view(R, 0, 2, F32).rearrange("p (a n) -> p a n", a=DB)
        bvb = view(R, 2, 2, F32).rearrange("p (a n) -> p a n", a=DB)
        bm_b = view(R, 4, 2, F32)
        w2hl = view(R, 8, 8, F16).rearrange("p (a h d) -> p a h d", a=DB, h=2)
        w1hl = view(R, 16, 8, F16).rearrange("p (a h d) -> p a h d", a=DB, h=2)
        kv_in = [view(R, 56 + 8 * n, 8, F32).rearrange("p (s d) -> p s d", s=GT) for n in range(2)]
        xg = view(R, 0, 8, F32).rearrange("p (s d) -> p s d", s=GT)
        hhl = view(R, 8, 8, F16).rearrange("p (h s d) -> p h s d", h=2, s=GT)
        hT = view(R, 16, 8, F16).rearrange("p (h a n) -> p h a n", h=2, a=DB)
        q32 = view(R, 24, 4, F32).rearrange("p (b n) -> p b n", b=2)
        u_b = view(R, 28, 2, F32)
        junk = view(R, 12, 4, BF16).rearrange("p (s d) -> p s d", s=GT)
        khl = view(R, 32, 8, F16).rearrange("p (h s d) -> p h s d", h=2, s=GT)
        qst = view(R, 40, 8, F16).rearrange("p (s h a n) -> p s h a n", s=GT, h=2, a=DB)
        mhl = view(R, 48, 8, F16).rearrange("p (a h d) -> p a h d", a=DB, h=2)
        tt = [view(R, 16 * n, 16, F32) for n in range(2)]
        phl = view(R, 32, 16, F16).rearrange("p (h m) -> p h m", h=2)
        p32 = view(R, 48, 8, F32).rearrange("p (b m) -> p b m", b=2)
        pT = view(R, 56, 4, F16).rearrange("p (b t h n) -> p b t h n", b=2, t=4, h=2)
        qT = [view(R, 64 + 2 * n, 2, F16).rearrange("p (h a n) -> p h a n", h=2, a=DB) for n in range(2)]
        o32 = view(R, 68, 2, F32)
        w2p = view(VR, 0, 8, F16).rearrange("p (a h d) -> p a h d", a=DB, h=2)
        w1p = view(VR, 8, 8, F16).rearrange("p (a h d) -> p a h d", a=DB, h=2)
        b1_b = view(VR, 16, 2, F32)
        o_in = [view(VR, 18 + 2 * n, 2, F32) for n in range(2)]
        x_in = [view(VR, 22 + 2 * n, 2, F32) for n in range(2)]
        ohl = view(VR, 26, 2, F16).rearrange("p (h d) -> p h d", h=2)
        oT = view(VR, 28, 2, F16).rearrange("p (h a n) -> p h a n", h=2, a=DB)
        x1 = view(VR, 30, 2, F32)
        xn = view(VR, 32, 2, F32)
        x1b = view(VR, 34, 2, F32)
        h2hl = view(VR, 36, 2, F16).rearrange("p (h d) -> p h d", h=2)
        h2T = view(VR, 38, 2, F16).rearrange("p (h a n) -> p h a n", h=2, a=DB)
        s32 = view(VR, 40, 2, F32)
        SUP = view(KR, 0, 64, F16).rearrange("p (t h d) -> p t h d", h=2, d=D)
        aT = view(R, 48, 4, BF16).rearrange("p (b t n) -> p b t n", b=2, t=8)
        a_bf = view(R, 32, 16, BF16).rearrange("p (b m) -> p b m", b=2)
        unequal = view(R, 52, 8, BF16)
        x1_in = [view(R, 60 + 2 * n, 2, F32) for n in range(2)]
        o_out = [view(R, 64 + 2 * n, 2, F32) for n in range(2)]
        sup32 = view(VR, 0, 64, F32).rearrange("p (t d) -> p t d", d=D)
        restT = view(R, 48, 2, F32)
        fix_in = view(R, 60, 2, F32)
        fix_out = view(R, 64, 2, F32)

        ones = sb("ones", [P, P], F32)
        ident32 = sb("ident32", [P, P], F32)
        ident16 = sb("ident16", [P, P], F16)
        identb = sb("identb", [P, P], BF16)
        b2_b = sb("b2_b", [P, D], F32)
        bcol = sb("bcol", [P, 3, DB], F32)
        cs = sb("cs", [P, DB + 1], F32)
        kmx = sb("kmx", [P, 2, NG], F32)
        mx = sb("mx", [P, 6], F32)
        gmx = sb("gmx", [P, 6], F32)
        fl = sb("fl", [P, 8], F32)
        sc = sb("sc", [P, 16], F32)
        cq = sb("cq", [P, DB], F32)
        r_s = sb("r_s", [P, NT], F32)
        stats = sb("stats", [P, GT, 6], F32)
        mv = sb("mv", [P, GT, 2], F32)
        rs = sb("rs", [P, GT], F32)
        rsum = sb("rsum", [P, HC], F32)
        rmax = sb("rmax", [P, HC], F32)
        nbias = sb("nbias", [P, 4], F32)
        linv = sb("linv", [P, 4], F32)
        miss = sb("miss", [P, NT], F32)
        miss2 = sb("miss2", [P, 2], F32)
        flag = sb("flag", [P, 1], I32)

        (G_K, G_V, G_M, G_W2, G_W1, G_Q, S_Q, S_R, S_R0, G_ALL, I_G, THR, BIG, I_O, I_S, TMP) = range(16)

        def col(n):
            return sc[:, n:n + 1]

        PS = ctx.enter_context(nc.psum_tensor("ps", [P, 8, D], F32))

        def bank(n):
            return PS[:, n, :]

        def bank16(n, dt=F16):
            return PS[:, n, :].bitcast(dt).rearrange("p (t n) -> p t n", n=P)

        wqk_in, wvm_in, w1_in, bias_in = sem("wqk_in"), sem("wvm_in"), sem("w1_in"), sem("bias_in")
        ident_zero, ident_made, cols_spread = sem("ident_zero"), sem("ident_made"), sem("cols_spread")
        weight_product, weight_evacuated = sem("weight_product"), sem("weight_evacuated")
        kscan_in, vscan_in, key_scanned, value_scanned = sem("kscan_in"), sem("vscan_in"), sem("key_scanned"), sem("value_scanned")
        maxima_made, maxima_shared, dve_own, scales_made = sem("maxima_made"), sem("maxima_shared"), sem("dve_own"), sem("scales_made")
        weight_hi, weight_lo, weights_stored = sem("weight_hi"), sem("weight_lo"), sem("weights_stored")
        x_loaded, key_loaded, value_loaded = sem("x_loaded"), sem("key_loaded"), sem("value_loaded")
        var_made, std_made, xn_made, h_hi_made, h_lo_made = [sem(s) for s in (
            "var_made", "std_made", "xn_made", "h_hi_made", "h_lo_made")]
        key_hi, key_lo, value_hi, value_lo = sem("key_hi"), sem("key_lo"), sem("value_hi"), sem("value_lo")
        keyT_made, keyT_evacuated, hT_made, hT_evacuated = sem("keyT_made"), sem("keyT_evacuated"), sem("hT_made"), sem("hT_evacuated")
        q_product, q32_made, q_hi, q_lo, q_stored = sem("q_product"), sem("q32_made"), sem("q_hi"), sem("q_lo"), sem("q_stored")
        adj_in = [sem(f"adj_in{b}") for b in range(2)]
        q_in = [sem(f"q_in{b}") for b in range(2)]
        scores_full, scores_scaled, hidden_found, scores_masked, max_chunk, shift_made = [sem(s) for s in (
            "scores_full", "scores_scaled", "hidden_found", "scores_masked", "max_chunk", "shift_made")]
        exp_made, p_hi, p_lo, pT_made, pT_evacuated = sem("exp_made"), sem("p_hi"), sem("p_lo"), sem("pT_made"), sem("pT_evacuated")
        context_full, context_made, context_stored, dve_att = sem("context_full"), sem("context_made"), sem("context_stored"), sem("dve_att")
        sum_made, inverse_made, abs_made = sem("sum_made"), sem("inverse_made"), sem("abs_made")
        proj_w_in, o_loaded, x4_loaded = sem("proj_w_in"), [sem(f"o_loaded{b}") for b in range(2)], [sem(f"x4_loaded{b}") for b in range(2)]
        o_hi, o_lo, oT_made, oT_evacuated, proj_full, proj_taken = [sem(s) for s in (
            "o_hi", "o_lo", "oT_made", "oT_evacuated", "proj_full", "proj_taken")]
        var4_made, std4_made, xn4_made, h2_hi, h2_lo, h2T_made, h2T_evacuated = [sem(s) for s in (
            "var4_made", "std4_made", "xn4_made", "h2_hi", "h2_lo", "h2T_made", "h2T_evacuated")]
        support_full, support32_made, support_hi, support_lo = [sem(s) for s in (
            "support_full", "support32_made", "support_hi", "support_lo")]
        x1b_made, x1b_stored, dve_proj = sem("x1b_made"), sem("x1b_stored"), sem("dve_proj")
        adj5_in = [sem(f"adj5_in{b}") for b in range(2)]
        x1_loaded = [sem(f"x1_loaded{b}") for b in range(2)]
        adj_rounded, adj_compared, aT_made, aT_evacuated, conv_full, out_made = [sem(s) for s in (
            "adj_rounded", "adj_compared", "aT_made", "aT_evacuated", "conv_full", "out_made")]
        out_stored = [sem(f"out_stored{b}") for b in range(2)]
        misses_summed, misses_shared, flag_made = sem("misses_summed"), sem("misses_shared"), sem("flag_made")
        sup32_made, adj6_in, rest_made, restT_made, restT_evacuated, rest_full = [sem(s) for s in (
            "sup32_made", "adj6_in", "rest_made", "restT_made", "restT_evacuated", "rest_full")]
        fix_loaded, fix_made, fix_stored, rounded6 = sem("fix_loaded"), sem("fix_made"), sem("fix_stored"), sem("rounded6")

        block = ctx.enter_context(nc.Block())

        def rows(t, n=1):
            return bass.ds(t * P, n * P)

        def group_rows(t, g):
            return t[bass.ds(g * (GT * P), GT * P), :].rearrange("(s p) d -> p s d", p=P)

        def idx(tile):
            return 2 * tile[0] + tile[1]

        def attention_steps(eng, step):
            step((0, 0), None)
            step((0, 1), (0, 0))
            step((1, 0), (0, 1))
            with eng.Fori(1, NT // 2 - 1) as j:
                step((j, 1), (j, 0))
                step((j + 1, 0), (j, 1))
            last = NT // 2 - 1
            step((last, 1), (last, 0))
            step(None, (last, 1))

        def projection_steps(eng, step):
            for k in range(4):
                step(k, k // 2, k % 2)
            with eng.Fori(2, NT // 2) as j:
                step(None, j, 0)
                step(None, j, 1)
            for k in range(NT, NT + 3):
                step(k, k // 2, k % 2)

        def staged(k, j, b, n):
            if k is not None and not 0 <= k - n < NT:
                return None
            t = 2 * j + b - n
            return t, j + (b - n) // 2, (b - n) % 2

        @block.sync
        def _(sp):
            sp.dma_start(wq_s, wq.rearrange("(a p) d -> p a d", p=P)).then_inc(wqk_in, 16)
            sp.dma_start(wk_s, wk.rearrange("(a p) d -> p a d", p=P)).then_inc(wqk_in, 16)
            with nc.allow_non_contiguous_dma(reason="three vectors of 512, once"):
                for n, v in enumerate((bq, bk, bv)):
                    sp.dma_start(bcol[:, n, :], v.rearrange("(a p) -> p a", p=P)).then_inc(bias_in, 16)
            sp.dma_start(wm_s, wm.rearrange("(a p) d -> p a d", p=P)).then_inc(wvm_in, 16)
            sp.dma_start(wv_s, wv.rearrange("(a p) d -> p a d", p=P)).then_inc(wvm_in, 16)
            sp.dma_start(bm_b, bm.rearrange("(a d) -> a d", a=1).to_broadcast([P, D])).then_inc(wvm_in, 16)
            sp.dma_start(w1_s, w1.rearrange("(a p) d -> p a d", p=P)).then_inc(w1_in, 16)

            def scan_loads(g):
                wait_from(sp, key_scanned, g)
                sp.dma_start(kv_in[0], group_rows(key, g)).then_inc(kscan_in, 16)
                wait_from(sp, value_scanned, g)
                sp.dma_start(kv_in[1], group_rows(value, g)).then_inc(vscan_in, 16)
            scan_loads(0)
            with sp.Fori(1, NG) as g:
                scan_loads(g)
            sp.wait_ge(weight_lo, 3)
            sp.wait_ge(weight_hi, 3)
            sp.dma_start(w2_scr, view(R, 8, 8, F16)).then_inc(weights_stored, 16)
            sp.dma_start(w1_scr, view(R, 16, 8, F16)).then_inc(weights_stored, 16)
            sp.wait_ge(weights_stored, 32)
            sp.wait_ge(key_scanned, NG)
            sp.wait_ge(value_scanned, NG)

            def phase2_loads(g):
                wait_from(sp, h_hi_made, g)
                wait_from(sp, h_lo_made, g)
                sp.dma_start(xg, group_rows(x, g)).then_inc(x_loaded, 16)
                wait_from(sp, key_lo, g)
                wait_from(sp, key_hi, g)
                sp.dma_start(kv_in[0], group_rows(key, g)).then_inc(key_loaded, 16)
                wait_from(sp, value_lo, g)
                wait_from(sp, value_hi, g)
                sp.dma_start(kv_in[1], group_rows(value, g)).then_inc(value_loaded, 16)

            def store_q(g):
                sp.wait_ge(q_hi, DB * (g + 1))
                sp.wait_ge(q_lo, DB * (g + 1))
                sp.dma_start(q_scr[bass.ds(g * GT, GT)].rearrange("s p m -> p s m"),
                             view(R, 40, 8, F16).rearrange("p (s m) -> p s m", s=GT)).then_inc(q_stored, 16)
            phase2_loads(0)
            with sp.Fori(1, NG) as g:
                phase2_loads(g)
                store_q(g - 1)
            store_q(NG - 1)

            sp.wait_ge(h_lo_made, NG)
            sp.wait_ge(hT_made, NG * GT)
            sp.dma_start(tt[0], adj[rows(0), :]).then_inc(adj_in[0], 16)
            sp.wait_ge(q_product, NG * DB)
            sp.wait_ge(q_lo, NG * DB)
            sp.wait_ge(q_hi, NG * DB)
            sp.dma_start(tt[1], adj[rows(1), :]).then_inc(adj_in[1], 16)
            sp.wait_ge(q_stored, 16 * NG)
            sp.wait_ge(value_lo, NG)
            sp.wait_ge(value_hi, NG)
            for b in range(2):
                sp.dma_start(qT[b], q_scr[b].rearrange("p (h a n) -> p h a n", h=2, a=DB)).then_inc(q_in[b], 16)

            def store_context(t):
                sp.wait_ge(context_made, t + 1)
                sp.dma_start(o_scr[rows(t), :], o32).then_inc(context_stored, 16)

            def attention_loads(j, b):
                t = 2 * j + b
                sp.wait_ge(exp_made, HC * (t - 1))
                sp.dma_start(tt[b], adj[rows(t), :]).then_inc(adj_in[b], 16)
                sp.wait_ge(scores_full, CH * (t - 1))
                sp.dma_start(qT[b], q_scr[bass.ds(t, 1)].rearrange("o p (h a n) -> p (o h) a n", h=2, a=DB)).then_inc(q_in[b], 16)
            attention_loads(1, 0)
            with sp.Fori(1, NT // 2 - 1) as j:
                attention_loads(j, 1)
                store_context(2 * j - 2)
                attention_loads(j + 1, 0)
                store_context(2 * j - 1)
            attention_loads(NT // 2 - 1, 1)
            for t in range(NT - 4, NT):
                store_context(t)

            sp.wait_ge(context_full, NT)
            sp.dma_start(view(VR, 0, 8, F16), w2_scr).then_inc(proj_w_in, 16)
            sp.dma_start(view(VR, 8, 8, F16), w1_scr).then_inc(proj_w_in, 16)
            sp.dma_start(b1_b, b1.rearrange("(a d) -> a d", a=1).to_broadcast([P, D])).then_inc(proj_w_in, 16)
            sp.wait_ge(context_stored, 16 * NT)

            def projection_loads(k, j, b):
                if k is None or k < NT:
                    t = 2 * j + b
                    if k is None or k >= 2:
                        sp.wait_ge(o_lo, t - 1)
                        sp.wait_ge(o_hi, t - 1)
                    sp.dma_start(o_in[b], o_scr[rows(t), :]).then_inc(o_loaded[b], 16)
                    if k is None or k >= 2:
                        sp.wait_ge(proj_taken, t - 1)
                    sp.dma_start(x_in[b], x[rows(t), :]).then_inc(x4_loaded[b], 16)
                if k == 1:
                    for bb in range(2):
                        sp.dma_start(tt[bb], adj[rows(bb), :]).then_inc(adj5_in[bb], 16)
                done = staged(k, j, b, 3)
                if done:
                    sp.wait_ge(x1b_made, done[0] + 1)
                    sp.dma_start(x1_scr[rows(done[0]), :], x1b).then_inc(x1b_stored, 16)
            projection_steps(sp, projection_loads)

            sp.wait_ge(x1b_stored, 16 * NT)
            for b in range(2):
                sp.dma_start(x1_in[b], x1_scr[rows(b), :]).then_inc(x1_loaded[b], 16)

            def store_out(t, b):
                sp.wait_ge(out_made, t + 1)
                sp.dma_start(out[rows(t), :], o_out[b]).then_inc(out_stored[b], 16)
            with sp.Fori(1, NT // 2) as j:
                for b in range(2):
                    t = 2 * j + b
                    sp.wait_ge(adj_rounded, t - 1)
                    sp.wait_ge(adj_compared, t - 1)
                    sp.dma_start(tt[b], adj[rows(t), :]).then_inc(adj5_in[b], 16)
                    store_out(t - 2, b)
                    sp.dma_start(x1_in[b], x1_scr[rows(t), :]).then_inc(x1_loaded[b], 16)
            for b in range(2):
                store_out(NT - 2 + b, b)
            for b in range(2):
                sp.wait_ge(out_stored[b], 16 * NT // 2)

            sp.wait_ge(flag_made, 1)
            with sp.If(sp.value_load(flag[0:1, 0:1], min_val=0, max_val=1) > 0):
                def rest_traffic(t):
                    wait_from(sp, fix_stored, 16 * t)
                    sp.dma_start(tt[0], adj[rows(t), :]).then_inc(adj6_in, 16)
                    sp.dma_start(fix_in, out[rows(t), :]).then_inc(fix_loaded, 16)
                    sp.wait_ge(fix_made, t + 1)
                    sp.dma_start(out[rows(t), :], fix_out).then_inc(fix_stored, 16)
                rest_traffic(0)
                with sp.Fori(1, NT) as t:
                    rest_traffic(t)
                sp.wait_ge(fix_stored, 16 * NT)

        @block.gpsimd
        def _(pool):
            pool.memset(ident32[:], 0.0).then_inc(ident_zero, 1)
            pool.memset(ident16[:], 0.0).then_inc(ident_zero, 1)
            pool.memset(identb[:], 0.0).then_inc(ident_zero, 1)
            pool.wait_ge(ident_zero, 3)
            for m in (ident32, ident16, identb):
                pool.affine_select(out=m[:], in_=m[:], compare_op=ALU.not_equal, fill=1.0, base=0,
                                   pattern=[[-1, P]], channel_multiplier=1).then_inc(ident_made, 1)
            pool.wait_ge(maxima_made, 1)
            pool.partition_all_reduce(gmx[:], mx[:], P, RMAX).then_inc(maxima_shared, 1)
            pool.wait_ge(misses_summed, 1)
            pool.partition_all_reduce(miss2[:, 1:2], miss2[:, 0:1], P, RADD).then_inc(misses_shared, 1)

        @block.tensor
        def _(pe):
            item = [0]

            def weight_item(emit):
                n = item[0]
                if n >= 8:
                    pe.wait_ge(weight_evacuated, n - 7)
                emit(bank(n % 8)).then_inc(weight_product, 1)
                item[0] += 1

            def product(lhs, rhs):
                def emit(to):
                    for a in range(DB):
                        last = pe.matmul(to[:, 0:rhs(a).shape[1]], lhs(a), rhs(a), start=(a == 0), stop=(a == DB - 1))
                    return last
                return emit

            pe.wait_ge(wqk_in, 32)
            for d in range(DB):
                weight_item(product(lambda a: wq_s[:, a, d * P:(d + 1) * P], lambda a: wk_s[:, a, :]))
            pe.wait_ge(bias_in, 48)
            pe.wait_ge(cols_spread, 2)
            weight_item(product(lambda a: bkb[:, a, :], lambda a: wq_s[:, a, :]))

            def columns(to):
                for d in range(DB):
                    for a in range(DB):
                        pe.matmul(to[:, d:d + 1], wk_s[:, a, d * P:(d + 1) * P], bcol[:, 0, a:a + 1],
                                  start=(a == 0), stop=(a == DB - 1))
                for a in range(DB):
                    last = pe.matmul(to[:, DB:DB + 1], bkb[:, a, :], bcol[:, 0, a:a + 1],
                                     start=(a == 0), stop=(a == DB - 1))
                return last
            weight_item(columns)
            pe.wait_ge(wvm_in, 48)
            pe.wait_ge(ident_made, 3)
            for a in range(DB):
                def turned(to, a=a):
                    for e in range(DB):
                        last = pe.transpose(to[:, e * P:(e + 1) * P], wm_s[:, e, a * P:(a + 1) * P], ident32[:])
                    return last
                weight_item(turned)
            pe.wait_ge(weight_evacuated, item[0])
            for d in range(DB):
                weight_item(product(lambda a: wv_s[:, a, d * P:(d + 1) * P], lambda a: wmT[:, a, :]))
            weight_item(product(lambda a: bvb[:, a, :], lambda a: wmT[:, a, :]))

            pe.wait_ge(weight_evacuated, item[0])

            def key_transposes(g):
                pe.wait_ge(key_hi, g + 1)
                pe.wait_ge(key_lo, g + 1)
                for s in range(GT):
                    if s >= 2 or not isinstance(g, int) or g:
                        pe.wait_ge(keyT_evacuated, GT * g + s - 1)
                    to = bank16(s % 2)
                    for h in range(2):
                        for a in range(DB):
                            last = pe.transpose(to[:, h * DB + a, :], khl[:, h, s, a * P:(a + 1) * P], ident16[:])
                    last.then_inc(keyT_made, 1)

            def h_transposes(g):
                pe.wait_ge(h_hi_made, g + 1)
                pe.wait_ge(h_lo_made, g + 1)
                for s in range(GT):
                    if s >= 2 or not isinstance(g, int) or g:
                        pe.wait_ge(hT_evacuated, GT * g + s - 1)
                    to = bank16(2 + s % 2)
                    for h in range(2):
                        for a in range(DB):
                            last = pe.transpose(to[:, h * DB + a, :], hhl[:, h, s, a * P:(a + 1) * P], ident16[:])
                    last.then_inc(hT_made, 1)

            def query_products(g):
                pe.wait_ge(hT_evacuated, GT * (g + 1))
                for o in range(DB):
                    wait_from(pe, q32_made, DB * g)
                    n = 0
                    for lh, rh in ((0, 0), (0, 1), (1, 0)):
                        for a in range(DB):
                            last = pe.matmul(bank(4 + o), mhl[:, a, lh, o * P:(o + 1) * P], hT[:, rh, a, :],
                                             start=(n == 0), stop=(n == 3 * DB - 1))
                            n += 1
                    last.then_inc(q_product, 1)
            pe.wait_ge(weight_hi, 3)
            pe.wait_ge(weight_lo, 3)
            key_transposes(0)
            h_transposes(0)
            key_transposes(1)
            query_products(0)
            h_transposes(1)
            with pe.Fori(2, NG) as g:
                key_transposes(g)
                query_products(g - 1)
                h_transposes(g)
            query_products(NG - 1)

            pe.wait_ge(keyT_evacuated, NT)
            pe.wait_ge(hT_evacuated, NT)
            pe.wait_ge(q32_made, NG * DB)
            pe.wait_ge(value_hi, NG)
            pe.wait_ge(value_lo, NG)

            def p_transposes(t, g):
                pe.wait_ge(p_hi, HC * t + g // 2 + 1)
                pe.wait_ge(p_lo, HC * t + g // 2 + 1)
                if g >= 2 or not isinstance(t, int) or t:
                    pe.wait_ge(pT_evacuated, TG * t + g)
                to = bank16(4 + g % 2)
                for m in range(4):
                    for h in range(2):
                        last = pe.transpose(to[:, 2 * m + h, :], phl[:, h, (4 * g + m) * P:(4 * g + m + 1) * P], ident16[:])
                last.then_inc(pT_made, 1)

            def context_products(t, g):
                pe.wait_ge(pT_evacuated, TG * t + g + 1)
                for m in range(4):
                    for i, (lh, rh) in enumerate(((0, 0), (0, 1), (1, 0))):
                        last = pe.matmul(bank(6), pT[:, g % 2, m, lh, :], VV[:, 4 * g + m, rh, :],
                                         start=(g == 0 and m == 0 and i == 0), stop=(g == TG - 1 and m == 3 and i == 2))
                return last

            def attention_step(s, c):
                if s:
                    t = idx(s)
                    pe.wait_ge(q_in[s[1]], 16 * s[0] + 16)
                    for n in range(CH):
                        if c and n == CH - 1:
                            p_transposes(idx(c), 0)
                        if n >= 4 or c:
                            pe.wait_ge(scores_scaled, CH * t + n - 3)
                        i = 0
                        for lh, rh in ((0, 0), (0, 1), (1, 0)):
                            for a in range(DB):
                                last = pe.matmul(bank(n % 4), qT[s[1]][:, lh, a, :], KT[:, rh, a, n * D:(n + 1) * D],
                                                 start=(i == 0), stop=(i == 3 * DB - 1))
                                i += 1
                        last.then_inc(scores_full, 1)
                elif c:
                    p_transposes(idx(c), 0)
                if c:
                    t = idx(c)
                    wait_from(pe, context_made, t)
                    for g in range(TG):
                        if g + 1 < TG:
                            p_transposes(t, g + 1)
                        last = context_products(t, g)
                    last.then_inc(context_full, 1)
            attention_steps(pe, attention_step)

            pe.wait_ge(proj_w_in, 48)

            def turn_tile(to, src):
                for h in range(2):
                    for a in range(DB):
                        last = pe.transpose(to[:, h * DB + a, :], src[:, h, a * P:(a + 1) * P], ident16[:])
                return last

            def tile_product(to, left, w):
                n = 0
                for lh, rh in ((0, 0), (0, 1), (1, 0)):
                    for a in range(DB):
                        last = pe.matmul(to, left[:, lh, a, :], w[:, a, rh, :], start=(n == 0), stop=(n == 3 * DB - 1))
                        n += 1
                return last

            def projection_step(k, j, b):
                if s := staged(k, j, b, 0):
                    pe.wait_ge(o_hi, s[0] + 1)
                    pe.wait_ge(o_lo, s[0] + 1)
                    pe.wait_ge(oT_evacuated, s[0])
                    turn_tile(bank16(0), ohl).then_inc(oT_made, 1)
                if s := staged(k, j, b, 3):
                    pe.wait_ge(h2T_evacuated, s[0] + 1)
                    pe.wait_ge(support32_made, s[0])
                    tile_product(bank(3), h2T, w1p).then_inc(support_full, 1)
                if s := staged(k, j, b, 2):
                    pe.wait_ge(h2_hi, s[0] + 1)
                    pe.wait_ge(h2_lo, s[0] + 1)
                    pe.wait_ge(h2T_evacuated, s[0])
                    turn_tile(bank16(2), h2hl).then_inc(h2T_made, 1)
                if s := staged(k, j, b, 1):
                    pe.wait_ge(oT_evacuated, s[0] + 1)
                    pe.wait_ge(proj_taken, s[0])
                    tile_product(bank(1), oT, w2p).then_inc(proj_full, 1)
            projection_steps(pe, projection_step)

            pe.wait_ge(support_hi, NT)
            pe.wait_ge(support_lo, NT)

            def adj_transposes(t, b, g):
                if g == 0:
                    pe.wait_ge(adj_rounded, t + 1)
                if g >= 2 or not isinstance(t, int) or t:
                    pe.wait_ge(aT_evacuated, 4 * t + g - 1)
                for m in range(8):
                    last = pe.transpose(bank16(4 + g % 2, BF16)[:, m, :],
                                        a_bf[:, b, (8 * g + m) * P:(8 * g + m + 1) * P], identb[:])
                last.then_inc(aT_made, 1)

            def conv_products(t, b, g):
                pe.wait_ge(aT_evacuated, 4 * t + g + 1)
                for m in range(8):
                    for h in range(2):
                        last = pe.matmul(bank(6 + b), aT[:, g % 2, m, :], SUP[:, 8 * g + m, h, :],
                                         start=(g == 0 and m == 0 and h == 0), stop=(g == 3 and m == 7 and h == 1))
                return last

            def conv_tile(t, b):
                if not isinstance(t, int) or t > 1:
                    pe.wait_ge(out_made, t - 1)
                for g in range(4):
                    if g + 1 < 4:
                        adj_transposes(t, b, g + 1)
                    last = conv_products(t, b, g)
                last.then_inc(conv_full, 1)
            adj_transposes(0, 0, 0)
            def conv_pair(j):
                for b in range(2):
                    conv_tile(2 * j + b, b)
                    adj_transposes(2 * j + b + 1, 1 - b, 0)
            conv_pair(0)
            with pe.Fori(1, NT // 2 - 1) as j:
                conv_pair(j)
            conv_tile(NT - 2, 0)
            adj_transposes(NT - 1, 1, 0)
            conv_tile(NT - 1, 1)

            pe.wait_ge(flag_made, 1)
            with pe.If(pe.value_load(flag[0:1, 0:1], min_val=0, max_val=1) > 0):
                pe.wait_ge(sup32_made, 1)
                pe.wait_ge(out_made, NT)

                def rest_tile(t):
                    pe.wait_ge(rest_made, t + 1)
                    wait_from(pe, fix_made, t)
                    for q in range(8):
                        wait_from(pe, restT_evacuated, 8 * t + q)
                        for m in range(4):
                            last = pe.transpose(bank(4)[:, m * P:(m + 1) * P], tt[1][:, (4 * q + m) * P:(4 * q + m + 1) * P], ident32[:])
                        last.then_inc(restT_made, 1)
                        pe.wait_ge(restT_evacuated, 8 * t + q + 1)
                        for m in range(4):
                            last = pe.matmul(bank(6), restT[:, m * P:(m + 1) * P], sup32[:, 4 * q + m, :],
                                             start=(q == 0 and m == 0), stop=(q == 7 and m == 3))
                    last.then_inc(rest_full, 1)
                rest_tile(0)
                with pe.Fori(1, NT) as t:
                    rest_tile(t)

        @block.scalar
        def _(act):
            homes = [m32[:, d, :] for d in range(DB)] + [u_b, cs[:]] + [wmT[:, a, :] for a in range(DB)] \
                + [w232[:, d, :] for d in range(DB)] + [b2_b[:]]
            for n, home in enumerate(homes):
                act.wait_ge(weight_product, n + 1)
                act.copy(home, bank(n % 8)[:, 0:home.shape[1]]).then_inc(weight_evacuated, 1)
            act.wait_ge(scales_made, 1)
            act.wait_ge(weight_evacuated, len(homes))
            act.activation(mhl[:, :, 0, :], m32, ACT.Copy, scale=col(G_M)).then_inc(weight_hi, 1)
            act.activation(w2hl[:, :, 0, :], w232, ACT.Copy, scale=col(G_W2)).then_inc(weight_hi, 1)
            act.activation(w1hl[:, :, 0, :], w1_s, ACT.Copy, scale=col(G_W1)).then_inc(weight_hi, 1)

            def phase2_step(g, prior):
                if g is not None:
                    act.wait_ge(key_loaded, 16 * g + 16)
                    wait_from(act, keyT_made, GT * g)
                    act.activation(khl[:, 0], kv_in[0], ACT.Copy, scale=col(G_K)).then_inc(key_hi, 1)
                    act.wait_ge(value_loaded, 16 * g + 16)
                    if isinstance(g, int) and g == 0:
                        act.wait_ge(weight_lo, 3)
                    act.activation(VV[:, bass.ds(g * GT, GT), 0, :], kv_in[1], ACT.Copy, scale=col(G_V)).then_inc(value_hi, 1)
                    act.wait_ge(var_made, g + 1)
                    act.activation(rs[:], mv[:, :, 1], ACT.Sqrt).then_inc(std_made, 1)
                    wait_from(act, hT_made, GT * g)
                    act.wait_ge(xn_made, GT * g + GT)
                    if isinstance(g, int):
                        act.wait_ge(weights_stored, 32)
                    act.activation(hhl[:, 0], xg, ACT.Relu).then_inc(h_hi_made, 1)
                    for s in range(GT):
                        act.wait_ge(keyT_made, GT * g + s + 1)
                        act.copy(KT[:, :, :, bass.ds((g * GT + s) * P, P)],
                                 bank16(s % 2).rearrange("p (h a) n -> p h a n", h=2)).then_inc(keyT_evacuated, 1)
                if prior is not None:
                    for o in range(DB):
                        act.wait_ge(q32_made, DB * prior + o + 1)
                        if o == 0:
                            wait_from(act, q_stored, 16 * prior)
                        act.copy(qst[:, :, 0, o, :], q32[:, o % 2, :].rearrange("p (s n) -> p s n", s=GT)).then_inc(q_hi, 1)
                if g is not None:
                    for s in range(GT):
                        act.wait_ge(hT_made, GT * g + s + 1)
                        if s == 0:
                            wait_from(act, q_product, DB * g)
                        act.copy(hT[:, :, :, s * P:(s + 1) * P],
                                 bank16(2 + s % 2).rearrange("p (h a) n -> p h a n", h=2)).then_inc(hT_evacuated, 1)
            phase2_step(0, None)
            phase2_step(1, 0)
            with act.Fori(2, NG) as g:
                phase2_step(g, g - 1)
            phase2_step(None, NG - 1)

            act.wait_ge(q_stored, 16 * NG)

            def take_pT(t, g):
                act.wait_ge(pT_made, TG * t + g + 1)
                act.copy(pT[:, g % 2], bank16(4 + g % 2).rearrange("p (t h) n -> p t h n", h=2)).then_inc(pT_evacuated, 1)

            def attention_step(s, c):
                def magnitudes(n):
                    t = idx(s)
                    act.wait_ge(scores_scaled, CH * t + 2 * n + 2)
                    if n >= 2:
                        act.wait_ge(scores_masked, HC * t + n - 1)
                    elif c:
                        act.wait_ge(p_lo, HC * t)
                    act.activation(p32[:, n % 2, :], tt[s[1]][:, n * SC:(n + 1) * SC], ACT.Abs).then_inc(abs_made, 1)

                def exponentials(n):
                    t = idx(s)
                    if n == 0:
                        act.wait_ge(shift_made, t + 1)
                    if n >= 2:
                        act.wait_ge(p_lo, HC * t + n - 1)
                    act.activation(p32[:, n % 2, :], tt[s[1]][:, n * SC:(n + 1) * SC], ACT.Exp,
                                   bias=nbias[:, 2:3], scale=col(I_G), accum_out=rsum[:, n:n + 1]).then_inc(exp_made, 1)

                def upper_parts(n):
                    t = idx(s)
                    act.wait_ge(exp_made, HC * t + n + 1)
                    if c:
                        act.wait_ge(pT_made, TG * idx(c) + 2 * n + 2)
                    act.copy(phl[:, 0, n * SC:(n + 1) * SC], p32[:, n % 2, :]).then_inc(p_hi, 1)

                if s:
                    for n in range(HC - 1):
                        magnitudes(n)
                if c:
                    take_pT(idx(c), 0)
                if s:
                    magnitudes(HC - 1)
                if c:
                    take_pT(idx(c), 1)
                for g in range(2, TG):
                    if c:
                        take_pT(idx(c), g)
                    if s and g % 2 == 0:
                        exponentials(g // 2 - 1)
                    if s and g % 2:
                        upper_parts(g // 2 - 1)
                if s:
                    exponentials(HC - 1)
                    upper_parts(HC - 1)
            attention_steps(act, attention_step)

            act.wait_ge(context_full, NT)

            def projection_step(k, j, b):
                if s := staged(k, j, b, 0):
                    act.wait_ge(o_loaded[b], 16 * j + 16)
                    act.wait_ge(oT_made, s[0])
                    act.copy(ohl[:, 0, :], o_in[b]).then_inc(o_hi, 1)
                if s := staged(k, j, b, 0):
                    act.wait_ge(oT_made, s[0] + 1)
                    act.wait_ge(proj_full, s[0])
                    act.copy(oT, bank16(0).rearrange("p (h a) n -> p h a n", h=2)).then_inc(oT_evacuated, 1)
                if s := staged(k, j, b, 3):
                    act.wait_ge(support32_made, s[0] + 1)
                    act.copy(SUP[:, bass.ds(s[0], 1), 0, :], s32).then_inc(support_hi, 1)
                if s := staged(k, j, b, 2):
                    act.wait_ge(h2T_made, s[0] + 1)
                    act.wait_ge(support_full, s[0])
                    act.copy(h2T, bank16(2).rearrange("p (h a) n -> p h a n", h=2)).then_inc(h2T_evacuated, 1)
                if s := staged(k, j, b, 1):
                    act.wait_ge(var4_made, s[0] + 1)
                    act.activation(rs[:, 0:1], mv[:, 0, 1:2], ACT.Sqrt).then_inc(std4_made, 1)
                    act.wait_ge(xn4_made, s[0] + 1)
                    act.wait_ge(h2T_made, s[0])
                    act.activation(h2hl[:, 0, :], xn, ACT.Relu).then_inc(h2_hi, 1)
            projection_steps(act, projection_step)

            def take_aT(t):
                for g in range(4):
                    act.wait_ge(aT_made, 4 * t + g + 1)
                    act.copy(aT[:, g % 2], bank16(4 + g % 2, BF16)).then_inc(aT_evacuated, 1)
            with act.Fori(0, NT) as t:
                take_aT(t)

            act.wait_ge(flag_made, 1)
            with act.If(act.value_load(flag[0:1, 0:1], min_val=0, max_val=1) > 0):
                with act.Fori(0, NT) as t:
                    for q in range(8):
                        act.wait_ge(restT_made, 8 * t + q + 1)
                        act.copy(restT, bank(4)).then_inc(restT_evacuated, 1)

        @block.vector
        def _(dve):
            own = Chain(dve, dve_own)
            own.mark(dve.memset(ones[:], 1.0))
            own.settle()
            dve.wait_ge(bias_in, 48)
            for n, spread in ((1, bkb), (2, bvb)):
                for a in range(DB):
                    last = dve.tensor_scalar(spread[:, a, :], ones[:], bcol[:, n, a:a + 1], None, ALU.mult)
                last.then_inc(cols_spread, 1)

            with dve.Fori(0, NG) as g:
                for n, (loaded, scanned) in enumerate(((kscan_in, key_scanned), (vscan_in, value_scanned))):
                    dve.wait_ge(loaded, 16 * g + 16)
                    dve.tensor_reduce(kmx[:, n, bass.ds(g, 1)], kv_in[n], AX_XY, ALU.max,
                                      apply_absolute_value=True).then_inc(scanned, 1)
            dve.wait_ge(weight_evacuated, 15)
            dve.wait_ge(w1_in, 16)
            dve.wait_ge(wvm_in, 48)
            own.mark(dve.tensor_tensor(b2_b[:], b2_b[:], bm_b, ALU.add))
            dve.wait_ge(key_scanned, NG)
            dve.wait_ge(value_scanned, NG)
            own.mark(dve.tensor_reduce(mx[:, 0:2], kmx[:], AX_X, ALU.max))
            for n, w in ((2, m32), (4, w232), (5, w1_s)):
                own.mark(dve.tensor_reduce(mx[:, n:n + 1], w, AX_XY, ALU.max, apply_absolute_value=True))
            dve.tensor_reduce(mx[:, 3:4], cs[:, 0:DB], AX_X, ALU.max, apply_absolute_value=True).then_inc(maxima_made, 1)

            dve.wait_ge(maxima_shared, 1)
            own.mark(dve.tensor_scalar(sc[:, TMP:TMP + 1], gmx[:, 2:3], float(D), gmx[:, 3:4], ALU.mult, ALU.add))
            own.settle()
            own.mark(dve.tensor_copy(gmx[:, 3:4], sc[:, TMP:TMP + 1]))
            own.settle()
            own.mark(dve.tensor_scalar(gmx[:], gmx[:], 2.0 ** -20, None, ALU.max))
            own.settle()
            own.mark(dve.tensor_scalar(fl[:, 0:6].bitcast(I32), gmx[:].bitcast(I32), EXPONENT_BITS, None, ALU.bitwise_and))
            own.settle()
            own.mark(dve.reciprocal(gmx[:], fl[:, 0:6]))
            own.settle()
            for to, n in ((G_K, 0), (G_V, 1), (G_M, 2), (G_Q, 3), (G_W2, 4), (G_W1, 5)):
                own.mark(dve.tensor_scalar(col(to), gmx[:, n:n + 1], TOP, None, ALU.mult))
            own.settle()
            own.mark(dve.tensor_scalar(col(S_Q), fl[:, 2:3], 1.0 / (H_SCALE * TOP), col(G_Q), ALU.mult, ALU.mult))
            own.mark(dve.tensor_scalar(col(S_R0), col(G_Q), col(G_K), None, ALU.mult))
            own.settle()
            own.mark(dve.tensor_scalar(col(S_R), col(S_R0), 1.0 / H_SCALE, None, ALU.mult))
            own.mark(dve.tensor_scalar(col(G_ALL), col(S_R0), SCORE_DIV, None, ALU.mult))
            own.settle()
            own.mark(dve.reciprocal(col(I_G), col(G_ALL)))
            own.mark(dve.tensor_scalar(col(THR), col(G_ALL), NEAR_ZERO, None, ALU.mult))
            own.mark(dve.tensor_scalar(col(BIG), col(G_ALL), MASKED, None, ALU.mult))
            own.mark(dve.tensor_scalar(col(I_O), fl[:, 1:2], TOP ** -2, fl[:, 4:5], ALU.mult, ALU.mult))
            own.mark(dve.tensor_scalar(col(I_S), fl[:, 5:6], D / TOP, None, ALU.mult))
            own.mark(dve.tensor_scalar(cq[:], cs[:, 0:DB], col(G_Q), None, ALU.mult))
            own.mark(dve.tensor_scalar(col(S_R0), cs[:, DB:DB + 1], col(S_R0), None, ALU.mult))
            own.settle()
            dve.tensor_scalar(u_b, u_b, col(S_R), None, ALU.mult).then_inc(scales_made, 1)
            dve.wait_ge(scales_made, 1)
            for n, (hl, w, g) in enumerate(((mhl, m32, G_M), (w2hl, w232, G_W2), (w1hl, w1_s, G_W1))):
                dve.wait_ge(weight_hi, n + 1)
                for a in range(DB):
                    last = dve.scalar_tensor_tensor(hl[:, a, 1, :], w[:, a, :], col(g), hl[:, a, 0, :], ALU.mult, ALU.subtract)
                last.then_inc(weight_lo, 1)
            own.settle()

            BASE2 = own.base + own.k
            PER2 = 5

            def phase2_step(g, prior):
                own.rebase(BASE2 + (PER2 * g if g is not None else PER2 * NG))
                if g is not None:
                    dve.wait_ge(x_loaded, 16 * g + 16)
                    if isinstance(g, int):
                        dve.wait_ge(weights_stored, 32)
                    for s in range(GT):
                        last = dve.bn_stats(stats[:, s, :], xg[:, s, :])
                    own.mark(last)
                    dve.wait_ge(key_loaded, 16 * g + 16)
                    dve.wait_ge(key_hi, g + 1)
                    own.settle()
                    dve.scalar_tensor_tensor(khl[:, 1].rearrange("p s d -> p (s d)"), kv_in[0].rearrange("p s d -> p (s d)"), col(G_K),
                                             khl[:, 0].rearrange("p s d -> p (s d)"), ALU.mult, ALU.subtract).then_inc(key_lo, 1)
                    for s in range(GT):
                        last = dve.bn_aggr(mv[:, s, :], stats[:, s, :])
                    own.mark(last)
                    own.settle()
                    dve.tensor_scalar(mv[:, :, 1], mv[:, :, 1], EPS, None, ALU.add).then_inc(var_made, 1)
                    dve.wait_ge(std_made, g + 1)
                    own.mark(dve.reciprocal(rs[:], rs[:]))
                    own.settle()
                    own.mark(dve.tensor_scalar(rs[:], rs[:], H_SCALE, None, ALU.mult))
                    own.settle()
                    for s in range(GT):
                        dve.tensor_scalar(xg[:, s, :], xg[:, s, :], mv[:, s, 0:1], rs[:, s:s + 1],
                                          ALU.subtract, ALU.mult).then_inc(xn_made, 1)
                    dve.wait_ge(value_loaded, 16 * g + 16)
                    dve.wait_ge(value_hi, g + 1)
                    dve.scalar_tensor_tensor(VV[:, bass.ds(g * GT, GT), 1, :], kv_in[1], col(G_V),
                                             VV[:, bass.ds(g * GT, GT), 0, :], ALU.mult, ALU.subtract).then_inc(value_lo, 1)
                    dve.wait_ge(xn_made, GT * g + GT)
                    wait_from(dve, hT_made, GT * g)
                    for s in range(GT):
                        last = dve.scalar_tensor_tensor(junk[:, s, :], xg[:, s, :], 0.0, u_b, ALU.max, ALU.mult,
                                                        accum_out=r_s[:, bass.ds(g * GT + s, 1)])
                    own.mark(last)
                    own.settle()
                    dve.wait_ge(h_hi_made, g + 1)
                    dve.scalar_tensor_tensor(hhl[:, 1].rearrange("p s d -> p (s d)"), xg.rearrange("p s d -> p (s d)"), 0.0,
                                             hhl[:, 0].rearrange("p s d -> p (s d)"), ALU.max, ALU.subtract).then_inc(h_lo_made, 1)
                    assert own.k == PER2
                if prior is not None:
                    for o in range(DB):
                        if o >= 2:
                            dve.wait_ge(q_hi, DB * prior + o - 1)
                        else:
                            wait_from(dve, q_hi, DB * prior)
                        dve.wait_ge(q_product, DB * prior + o + 1)
                        dve.tensor_scalar(q32[:, o % 2, :], bank(4 + o), col(S_Q), cq[:, o:o + 1],
                                          ALU.mult, ALU.add).then_inc(q32_made, 1)
                        dve.wait_ge(q_hi, DB * prior + o + 1)
                        dve.tensor_tensor(qst[:, :, 1, o, :], q32[:, o % 2, :].rearrange("p (s n) -> p s n", s=GT),
                                          qst[:, :, 0, o, :], ALU.subtract).then_inc(q_lo, 1)
            phase2_step(0, None)
            phase2_step(1, 0)
            with dve.Fori(2, NG) as g:
                phase2_step(g, g - 1)
            phase2_step(None, NG - 1)
            own.rebase(BASE2 + PER2 * NG)
            own.mark(dve.tensor_scalar(r_s[:], r_s[:], col(S_R0), None, ALU.add))
            own.settle()

            att = Chain(dve, dve_att)

            def mask_chunk(t, T, m):
                wide = T[:, m * SC:(m + 1) * SC]
                dve.wait_ge(abs_made, HC * t + m + 1)
                dve.tensor_scalar(p32[:, m % 2, :], p32[:, m % 2, :], col(THR), col(BIG),
                                  ALU.is_lt, ALU.mult).then_inc(hidden_found, 1)
                dve.wait_ge(hidden_found, HC * t + m + 1)
                dve.tensor_tensor(wide, wide, p32[:, m % 2, :], ALU.add).then_inc(scores_masked, 1)
                dve.wait_ge(scores_masked, HC * t + m + 1)
                dve.tensor_reduce(rmax[:, m:m + 1], wide, AX_X, ALU.max).then_inc(max_chunk, 1)

            def attention_step(s, c):
                if s:
                    t = idx(s)
                    T = tt[s[1]]
                    dve.wait_ge(adj_in[s[1]], 16 * s[0] + 16)
                    for n in range(CH):
                        dve.wait_ge(scores_full, CH * t + n + 1)
                        chunk = T[:, n * D:(n + 1) * D]
                        dve.scalar_tensor_tensor(chunk, bank(n % 4), r_s[:, bass.ds(t, 1)], chunk,
                                                 ALU.add, ALU.mult).then_inc(scores_scaled, 1)
                        if n % 2 == 0 and n:
                            mask_chunk(t, T, n // 2 - 1)
                    mask_chunk(t, T, HC - 1)
                    dve.wait_ge(max_chunk, HC * t + HC)
                    att.rebase(2 * t)
                    att.mark(dve.tensor_reduce(nbias[:, 0:1], rmax[:], AX_X, ALU.max))
                    att.settle()
                    att.mark(dve.tensor_scalar(nbias[:, 1:2], nbias[:, 0:1], col(I_G), -1.0, ALU.mult, ALU.mult))
                    att.settle()
                    dve.tensor_scalar(nbias[:, 2:3], nbias[:, 1:2], P_SHIFT, None, ALU.add).then_inc(shift_made, 1)
                if s:
                    for m in range(HC):
                        dve.wait_ge(p_hi, HC * t + m + 1)
                        dve.tensor_tensor(phl[:, 1, m * SC:(m + 1) * SC], p32[:, m % 2, :],
                                          phl[:, 0, m * SC:(m + 1) * SC], ALU.subtract).then_inc(p_lo, 1)
                if c:
                    dve.wait_ge(context_full, idx(c) + 1)
                    wait_from(dve, context_stored, 16 * idx(c))
                    dve.tensor_scalar(o32, bank(6), linv[:, 1:2], None, ALU.mult).then_inc(context_made, 1)
                if s:
                    dve.wait_ge(exp_made, HC * t + HC)
                    dve.tensor_reduce(linv[:, 0:1], rsum[:], AX_X, ALU.add).then_inc(sum_made, 1)
                    dve.wait_ge(sum_made, t + 1)
                    dve.reciprocal(linv[:, 1:2], linv[:, 0:1]).then_inc(inverse_made, 1)
                    dve.wait_ge(inverse_made, t + 1)
            attention_steps(dve, attention_step)

            dve.wait_ge(context_full, NT)
            dve.wait_ge(proj_w_in, 48)
            proj = Chain(dve, dve_proj)
            PER4 = 5

            def projection_step(k, j, b):
                if s := staged(k, j, b, 0):
                    dve.wait_ge(o_loaded[b], 16 * j + 16)
                    dve.wait_ge(o_hi, s[0] + 1)
                    dve.tensor_tensor(ohl[:, 1, :], o_in[b], ohl[:, 0, :], ALU.subtract).then_inc(o_lo, 1)
                if s := staged(k, j, b, 3):
                    dve.wait_ge(support_full, s[0] + 1)
                    dve.wait_ge(support_lo, s[0])
                    dve.tensor_scalar(s32, bank(3), SUPPORT_SCALE, None, ALU.mult).then_inc(support32_made, 1)
                    dve.wait_ge(support_hi, s[0] + 1)
                    dve.tensor_tensor(SUP[:, bass.ds(s[0], 1), 1, :], s32, SUP[:, bass.ds(s[0], 1), 0, :],
                                      ALU.subtract).then_inc(support_lo, 1)
                if s := staged(k, j, b, 1):
                    t = s[0]
                    proj.rebase(PER4 * t)
                    dve.wait_ge(proj_full, t + 1)
                    dve.wait_ge(x4_loaded[s[2]], 16 * s[1] + 16)
                    own_x = x_in[s[2]]
                    dve.scalar_tensor_tensor(x1, bank(1), col(I_O), own_x, ALU.mult, ALU.add).then_inc(proj_taken, 1)
                    dve.wait_ge(proj_taken, t + 1)
                    proj.mark(dve.tensor_tensor(x1, x1, b2_b[:], ALU.add))
                    proj.settle()
                    proj.mark(dve.bn_stats(stats[:, 0, :], x1))
                    dve.wait_ge(x1b_stored, 16 * t)
                    proj.settle()
                    dve.tensor_tensor(x1b, x1, b1_b, ALU.add).then_inc(x1b_made, 1)
                    proj.mark(dve.bn_aggr(mv[:, 0, :], stats[:, 0, :]))
                    proj.settle()
                    dve.tensor_scalar(mv[:, 0, 1:2], mv[:, 0, 1:2], EPS, None, ALU.add).then_inc(var4_made, 1)
                    dve.wait_ge(std4_made, t + 1)
                    proj.mark(dve.reciprocal(rs[:, 1:2], rs[:, 0:1]))
                    proj.settle()
                    proj.mark(dve.tensor_scalar(rs[:, 2:3], rs[:, 1:2], H_SCALE, None, ALU.mult))
                    proj.settle()
                    dve.tensor_scalar(xn, x1, mv[:, 0, 0:1], rs[:, 2:3], ALU.subtract, ALU.mult).then_inc(xn4_made, 1)
                    dve.wait_ge(h2_hi, t + 1)
                    dve.scalar_tensor_tensor(h2hl[:, 1, :], xn, 0.0, h2hl[:, 0, :], ALU.max, ALU.subtract).then_inc(h2_lo, 1)
                    assert proj.k == PER4
            projection_steps(dve, projection_step)

            dve.wait_ge(pT_evacuated, TG * NT)

            def conv_step(j, b):
                t = 2 * j + b
                dve.wait_ge(adj5_in[b], 16 * j + 16)
                if not isinstance(j, int) or t:
                    dve.wait_ge(aT_made, 4 * t - 4)
                wait_from(dve, adj_compared, t)
                dve.tensor_copy(a_bf[:, b, :], tt[b]).then_inc(adj_rounded, 1)
                dve.wait_ge(adj_rounded, t + 1)
                dve.scalar_tensor_tensor(unequal, tt[b], 0.0, a_bf[:, b, :], ALU.add, ALU.not_equal,
                                         accum_out=miss[:, bass.ds(t, 1)]).then_inc(adj_compared, 1)

            def conv_out(j, b):
                t = 2 * j + b
                dve.wait_ge(conv_full, t + 1)
                dve.wait_ge(x1_loaded[b], 16 * j + 16)
                wait_from(dve, out_stored[b], 16 * j)
                dve.scalar_tensor_tensor(o_out[b], bank(6 + b), col(I_S), x1_in[b], ALU.mult, ALU.add).then_inc(out_made, 1)

            def conv_pair(j):
                conv_step(j, 1)
                conv_out(j, 0)
                conv_step(j + 1, 0)
                conv_out(j, 1)
            conv_step(0, 0)
            conv_pair(0)
            with dve.Fori(1, NT // 2 - 1) as j:
                conv_pair(j)
            conv_step(NT // 2 - 1, 1)
            conv_out(NT // 2 - 1, 0)
            conv_out(NT // 2 - 1, 1)

            dve.wait_ge(adj_compared, NT)
            dve.tensor_reduce(miss2[:, 0:1], miss[:], AX_X, ALU.add).then_inc(misses_summed, 1)
            dve.wait_ge(misses_shared, 1)
            dve.tensor_scalar(flag[:], miss2[:, 1:2], 1.0, None, ALU.min).then_inc(flag_made, 1)
            dve.wait_ge(flag_made, 1)
            with dve.If(dve.value_load(flag[0:1, 0:1], min_val=0, max_val=1) > 0):
                dve.tensor_tensor(sup32, SUP[:, :, 0, :], SUP[:, :, 1, :], ALU.add).then_inc(sup32_made, 1)

                def rest_step(t):
                    dve.wait_ge(adj6_in, 16 * t + 16)
                    dve.tensor_copy(a_bf[:, 0, :], tt[0]).then_inc(rounded6, 1)
                    dve.wait_ge(rounded6, t + 1)
                    dve.tensor_tensor(tt[1], tt[0], a_bf[:, 0, :], ALU.subtract).then_inc(rest_made, 1)
                    dve.wait_ge(rest_full, t + 1)
                    dve.wait_ge(fix_loaded, 16 * t + 16)
                    wait_from(dve, fix_stored, 16 * t)
                    dve.scalar_tensor_tensor(fix_out, bank(6), col(I_S), fix_in, ALU.mult, ALU.add).then_inc(fix_made, 1)
                rest_step(0)
                with dve.Fori(1, NT) as t:
                    rest_step(t)


_INS = ["x", "adj", "L0_gnn_key", "L0_gnn_value", "L0_gnn_Wq", "L0_gnn_bq", "L0_gnn_Wk", "L0_gnn_bk",
        "L0_gnn_Wv", "L0_gnn_bv", "L0_gnn_Wm", "L0_gnn_bm", "L1_gnn_weight", "L1_gnn_bias"]


def kernel(**inputs):
    import numpy as _np
    import concourse.bacc as _bacc
    from concourse import mybir as _mybir
    from concourse.bass_utils import run_bass_kernel_spmd as _run

    nc = _bacc.Bacc("TRN2", target_bir_lowering=False, num_devices=1)
    arrays, args = {}, []
    for name in _INS:
        a = _np.ascontiguousarray(inputs[name])
        arrays[f"in_{name}_dram"] = a
        args.append(nc.dram_tensor(f"in_{name}_dram", a.shape, _mybir.dt.from_np(a.dtype), kind="ExternalInput").ap())
    args.append(nc.dram_tensor("out_dram", (N, D), F32, kind="ExternalOutput").ap())
    program(nc, *args)
    r = _run(nc, [arrays], core_ids=[0])
    return r.results[0]["out_dram"]
```

```python
import concourse.bass as bass
from concourse import mybir

F32 = mybir.dt.float32
F16 = mybir.dt.float16
BF16 = mybir.dt.bfloat16
I32 = mybir.dt.int32
ALU = mybir.AluOpType
ACT = mybir.ActivationFunctionType
AX_X = mybir.AxisListType.X
AX_XY = mybir.AxisListType.XY
RMAX = bass.bass_isa.ReduceOp.max
RADD = bass.bass_isa.ReduceOp.add

P = 128
N = 4096
D = 512
DB = D // P
NT = N // P
GT = 4
NG = NT // GT
CH = N // D
HC = CH // 2
SC = N // HC
TG = NT // 4
KB = 1024

EPS = 1e-5
NEAR_ZERO = 1e-5
MASKED = -1e9
H_SCALE = 256.0
P_SHIFT = 9.0
TOP = 2.0 ** 14
SCORE_DIV = float(N) ** 0.5
EXPONENT_BITS = 0x7F800000
SUPPORT_SCALE = 1.0 / (H_SCALE * D)


def wait_from(eng, sem, count):
    if not isinstance(count, int) or count > 0:
        eng.wait_ge(sem, count)


class Chain:

    def __init__(self, eng, sem):
        self.eng, self.sem, self.base, self.k = eng, sem, 0, 0

    def mark(self, ins):
        self.k += 1
        return ins.then_inc(self.sem, 1)

    def settle(self):
        self.eng.wait_ge(self.sem, self.base + self.k)

    def rebase(self, base):
        self.base, self.k = base, 0


def program(nc, x, adj, key, value, wq, bq, wk, bk, wv, bv, wm, bm, w1, b1, out):
    from contextlib import ExitStack
    ctx = ExitStack()
    with ctx:
        def sb(name, shape, dt):
            return ctx.enter_context(nc.sbuf_tensor(name, shape, dt))

        def sem(name):
            return ctx.enter_context(nc.semaphore(name))

        q_scr = nc.dram_tensor("q_scr", (NT, P, 2 * DB * P), F16, kind="Internal").ap()
        w2_scr = nc.dram_tensor("w2_scr", (P, DB * 2 * D), F16, kind="Internal").ap()
        w1_scr = nc.dram_tensor("w1_scr", (P, DB * 2 * D), F16, kind="Internal").ap()
        o_scr = nc.dram_tensor("o_scr", (N, D), F32, kind="Internal").ap()
        x1_scr = nc.dram_tensor("x1_scr", (N, D), F32, kind="Internal").ap()

        KR = sb("key_region", [P, 16 * KB], F32)
        VR = sb("value_region", [P, 16 * KB], F32)
        R = sb("work_region", [P, 18 * KB], F32)

        def view(region, kb, size_kb, dt):
            w = region[:, kb * KB // 4:(kb + size_kb) * KB // 4]
            return w if dt == F32 else w.bitcast(dt)

        KT = view(KR, 0, 64, F16).rearrange("p (h a n) -> p h a n", h=2, a=DB)
        VV = view(VR, 0, 64, F16).rearrange("p (t h d) -> p t h d", h=2, d=D)
        def wview(kb):
            return view(VR, kb, 8, F32).rearrange("p (a d) -> p a d", a=DB)
        wq_s, wk_s, wv_s, wm_s, wmT, m32, w232, w1_s = [wview(8 * n) for n in range(8)]
        bkb = view(R, 0, 2, F32).rearrange("p (a n) -> p a n", a=DB)
        bvb = view(R, 2, 2, F32).rearrange("p (a n) -> p a n", a=DB)
        bm_b = view(R, 4, 2, F32)
        w2hl = view(R, 8, 8, F16).rearrange("p (a h d) -> p a h d", a=DB, h=2)
        w1hl = view(R, 16, 8, F16).rearrange("p (a h d) -> p a h d", a=DB, h=2)
        kv_in = [view(R, 56 + 8 * n, 8, F32).rearrange("p (s d) -> p s d", s=GT) for n in range(2)]
        xg = view(R, 0, 8, F32).rearrange("p (s d) -> p s d", s=GT)
        hhl = view(R, 8, 8, F16).rearrange("p (h s d) -> p h s d", h=2, s=GT)
        hT = view(R, 16, 8, F16).rearrange("p (h a n) -> p h a n", h=2, a=DB)
        q32 = view(R, 24, 4, F32).rearrange("p (b n) -> p b n", b=2)
        u_b = view(R, 28, 2, F32)
        junk = view(R, 12, 4, BF16).rearrange("p (s d) -> p s d", s=GT)
        khl = view(R, 32, 8, F16).rearrange("p (h s d) -> p h s d", h=2, s=GT)
        qst = view(R, 40, 8, F16).rearrange("p (s h a n) -> p s h a n", s=GT, h=2, a=DB)
        mhl = view(R, 48, 8, F16).rearrange("p (a h d) -> p a h d", a=DB, h=2)
        tt = [view(R, 16 * n, 16, F32) for n in range(2)]
        phl = view(R, 32, 16, F16).rearrange("p (h m) -> p h m", h=2)
        p32 = view(R, 48, 8, F32).rearrange("p (b m) -> p b m", b=2)
        pT = view(R, 56, 4, F16).rearrange("p (b t h n) -> p b t h n", b=2, t=4, h=2)
        qT = [view(R, 64 + 2 * n, 2, F16).rearrange("p (h a n) -> p h a n", h=2, a=DB) for n in range(2)]
        o32 = view(R, 68, 2, F32)
        w2p = view(VR, 0, 8, F16).rearrange("p (a h d) -> p a h d", a=DB, h=2)
        w1p = view(VR, 8, 8, F16).rearrange("p (a h d) -> p a h d", a=DB, h=2)
        b1_b = view(VR, 16, 2, F32)
        o_in = view(VR, 22, 8, F32).rearrange("p (s d) -> p s d", s=GT)
        xs = [view(VR, 30 + 8 * n, 8, F32).rearrange("p (s d) -> p s d", s=GT) for n in range(2)]
        ohl = view(VR, 46, 8, F16).rearrange("p (h s d) -> p h s d", h=2, s=GT)
        oT = view(R, 32, 8, F16).rearrange("p (s h a n) -> p s h a n", s=GT, h=2, a=DB)
        x1b = view(R, 40, 8, F32).rearrange("p (s d) -> p s d", s=GT)
        h2hl = view(R, 48, 8, F16).rearrange("p (h s d) -> p h s d", h=2, s=GT)
        h2T = view(R, 56, 8, F16).rearrange("p (s h a n) -> p s h a n", s=GT, h=2, a=DB)
        SUP = view(KR, 0, 64, F16).rearrange("p (t h d) -> p t h d", h=2, d=D)
        aT = view(R, 48, 4, BF16).rearrange("p (b t n) -> p b t n", b=2, t=8)
        a_bf = view(R, 32, 16, BF16).rearrange("p (b m) -> p b m", b=2)
        unequal = view(R, 52, 8, BF16)
        x1_in = [view(R, 68 + 2 * n, 2, F32) for n in range(2)]
        o_out = [view(R, 64 + 2 * n, 2, F32) for n in range(2)]
        sup32 = view(VR, 0, 64, F32).rearrange("p (t d) -> p t d", d=D)
        restT = view(R, 48, 2, F32)
        fix_in = view(R, 60, 2, F32)
        fix_out = view(R, 64, 2, F32)

        ones = sb("ones", [P, P], F32)
        ident32 = sb("ident32", [P, P], F32)
        ident16 = sb("ident16", [P, P], F16)
        identb = sb("identb", [P, P], BF16)
        b2_b = sb("b2_b", [P, D], F32)
        bcol = sb("bcol", [P, 3, DB], F32)
        cs = sb("cs", [P, DB + 1], F32)
        kmx = sb("kmx", [P, 2, NG], F32)
        mx = sb("mx", [P, 6], F32)
        gmx = sb("gmx", [P, 6], F32)
        fl = sb("fl", [P, 8], F32)
        sc = sb("sc", [P, 16], F32)
        cq = sb("cq", [P, DB], F32)
        r_s = sb("r_s", [P, NT], F32)
        stats = sb("stats", [P, GT, 6], F32)
        mv = sb("mv", [P, GT, 2], F32)
        rs = sb("rs", [P, GT], F32)
        rsum = sb("rsum", [P, HC], F32)
        rmax = sb("rmax", [P, HC], F32)
        nbias = sb("nbias", [P, 4], F32)
        linv = sb("linv", [P, 4], F32)
        miss = sb("miss", [P, NT], F32)
        miss2 = sb("miss2", [P, 2], F32)
        flag = sb("flag", [P, 1], I32)

        (G_K, G_V, G_M, G_W2, G_W1, G_Q, S_Q, S_R, S_R0, G_ALL, I_G, THR, BIG, I_O, I_S, TMP) = range(16)

        def col(n):
            return sc[:, n:n + 1]

        PS = ctx.enter_context(nc.psum_tensor("ps", [P, 8, D], F32))

        def bank(n):
            return PS[:, n, :]

        def bank16(n, dt=F16):
            return PS[:, n, :].bitcast(dt).rearrange("p (t n) -> p t n", n=P)

        wqk_in, wvm_in, w1_in, bias_in = sem("wqk_in"), sem("wvm_in"), sem("w1_in"), sem("bias_in")
        ident_zero, ident_made, cols_spread = sem("ident_zero"), sem("ident_made"), sem("cols_spread")
        weight_product, weight_evacuated = sem("weight_product"), sem("weight_evacuated")
        kscan_in, vscan_in, key_scanned, value_scanned = sem("kscan_in"), sem("vscan_in"), sem("key_scanned"), sem("value_scanned")
        maxima_made, maxima_shared, dve_own, scales_made = sem("maxima_made"), sem("maxima_shared"), sem("dve_own"), sem("scales_made")
        weight_hi, weight_lo, weights_stored = sem("weight_hi"), sem("weight_lo"), sem("weights_stored")
        x_loaded, key_loaded, value_loaded = sem("x_loaded"), sem("key_loaded"), sem("value_loaded")
        var_made, std_made, xn_made, h_hi_made, h_lo_made = [sem(s) for s in (
            "var_made", "std_made", "xn_made", "h_hi_made", "h_lo_made")]
        key_hi, key_lo, value_hi, value_lo = sem("key_hi"), sem("key_lo"), sem("value_hi"), sem("value_lo")
        keyT_made, keyT_evacuated, hT_made, hT_evacuated = sem("keyT_made"), sem("keyT_evacuated"), sem("hT_made"), sem("hT_evacuated")
        q_product, q32_made, q_hi, q_lo, q_stored = sem("q_product"), sem("q32_made"), sem("q_hi"), sem("q_lo"), sem("q_stored")
        adj_in = [sem(f"adj_in{b}") for b in range(2)]
        q_in = [sem(f"q_in{b}") for b in range(2)]
        scores_full, scores_scaled, hidden_found, scores_masked, max_chunk, shift_made = [sem(s) for s in (
            "scores_full", "scores_scaled", "hidden_found", "scores_masked", "max_chunk", "shift_made")]
        exp_made, p_hi, p_lo, pT_made, pT_evacuated = sem("exp_made"), sem("p_hi"), sem("p_lo"), sem("pT_made"), sem("pT_evacuated")
        context_full, context_made, context_stored, dve_att = sem("context_full"), sem("context_made"), sem("context_stored"), sem("dve_att")
        sum_made, inverse_made, abs_made = sem("sum_made"), sem("inverse_made"), sem("abs_made")
        proj_w_in, o_loaded, x4_loaded = sem("proj_w_in"), sem("o_loaded"), [sem(f"x4_loaded{b}") for b in range(2)]
        o_hi, o_lo, oT_made, oT_evacuated, proj_full, xb_made, x1_made = [sem(s) for s in (
            "o_hi", "o_lo", "oT_made", "oT_evacuated", "proj_full", "xb_made", "x1_made")]
        var4_made, std4_made, xn4_made, h2_hi, h2_lo, h2T_made, h2T_evacuated = [sem(s) for s in (
            "var4_made", "std4_made", "xn4_made", "h2_hi", "h2_lo", "h2T_made", "h2T_evacuated")]
        support_full, support_hi, support_lo = sem("support_full"), sem("support_hi"), sem("support_lo")
        x1b_made, x1b_stored, dve_proj = sem("x1b_made"), sem("x1b_stored"), sem("dve_proj")
        adj5_in = [sem(f"adj5_in{b}") for b in range(2)]
        x1_loaded = [sem(f"x1_loaded{b}") for b in range(2)]
        adj_rounded, adj_compared, aT_made, aT_evacuated, conv_full, out_made = [sem(s) for s in (
            "adj_rounded", "adj_compared", "aT_made", "aT_evacuated", "conv_full", "out_made")]
        out_stored = [sem(f"out_stored{b}") for b in range(2)]
        misses_summed, misses_shared, flag_made = sem("misses_summed"), sem("misses_shared"), sem("flag_made")
        sup32_made, adj6_in, rest_made, restT_made, restT_evacuated, rest_full = [sem(s) for s in (
            "sup32_made", "adj6_in", "rest_made", "restT_made", "restT_evacuated", "rest_full")]
        fix_loaded, fix_made, fix_stored, rounded6 = sem("fix_loaded"), sem("fix_made"), sem("fix_stored"), sem("rounded6")

        block = ctx.enter_context(nc.Block())

        def rows(t, n=1):
            return bass.ds(t * P, n * P)

        def group_rows(t, g):
            return t[bass.ds(g * (GT * P), GT * P), :].rearrange("(s p) d -> p s d", p=P)

        def idx(tile):
            return 2 * tile[0] + tile[1]

        def attention_steps(eng, step):
            step((0, 0), None)
            step((0, 1), (0, 0))
            step((1, 0), (0, 1))
            with eng.Fori(1, NT // 2 - 1) as j:
                step((j, 1), (j, 0))
                step((j + 1, 0), (j, 1))
            last = NT // 2 - 1
            step((last, 1), (last, 0))
            step(None, (last, 1))

        def projection_steps(step):
            step((0, 0), None, None)
            step((0, 1), (0, 0), None)
            step((1, 0), (0, 1), (0, 0))

            def pair(j):
                step((j, 1), (j, 0), (j - 1, 1))
                step((j + 1, 0), (j, 1), (j, 0))
            return pair

        def projection_end(step):
            last = NG // 2 - 1
            step((last, 1), (last, 0), (last - 1, 1))
            step(None, (last, 1), (last, 0))
            step(None, None, (last, 1))

        @block.sync
        def _(sp):
            sp.dma_start(wq_s, wq.rearrange("(a p) d -> p a d", p=P)).then_inc(wqk_in, 16)
            sp.dma_start(wk_s, wk.rearrange("(a p) d -> p a d", p=P)).then_inc(wqk_in, 16)
            with nc.allow_non_contiguous_dma(reason="three vectors of 512, once"):
                for n, v in enumerate((bq, bk, bv)):
                    sp.dma_start(bcol[:, n, :], v.rearrange("(a p) -> p a", p=P)).then_inc(bias_in, 16)
            sp.dma_start(wm_s, wm.rearrange("(a p) d -> p a d", p=P)).then_inc(wvm_in, 16)
            sp.dma_start(wv_s, wv.rearrange("(a p) d -> p a d", p=P)).then_inc(wvm_in, 16)
            sp.dma_start(bm_b, bm.rearrange("(a d) -> a d", a=1).to_broadcast([P, D])).then_inc(wvm_in, 16)
            sp.dma_start(w1_s, w1.rearrange("(a p) d -> p a d", p=P)).then_inc(w1_in, 16)

            def scan_loads(g):
                wait_from(sp, key_scanned, g)
                sp.dma_start(kv_in[0], group_rows(key, g)).then_inc(kscan_in, 16)
                wait_from(sp, value_scanned, g)
                sp.dma_start(kv_in[1], group_rows(value, g)).then_inc(vscan_in, 16)
            scan_loads(0)
            with sp.Fori(1, NG) as g:
                scan_loads(g)
            sp.wait_ge(weight_lo, 3)
            sp.wait_ge(weight_hi, 3)
            sp.dma_start(w2_scr, view(R, 8, 8, F16)).then_inc(weights_stored, 16)
            sp.dma_start(w1_scr, view(R, 16, 8, F16)).then_inc(weights_stored, 16)
            sp.wait_ge(weights_stored, 32)
            sp.wait_ge(key_scanned, NG)
            sp.wait_ge(value_scanned, NG)

            def phase2_loads(g):
                wait_from(sp, h_hi_made, g)
                wait_from(sp, h_lo_made, g)
                sp.dma_start(xg, group_rows(x, g)).then_inc(x_loaded, 16)
                wait_from(sp, key_lo, g)
                wait_from(sp, key_hi, g)
                sp.dma_start(kv_in[0], group_rows(key, g)).then_inc(key_loaded, 16)
                wait_from(sp, value_lo, g)
                wait_from(sp, value_hi, g)
                sp.dma_start(kv_in[1], group_rows(value, g)).then_inc(value_loaded, 16)

            def store_q(g):
                sp.wait_ge(q_hi, DB * (g + 1))
                sp.wait_ge(q_lo, DB * (g + 1))
                sp.dma_start(q_scr[bass.ds(g * GT, GT)].rearrange("s p m -> p s m"),
                             view(R, 40, 8, F16).rearrange("p (s m) -> p s m", s=GT)).then_inc(q_stored, 16)
            phase2_loads(0)
            with sp.Fori(1, NG) as g:
                phase2_loads(g)
                store_q(g - 1)
            store_q(NG - 1)

            sp.wait_ge(h_lo_made, NG)
            sp.wait_ge(hT_made, NG * GT)
            sp.dma_start(tt[0], adj[rows(0), :]).then_inc(adj_in[0], 16)
            sp.wait_ge(q_product, NG * DB)
            sp.wait_ge(q_lo, NG * DB)
            sp.wait_ge(q_hi, NG * DB)
            sp.dma_start(tt[1], adj[rows(1), :]).then_inc(adj_in[1], 16)
            sp.wait_ge(q_stored, 16 * NG)
            sp.wait_ge(value_lo, NG)
            sp.wait_ge(value_hi, NG)
            for b in range(2):
                sp.dma_start(qT[b], q_scr[b].rearrange("p (h a n) -> p h a n", h=2, a=DB)).then_inc(q_in[b], 16)

            def store_context(t):
                sp.wait_ge(context_made, t + 1)
                sp.dma_start(o_scr[rows(t), :], o32).then_inc(context_stored, 16)

            def attention_loads(j, b):
                t = 2 * j + b
                sp.wait_ge(exp_made, HC * (t - 1))
                sp.dma_start(tt[b], adj[rows(t), :]).then_inc(adj_in[b], 16)
                sp.wait_ge(scores_full, CH * (t - 1))
                sp.dma_start(qT[b], q_scr[bass.ds(t, 1)].rearrange("o p (h a n) -> p (o h) a n", h=2, a=DB)).then_inc(q_in[b], 16)
            attention_loads(1, 0)
            with sp.Fori(1, NT // 2 - 1) as j:
                attention_loads(j, 1)
                store_context(2 * j - 2)
                attention_loads(j + 1, 0)
                store_context(2 * j - 1)
            attention_loads(NT // 2 - 1, 1)
            for t in range(NT - 4, NT):
                store_context(t)

            sp.wait_ge(context_full, NT)
            sp.wait_ge(exp_made, HC * NT)
            sp.dma_start(view(VR, 0, 8, F16), w2_scr).then_inc(proj_w_in, 16)
            sp.dma_start(view(VR, 8, 8, F16), w1_scr).then_inc(proj_w_in, 16)
            sp.dma_start(b1_b, b1.rearrange("(a d) -> a d", a=1).to_broadcast([P, D])).then_inc(proj_w_in, 16)
            sp.wait_ge(context_stored, 16 * NT)

            def projection_loads(j, b):
                g = 2 * j + b
                wait_from(sp, o_hi, g)
                wait_from(sp, o_lo, g)
                sp.dma_start(o_in, group_rows(o_scr, g)).then_inc(o_loaded, 16)
                if not isinstance(g, int) or g >= 2:
                    sp.wait_ge(h2_hi, g - 1)
                    sp.wait_ge(h2_lo, g - 1)
                sp.dma_start(xs[b], group_rows(x, g)).then_inc(x4_loaded[b], 16)

            def store_x1(g):
                sp.wait_ge(x1b_made, GT * g + GT)
                sp.dma_start(group_rows(x1_scr, g), x1b).then_inc(x1b_stored, 16)
            projection_loads(0, 0)
            projection_loads(0, 1)
            for b in range(2):
                sp.dma_start(tt[b], adj[rows(b), :]).then_inc(adj5_in[b], 16)
            with sp.Fori(1, NG // 2) as j:
                for b in range(2):
                    projection_loads(j, b)
                    store_x1(2 * j + b - 2)
            store_x1(NG - 2)
            store_x1(NG - 1)

            sp.wait_ge(x1b_stored, 16 * NG)
            for b in range(2):
                sp.dma_start(x1_in[b], x1_scr[rows(b), :]).then_inc(x1_loaded[b], 16)

            def store_out(t, b):
                sp.wait_ge(out_made, t + 1)
                sp.dma_start(out[rows(t), :], o_out[b]).then_inc(out_stored[b], 16)
            with sp.Fori(1, NT // 2) as j:
                for b in range(2):
                    t = 2 * j + b
                    sp.wait_ge(adj_rounded, t - 1)
                    sp.wait_ge(adj_compared, t - 1)
                    sp.dma_start(tt[b], adj[rows(t), :]).then_inc(adj5_in[b], 16)
                    store_out(t - 2, b)
                    sp.dma_start(x1_in[b], x1_scr[rows(t), :]).then_inc(x1_loaded[b], 16)
            for b in range(2):
                store_out(NT - 2 + b, b)
            for b in range(2):
                sp.wait_ge(out_stored[b], 16 * NT // 2)

            sp.wait_ge(flag_made, 1)
            with sp.If(sp.value_load(flag[0:1, 0:1], min_val=0, max_val=1) > 0):
                def rest_traffic(t):
                    wait_from(sp, fix_stored, 16 * t)
                    sp.dma_start(tt[0], adj[rows(t), :]).then_inc(adj6_in, 16)
                    sp.dma_start(fix_in, out[rows(t), :]).then_inc(fix_loaded, 16)
                    sp.wait_ge(fix_made, t + 1)
                    sp.dma_start(out[rows(t), :], fix_out).then_inc(fix_stored, 16)
                rest_traffic(0)
                with sp.Fori(1, NT) as t:
                    rest_traffic(t)
                sp.wait_ge(fix_stored, 16 * NT)

        @block.gpsimd
        def _(pool):
            pool.memset(ident32[:], 0.0).then_inc(ident_zero, 1)
            pool.memset(ident16[:], 0.0).then_inc(ident_zero, 1)
            pool.memset(identb[:], 0.0).then_inc(ident_zero, 1)
            pool.wait_ge(ident_zero, 3)
            for m in (ident32, ident16, identb):
                pool.affine_select(out=m[:], in_=m[:], compare_op=ALU.not_equal, fill=1.0, base=0,
                                   pattern=[[-1, P]], channel_multiplier=1).then_inc(ident_made, 1)
            pool.wait_ge(maxima_made, 1)
            pool.partition_all_reduce(gmx[:], mx[:], P, RMAX).then_inc(maxima_shared, 1)

            pool.wait_ge(proj_w_in, 48)

            def projection_step(a, g, d):
                if a:
                    pool.wait_ge(x4_loaded[a[1]], 16 * a[0] + 16)
                    for s in range(GT):
                        pool.tensor_tensor(xs[a[1]][:, s, :], xs[a[1]][:, s, :], b2_b[:], ALU.add).then_inc(xb_made, 1)
                if g:
                    k = idx(g)
                    wait_from(pool, x1b_stored, 16 * k)
                    for s in range(GT):
                        pool.wait_ge(x1_made, GT * k + s + 1)
                        pool.tensor_tensor(x1b[:, s, :], xs[g[1]][:, s, :], b1_b, ALU.add).then_inc(x1b_made, 1)
            pair = projection_steps(projection_step)
            with pool.Fori(1, NG // 2 - 1) as j:
                pair(j)
            projection_end(projection_step)

            pool.wait_ge(misses_summed, 1)
            pool.partition_all_reduce(miss2[:, 1:2], miss2[:, 0:1], P, RADD).then_inc(misses_shared, 1)

        @block.tensor
        def _(pe):
            item = [0]

            def weight_item(emit):
                n = item[0]
                if n >= 8:
                    pe.wait_ge(weight_evacuated, n - 7)
                emit(bank(n % 8)).then_inc(weight_product, 1)
                item[0] += 1

            def product(lhs, rhs):
                def emit(to):
                    for a in range(DB):
                        last = pe.matmul(to[:, 0:rhs(a).shape[1]], lhs(a), rhs(a), start=(a == 0), stop=(a == DB - 1))
                    return last
                return emit

            pe.wait_ge(wqk_in, 32)
            for d in range(DB):
                weight_item(product(lambda a: wq_s[:, a, d * P:(d + 1) * P], lambda a: wk_s[:, a, :]))
            pe.wait_ge(bias_in, 48)
            pe.wait_ge(cols_spread, 2)
            weight_item(product(lambda a: bkb[:, a, :], lambda a: wq_s[:, a, :]))

            def columns(to):
                for d in range(DB):
                    for a in range(DB):
                        pe.matmul(to[:, d:d + 1], wk_s[:, a, d * P:(d + 1) * P], bcol[:, 0, a:a + 1],
                                  start=(a == 0), stop=(a == DB - 1))
                for a in range(DB):
                    last = pe.matmul(to[:, DB:DB + 1], bkb[:, a, :], bcol[:, 0, a:a + 1],
                                     start=(a == 0), stop=(a == DB - 1))
                return last
            weight_item(columns)
            pe.wait_ge(wvm_in, 48)
            pe.wait_ge(ident_made, 3)
            for a in range(DB):
                def turned(to, a=a):
                    for e in range(DB):
                        last = pe.transpose(to[:, e * P:(e + 1) * P], wm_s[:, e, a * P:(a + 1) * P], ident32[:])
                    return last
                weight_item(turned)
            pe.wait_ge(weight_evacuated, item[0])
            for d in range(DB):
                weight_item(product(lambda a: wv_s[:, a, d * P:(d + 1) * P], lambda a: wmT[:, a, :]))
            weight_item(product(lambda a: bvb[:, a, :], lambda a: wmT[:, a, :]))

            pe.wait_ge(weight_evacuated, item[0])

            def key_transposes(g):
                pe.wait_ge(key_hi, g + 1)
                pe.wait_ge(key_lo, g + 1)
                for s in range(GT):
                    if s >= 2 or not isinstance(g, int) or g:
                        pe.wait_ge(keyT_evacuated, GT * g + s - 1)
                    to = bank16(s % 2)
                    for h in range(2):
                        for a in range(DB):
                            last = pe.transpose(to[:, h * DB + a, :], khl[:, h, s, a * P:(a + 1) * P], ident16[:])
                    last.then_inc(keyT_made, 1)

            def h_transposes(g):
                pe.wait_ge(h_hi_made, g + 1)
                pe.wait_ge(h_lo_made, g + 1)
                for s in range(GT):
                    if s >= 2 or not isinstance(g, int) or g:
                        pe.wait_ge(hT_evacuated, GT * g + s - 1)
                    to = bank16(2 + s % 2)
                    for h in range(2):
                        for a in range(DB):
                            last = pe.transpose(to[:, h * DB + a, :], hhl[:, h, s, a * P:(a + 1) * P], ident16[:])
                    last.then_inc(hT_made, 1)

            def query_products(g):
                pe.wait_ge(hT_evacuated, GT * (g + 1))
                for o in range(DB):
                    wait_from(pe, q32_made, DB * g)
                    n = 0
                    for lh, rh in ((0, 0), (0, 1), (1, 0)):
                        for a in range(DB):
                            last = pe.matmul(bank(4 + o), mhl[:, a, lh, o * P:(o + 1) * P], hT[:, rh, a, :],
                                             start=(n == 0), stop=(n == 3 * DB - 1))
                            n += 1
                    last.then_inc(q_product, 1)
            pe.wait_ge(weight_hi, 3)
            pe.wait_ge(weight_lo, 3)
            key_transposes(0)
            h_transposes(0)
            key_transposes(1)
            query_products(0)
            h_transposes(1)
            with pe.Fori(2, NG) as g:
                key_transposes(g)
                query_products(g - 1)
                h_transposes(g)
            query_products(NG - 1)

            pe.wait_ge(keyT_evacuated, NT)
            pe.wait_ge(hT_evacuated, NT)
            pe.wait_ge(q32_made, NG * DB)
            pe.wait_ge(value_hi, NG)
            pe.wait_ge(value_lo, NG)

            def p_transposes(t, g):
                pe.wait_ge(p_hi, HC * t + g // 2 + 1)
                pe.wait_ge(p_lo, HC * t + g // 2 + 1)
                if g >= 2 or not isinstance(t, int) or t:
                    pe.wait_ge(pT_evacuated, TG * t + g)
                to = bank16(4 + g % 2)
                for m in range(4):
                    for h in range(2):
                        last = pe.transpose(to[:, 2 * m + h, :], phl[:, h, (4 * g + m) * P:(4 * g + m + 1) * P], ident16[:])
                last.then_inc(pT_made, 1)

            def context_products(t, g):
                pe.wait_ge(pT_evacuated, TG * t + g + 1)
                for m in range(4):
                    for i, (lh, rh) in enumerate(((0, 0), (0, 1), (1, 0))):
                        last = pe.matmul(bank(6), pT[:, g % 2, m, lh, :], VV[:, 4 * g + m, rh, :],
                                         start=(g == 0 and m == 0 and i == 0), stop=(g == TG - 1 and m == 3 and i == 2))
                return last

            def attention_step(s, c):
                if s:
                    t = idx(s)
                    pe.wait_ge(q_in[s[1]], 16 * s[0] + 16)
                    for n in range(CH):
                        if c and n == CH - 1:
                            p_transposes(idx(c), 0)
                        if n >= 4 or c:
                            pe.wait_ge(scores_scaled, CH * t + n - 3)
                        i = 0
                        for lh, rh in ((0, 0), (0, 1), (1, 0)):
                            for a in range(DB):
                                last = pe.matmul(bank(n % 4), qT[s[1]][:, lh, a, :], KT[:, rh, a, n * D:(n + 1) * D],
                                                 start=(i == 0), stop=(i == 3 * DB - 1))
                                i += 1
                        last.then_inc(scores_full, 1)
                elif c:
                    p_transposes(idx(c), 0)
                if c:
                    t = idx(c)
                    wait_from(pe, context_made, t)
                    for g in range(TG):
                        if g + 1 < TG:
                            p_transposes(t, g + 1)
                        last = context_products(t, g)
                    last.then_inc(context_full, 1)
            attention_steps(pe, attention_step)

            pe.wait_ge(proj_w_in, 48)

            def turn_group(first, src, g, evacuated, made):
                for s in range(GT):
                    if s >= 2 or not isinstance(g, int) or g:
                        pe.wait_ge(evacuated, GT * g + s - 1)
                    to = bank16(first + s % 2)
                    for h in range(2):
                        for a in range(DB):
                            last = pe.transpose(to[:, h * DB + a, :], src[:, h, s, a * P:(a + 1) * P], ident16[:])
                    last.then_inc(made, 1)

            def group_products(first, left, w, g, taken, full):
                for s in range(GT):
                    if s >= 2 or not isinstance(g, int) or g:
                        for t in taken:
                            pe.wait_ge(t, GT * g + s - 1)
                    n = 0
                    for lh, rh in ((0, 0), (0, 1), (1, 0)):
                        for a in range(DB):
                            last = pe.matmul(bank(first + s % 2), left[:, s, lh, a, :], w[:, a, rh, :],
                                             start=(n == 0), stop=(n == 3 * DB - 1))
                            n += 1
                    last.then_inc(full, 1)

            def projection_step(a, g, d):
                if g:
                    pe.wait_ge(oT_evacuated, GT * idx(g) + GT)
                    group_products(4, oT, w2p, idx(g), (x1_made,), proj_full)
                if a:
                    pe.wait_ge(o_hi, idx(a) + 1)
                    pe.wait_ge(o_lo, idx(a) + 1)
                    turn_group(0, ohl, idx(a), oT_evacuated, oT_made)
                if d:
                    pe.wait_ge(h2T_evacuated, GT * idx(d) + GT)
                    group_products(6, h2T, w1p, idx(d), (support_hi, support_lo), support_full)
                if g:
                    pe.wait_ge(h2_hi, idx(g) + 1)
                    pe.wait_ge(h2_lo, idx(g) + 1)
                    turn_group(2, h2hl, idx(g), h2T_evacuated, h2T_made)
            pair = projection_steps(projection_step)
            with pe.Fori(1, NG // 2 - 1) as j:
                pair(j)
            projection_end(projection_step)

            pe.wait_ge(support_hi, NT)
            pe.wait_ge(support_lo, NT)

            def adj_transposes(t, b, g):
                if g == 0:
                    pe.wait_ge(adj_rounded, t + 1)
                if g >= 2 or not isinstance(t, int) or t:
                    pe.wait_ge(aT_evacuated, 4 * t + g - 1)
                for m in range(8):
                    last = pe.transpose(bank16(4 + g % 2, BF16)[:, m, :],
                                        a_bf[:, b, (8 * g + m) * P:(8 * g + m + 1) * P], identb[:])
                last.then_inc(aT_made, 1)

            def conv_products(t, b, g):
                pe.wait_ge(aT_evacuated, 4 * t + g + 1)
                for m in range(8):
                    for h in range(2):
                        last = pe.matmul(bank(6 + b), aT[:, g % 2, m, :], SUP[:, 8 * g + m, h, :],
                                         start=(g == 0 and m == 0 and h == 0), stop=(g == 3 and m == 7 and h == 1))
                return last

            def conv_tile(t, b):
                if not isinstance(t, int) or t > 1:
                    pe.wait_ge(out_made, t - 1)
                for g in range(4):
                    if g + 1 < 4:
                        adj_transposes(t, b, g + 1)
                    last = conv_products(t, b, g)
                last.then_inc(conv_full, 1)
            adj_transposes(0, 0, 0)
            def conv_pair(j):
                for b in range(2):
                    conv_tile(2 * j + b, b)
                    adj_transposes(2 * j + b + 1, 1 - b, 0)
            conv_pair(0)
            with pe.Fori(1, NT // 2 - 1) as j:
                conv_pair(j)
            conv_tile(NT - 2, 0)
            adj_transposes(NT - 1, 1, 0)
            conv_tile(NT - 1, 1)

            pe.wait_ge(flag_made, 1)
            with pe.If(pe.value_load(flag[0:1, 0:1], min_val=0, max_val=1) > 0):
                pe.wait_ge(sup32_made, 1)
                pe.wait_ge(out_made, NT)

                def rest_tile(t):
                    pe.wait_ge(rest_made, t + 1)
                    wait_from(pe, fix_made, t)
                    for q in range(8):
                        wait_from(pe, restT_evacuated, 8 * t + q)
                        for m in range(4):
                            last = pe.transpose(bank(4)[:, m * P:(m + 1) * P], tt[1][:, (4 * q + m) * P:(4 * q + m + 1) * P], ident32[:])
                        last.then_inc(restT_made, 1)
                        pe.wait_ge(restT_evacuated, 8 * t + q + 1)
                        for m in range(4):
                            last = pe.matmul(bank(6), restT[:, m * P:(m + 1) * P], sup32[:, 4 * q + m, :],
                                             start=(q == 0 and m == 0), stop=(q == 7 and m == 3))
                    last.then_inc(rest_full, 1)
                rest_tile(0)
                with pe.Fori(1, NT) as t:
                    rest_tile(t)

        @block.scalar
        def _(act):
            homes = [m32[:, d, :] for d in range(DB)] + [u_b, cs[:]] + [wmT[:, a, :] for a in range(DB)] \
                + [w232[:, d, :] for d in range(DB)] + [b2_b[:]]
            for n, home in enumerate(homes):
                act.wait_ge(weight_product, n + 1)
                act.copy(home, bank(n % 8)[:, 0:home.shape[1]]).then_inc(weight_evacuated, 1)
            act.wait_ge(scales_made, 1)
            act.wait_ge(weight_evacuated, len(homes))
            act.activation(mhl[:, :, 0, :], m32, ACT.Copy, scale=col(G_M)).then_inc(weight_hi, 1)
            act.activation(w2hl[:, :, 0, :], w232, ACT.Copy, scale=col(G_W2)).then_inc(weight_hi, 1)
            act.activation(w1hl[:, :, 0, :], w1_s, ACT.Copy, scale=col(G_W1)).then_inc(weight_hi, 1)

            def phase2_step(g, prior):
                if g is not None:
                    act.wait_ge(key_loaded, 16 * g + 16)
                    wait_from(act, keyT_made, GT * g)
                    act.activation(khl[:, 0], kv_in[0], ACT.Copy, scale=col(G_K)).then_inc(key_hi, 1)
                    act.wait_ge(value_loaded, 16 * g + 16)
                    if isinstance(g, int) and g == 0:
                        act.wait_ge(weight_lo, 3)
                    act.activation(VV[:, bass.ds(g * GT, GT), 0, :], kv_in[1], ACT.Copy, scale=col(G_V)).then_inc(value_hi, 1)
                    act.wait_ge(var_made, g + 1)
                    act.activation(rs[:], mv[:, :, 1], ACT.Sqrt).then_inc(std_made, 1)
                    wait_from(act, hT_made, GT * g)
                    act.wait_ge(xn_made, GT * g + GT)
                    if isinstance(g, int):
                        act.wait_ge(weights_stored, 32)
                    act.activation(hhl[:, 0], xg, ACT.Relu).then_inc(h_hi_made, 1)
                    for s in range(GT):
                        act.wait_ge(keyT_made, GT * g + s + 1)
                        act.copy(KT[:, :, :, bass.ds((g * GT + s) * P, P)],
                                 bank16(s % 2).rearrange("p (h a) n -> p h a n", h=2)).then_inc(keyT_evacuated, 1)
                if prior is not None:
                    for o in range(DB):
                        act.wait_ge(q32_made, DB * prior + o + 1)
                        if o == 0:
                            wait_from(act, q_stored, 16 * prior)
                        act.copy(qst[:, :, 0, o, :], q32[:, o % 2, :].rearrange("p (s n) -> p s n", s=GT)).then_inc(q_hi, 1)
                if g is not None:
                    for s in range(GT):
                        act.wait_ge(hT_made, GT * g + s + 1)
                        if s == 0:
                            wait_from(act, q_product, DB * g)
                        act.copy(hT[:, :, :, s * P:(s + 1) * P],
                                 bank16(2 + s % 2).rearrange("p (h a) n -> p h a n", h=2)).then_inc(hT_evacuated, 1)
            phase2_step(0, None)
            phase2_step(1, 0)
            with act.Fori(2, NG) as g:
                phase2_step(g, g - 1)
            phase2_step(None, NG - 1)

            act.wait_ge(q_stored, 16 * NG)

            def take_pT(t, g):
                act.wait_ge(pT_made, TG * t + g + 1)
                act.copy(pT[:, g % 2], bank16(4 + g % 2).rearrange("p (t h) n -> p t h n", h=2)).then_inc(pT_evacuated, 1)

            def attention_step(s, c):
                def magnitudes(n):
                    t = idx(s)
                    act.wait_ge(scores_scaled, CH * t + 2 * n + 2)
                    if n >= 2:
                        act.wait_ge(scores_masked, HC * t + n - 1)
                    elif c:
                        act.wait_ge(p_lo, HC * t)
                    act.activation(p32[:, n % 2, :], tt[s[1]][:, n * SC:(n + 1) * SC], ACT.Abs).then_inc(abs_made, 1)

                def exponentials(n):
                    t = idx(s)
                    if n == 0:
                        act.wait_ge(shift_made, t + 1)
                    if n >= 2:
                        act.wait_ge(p_lo, HC * t + n - 1)
                    act.activation(p32[:, n % 2, :], tt[s[1]][:, n * SC:(n + 1) * SC], ACT.Exp,
                                   bias=nbias[:, 2:3], scale=col(I_G), accum_out=rsum[:, n:n + 1]).then_inc(exp_made, 1)

                def upper_parts(n):
                    t = idx(s)
                    act.wait_ge(exp_made, HC * t + n + 1)
                    if c:
                        act.wait_ge(pT_made, TG * idx(c) + 2 * n + 2)
                    act.copy(phl[:, 0, n * SC:(n + 1) * SC], p32[:, n % 2, :]).then_inc(p_hi, 1)

                if s:
                    for n in range(HC - 1):
                        magnitudes(n)
                if c:
                    take_pT(idx(c), 0)
                if s:
                    magnitudes(HC - 1)
                if c:
                    take_pT(idx(c), 1)
                for g in range(2, TG):
                    if c:
                        take_pT(idx(c), g)
                    if s and g % 2 == 0:
                        exponentials(g // 2 - 1)
                    if s and g % 2:
                        upper_parts(g // 2 - 1)
                if s:
                    exponentials(HC - 1)
                    upper_parts(HC - 1)
            attention_steps(act, attention_step)

            act.wait_ge(context_full, NT)

            def take_turned(to, g, bank0, made, evacuated):
                for s in range(GT):
                    act.wait_ge(made, GT * g + s + 1)
                    act.copy(to[:, s], bank16(bank0 + s % 2).rearrange("p (h a) n -> p h a n", h=2)).then_inc(evacuated, 1)

            def support_upper(g, s):
                act.wait_ge(support_full, GT * g + s + 1)
                act.activation(SUP[:, bass.ds(GT * g + s, 1), 0, :].rearrange("p t d -> p (t d)"), bank(6 + s % 2), ACT.Copy,
                               scale=SUPPORT_SCALE).then_inc(support_hi, 1)

            def projection_step(a, g, d):
                if a:
                    act.wait_ge(o_loaded, 16 * idx(a) + 16)
                    wait_from(act, oT_made, GT * idx(a))
                    act.copy(ohl[:, 0], o_in).then_inc(o_hi, 1)
                    if g:
                        act.wait_ge(proj_full, GT * idx(g) + GT)
                    take_turned(oT, idx(a), 0, oT_made, oT_evacuated)
                if g:
                    act.wait_ge(var4_made, idx(g) + 1)
                    act.activation(rs[:], mv[:, :, 1], ACT.Sqrt).then_inc(std4_made, 1)
                if d:
                    support_upper(idx(d), 0)
                if g:
                    act.wait_ge(xn4_made, GT * idx(g) + GT)
                    wait_from(act, h2T_made, GT * idx(g))
                    act.activation(h2hl[:, 0], xs[g[1]], ACT.Relu).then_inc(h2_hi, 1)
                if d:
                    for s in range(1, GT):
                        support_upper(idx(d), s)
                if g:
                    take_turned(h2T, idx(g), 2, h2T_made, h2T_evacuated)
            pair = projection_steps(projection_step)
            with act.Fori(1, NG // 2 - 1) as j:
                pair(j)
            projection_end(projection_step)

            def take_aT(t):
                for g in range(4):
                    act.wait_ge(aT_made, 4 * t + g + 1)
                    act.copy(aT[:, g % 2], bank16(4 + g % 2, BF16)).then_inc(aT_evacuated, 1)
            with act.Fori(0, NT) as t:
                take_aT(t)

            act.wait_ge(flag_made, 1)
            with act.If(act.value_load(flag[0:1, 0:1], min_val=0, max_val=1) > 0):
                with act.Fori(0, NT) as t:
                    for q in range(8):
                        act.wait_ge(restT_made, 8 * t + q + 1)
                        act.copy(restT, bank(4)).then_inc(restT_evacuated, 1)

        @block.vector
        def _(dve):
            own = Chain(dve, dve_own)
            own.mark(dve.memset(ones[:], 1.0))
            own.settle()
            dve.wait_ge(bias_in, 48)
            for n, spread in ((1, bkb), (2, bvb)):
                for a in range(DB):
                    last = dve.tensor_scalar(spread[:, a, :], ones[:], bcol[:, n, a:a + 1], None, ALU.mult)
                last.then_inc(cols_spread, 1)

            with dve.Fori(0, NG) as g:
                for n, (loaded, scanned) in enumerate(((kscan_in, key_scanned), (vscan_in, value_scanned))):
                    dve.wait_ge(loaded, 16 * g + 16)
                    dve.tensor_reduce(kmx[:, n, bass.ds(g, 1)], kv_in[n], AX_XY, ALU.max,
                                      apply_absolute_value=True).then_inc(scanned, 1)
            dve.wait_ge(weight_evacuated, 15)
            dve.wait_ge(w1_in, 16)
            dve.wait_ge(wvm_in, 48)
            own.mark(dve.tensor_tensor(b2_b[:], b2_b[:], bm_b, ALU.add))
            dve.wait_ge(key_scanned, NG)
            dve.wait_ge(value_scanned, NG)
            own.mark(dve.tensor_reduce(mx[:, 0:2], kmx[:], AX_X, ALU.max))
            for n, w in ((2, m32), (4, w232), (5, w1_s)):
                own.mark(dve.tensor_reduce(mx[:, n:n + 1], w, AX_XY, ALU.max, apply_absolute_value=True))
            dve.tensor_reduce(mx[:, 3:4], cs[:, 0:DB], AX_X, ALU.max, apply_absolute_value=True).then_inc(maxima_made, 1)

            dve.wait_ge(maxima_shared, 1)
            own.mark(dve.tensor_scalar(sc[:, TMP:TMP + 1], gmx[:, 2:3], float(D), gmx[:, 3:4], ALU.mult, ALU.add))
            own.settle()
            own.mark(dve.tensor_copy(gmx[:, 3:4], sc[:, TMP:TMP + 1]))
            own.settle()
            own.mark(dve.tensor_scalar(gmx[:], gmx[:], 2.0 ** -20, None, ALU.max))
            own.settle()
            own.mark(dve.tensor_scalar(fl[:, 0:6].bitcast(I32), gmx[:].bitcast(I32), EXPONENT_BITS, None, ALU.bitwise_and))
            own.settle()
            own.mark(dve.reciprocal(gmx[:], fl[:, 0:6]))
            own.settle()
            for to, n in ((G_K, 0), (G_V, 1), (G_M, 2), (G_Q, 3), (G_W2, 4), (G_W1, 5)):
                own.mark(dve.tensor_scalar(col(to), gmx[:, n:n + 1], TOP, None, ALU.mult))
            own.settle()
            own.mark(dve.tensor_scalar(col(S_Q), fl[:, 2:3], 1.0 / (H_SCALE * TOP), col(G_Q), ALU.mult, ALU.mult))
            own.mark(dve.tensor_scalar(col(S_R0), col(G_Q), col(G_K), None, ALU.mult))
            own.settle()
            own.mark(dve.tensor_scalar(col(S_R), col(S_R0), 1.0 / H_SCALE, None, ALU.mult))
            own.mark(dve.tensor_scalar(col(G_ALL), col(S_R0), SCORE_DIV, None, ALU.mult))
            own.settle()
            own.mark(dve.reciprocal(col(I_G), col(G_ALL)))
            own.mark(dve.tensor_scalar(col(THR), col(G_ALL), NEAR_ZERO, None, ALU.mult))
            own.mark(dve.tensor_scalar(col(BIG), col(G_ALL), MASKED, None, ALU.mult))
            own.mark(dve.tensor_scalar(col(I_O), fl[:, 1:2], TOP ** -2, fl[:, 4:5], ALU.mult, ALU.mult))
            own.mark(dve.tensor_scalar(col(I_S), fl[:, 5:6], D / TOP, None, ALU.mult))
            own.mark(dve.tensor_scalar(cq[:], cs[:, 0:DB], col(G_Q), None, ALU.mult))
            own.mark(dve.tensor_scalar(col(S_R0), cs[:, DB:DB + 1], col(S_R0), None, ALU.mult))
            own.settle()
            dve.tensor_scalar(u_b, u_b, col(S_R), None, ALU.mult).then_inc(scales_made, 1)
            dve.wait_ge(scales_made, 1)
            for n, (hl, w, g) in enumerate(((mhl, m32, G_M), (w2hl, w232, G_W2), (w1hl, w1_s, G_W1))):
                dve.wait_ge(weight_hi, n + 1)
                for a in range(DB):
                    last = dve.scalar_tensor_tensor(hl[:, a, 1, :], w[:, a, :], col(g), hl[:, a, 0, :], ALU.mult, ALU.subtract)
                last.then_inc(weight_lo, 1)
            own.settle()

            BASE2 = own.base + own.k
            PER2 = 5

            def phase2_step(g, prior):
                own.rebase(BASE2 + (PER2 * g if g is not None else PER2 * NG))
                if g is not None:
                    dve.wait_ge(x_loaded, 16 * g + 16)
                    if isinstance(g, int):
                        dve.wait_ge(weights_stored, 32)
                    for s in range(GT):
                        last = dve.bn_stats(stats[:, s, :], xg[:, s, :])
                    own.mark(last)
                    dve.wait_ge(key_loaded, 16 * g + 16)
                    dve.wait_ge(key_hi, g + 1)
                    own.settle()
                    dve.scalar_tensor_tensor(khl[:, 1].rearrange("p s d -> p (s d)"), kv_in[0].rearrange("p s d -> p (s d)"), col(G_K),
                                             khl[:, 0].rearrange("p s d -> p (s d)"), ALU.mult, ALU.subtract).then_inc(key_lo, 1)
                    for s in range(GT):
                        last = dve.bn_aggr(mv[:, s, :], stats[:, s, :])
                    own.mark(last)
                    own.settle()
                    dve.tensor_scalar(mv[:, :, 1], mv[:, :, 1], EPS, None, ALU.add).then_inc(var_made, 1)
                    dve.wait_ge(std_made, g + 1)
                    own.mark(dve.reciprocal(rs[:], rs[:]))
                    own.settle()
                    own.mark(dve.tensor_scalar(rs[:], rs[:], H_SCALE, None, ALU.mult))
                    own.settle()
                    for s in range(GT):
                        dve.tensor_scalar(xg[:, s, :], xg[:, s, :], mv[:, s, 0:1], rs[:, s:s + 1],
                                          ALU.subtract, ALU.mult).then_inc(xn_made, 1)
                    dve.wait_ge(value_loaded, 16 * g + 16)
                    dve.wait_ge(value_hi, g + 1)
                    dve.scalar_tensor_tensor(VV[:, bass.ds(g * GT, GT), 1, :], kv_in[1], col(G_V),
                                             VV[:, bass.ds(g * GT, GT), 0, :], ALU.mult, ALU.subtract).then_inc(value_lo, 1)
                    dve.wait_ge(xn_made, GT * g + GT)
                    wait_from(dve, hT_made, GT * g)
                    for s in range(GT):
                        last = dve.scalar_tensor_tensor(junk[:, s, :], xg[:, s, :], 0.0, u_b, ALU.max, ALU.mult,
                                                        accum_out=r_s[:, bass.ds(g * GT + s, 1)])
                    own.mark(last)
                    own.settle()
                    dve.wait_ge(h_hi_made, g + 1)
                    dve.scalar_tensor_tensor(hhl[:, 1].rearrange("p s d -> p (s d)"), xg.rearrange("p s d -> p (s d)"), 0.0,
                                             hhl[:, 0].rearrange("p s d -> p (s d)"), ALU.max, ALU.subtract).then_inc(h_lo_made, 1)
                    assert own.k == PER2
                if prior is not None:
                    for o in range(DB):
                        if o >= 2:
                            dve.wait_ge(q_hi, DB * prior + o - 1)
                        else:
                            wait_from(dve, q_hi, DB * prior)
                        dve.wait_ge(q_product, DB * prior + o + 1)
                        dve.tensor_scalar(q32[:, o % 2, :], bank(4 + o), col(S_Q), cq[:, o:o + 1],
                                          ALU.mult, ALU.add).then_inc(q32_made, 1)
                        dve.wait_ge(q_hi, DB * prior + o + 1)
                        dve.tensor_tensor(qst[:, :, 1, o, :], q32[:, o % 2, :].rearrange("p (s n) -> p s n", s=GT),
                                          qst[:, :, 0, o, :], ALU.subtract).then_inc(q_lo, 1)
            phase2_step(0, None)
            phase2_step(1, 0)
            with dve.Fori(2, NG) as g:
                phase2_step(g, g - 1)
            phase2_step(None, NG - 1)
            own.rebase(BASE2 + PER2 * NG)
            own.mark(dve.tensor_scalar(r_s[:], r_s[:], col(S_R0), None, ALU.add))
            own.settle()

            att = Chain(dve, dve_att)

            def mask_chunk(t, T, m):
                wide = T[:, m * SC:(m + 1) * SC]
                dve.wait_ge(abs_made, HC * t + m + 1)
                dve.tensor_scalar(p32[:, m % 2, :], p32[:, m % 2, :], col(THR), col(BIG),
                                  ALU.is_lt, ALU.mult).then_inc(hidden_found, 1)
                dve.wait_ge(hidden_found, HC * t + m + 1)
                dve.tensor_tensor(wide, wide, p32[:, m % 2, :], ALU.add).then_inc(scores_masked, 1)
                dve.wait_ge(scores_masked, HC * t + m + 1)
                dve.tensor_reduce(rmax[:, m:m + 1], wide, AX_X, ALU.max).then_inc(max_chunk, 1)

            def attention_step(s, c):
                if s:
                    t = idx(s)
                    T = tt[s[1]]
                    dve.wait_ge(adj_in[s[1]], 16 * s[0] + 16)
                    for n in range(CH):
                        dve.wait_ge(scores_full, CH * t + n + 1)
                        chunk = T[:, n * D:(n + 1) * D]
                        dve.scalar_tensor_tensor(chunk, bank(n % 4), r_s[:, bass.ds(t, 1)], chunk,
                                                 ALU.add, ALU.mult).then_inc(scores_scaled, 1)
                        if n % 2 == 0 and n:
                            mask_chunk(t, T, n // 2 - 1)
                    mask_chunk(t, T, HC - 1)
                    dve.wait_ge(max_chunk, HC * t + HC)
                    att.rebase(2 * t)
                    att.mark(dve.tensor_reduce(nbias[:, 0:1], rmax[:], AX_X, ALU.max))
                    att.settle()
                    att.mark(dve.tensor_scalar(nbias[:, 1:2], nbias[:, 0:1], col(I_G), -1.0, ALU.mult, ALU.mult))
                    att.settle()
                    dve.tensor_scalar(nbias[:, 2:3], nbias[:, 1:2], P_SHIFT, None, ALU.add).then_inc(shift_made, 1)
                if s:
                    for m in range(HC):
                        dve.wait_ge(p_hi, HC * t + m + 1)
                        dve.tensor_tensor(phl[:, 1, m * SC:(m + 1) * SC], p32[:, m % 2, :],
                                          phl[:, 0, m * SC:(m + 1) * SC], ALU.subtract).then_inc(p_lo, 1)
                if c:
                    dve.wait_ge(context_full, idx(c) + 1)
                    wait_from(dve, context_stored, 16 * idx(c))
                    dve.tensor_scalar(o32, bank(6), linv[:, 1:2], None, ALU.mult).then_inc(context_made, 1)
                if s:
                    dve.wait_ge(exp_made, HC * t + HC)
                    dve.tensor_reduce(linv[:, 0:1], rsum[:], AX_X, ALU.add).then_inc(sum_made, 1)
                    dve.wait_ge(sum_made, t + 1)
                    dve.reciprocal(linv[:, 1:2], linv[:, 0:1]).then_inc(inverse_made, 1)
                    dve.wait_ge(inverse_made, t + 1)
            attention_steps(dve, attention_step)

            dve.wait_ge(context_full, NT)
            dve.wait_ge(proj_w_in, 48)
            proj = Chain(dve, dve_proj)
            PER4 = 5

            def support_lower(g, s):
                dve.wait_ge(support_hi, GT * g + s + 1)
                home = SUP[:, bass.ds(GT * g + s, 1)]
                dve.scalar_tensor_tensor(home[:, :, 1, :].rearrange("p t d -> p (t d)"), bank(6 + s % 2), SUPPORT_SCALE,
                                         home[:, :, 0, :].rearrange("p t d -> p (t d)"), ALU.mult, ALU.subtract).then_inc(support_lo, 1)

            def projection_step(a, g, d):
                if a:
                    dve.wait_ge(o_hi, idx(a) + 1)
                    dve.tensor_tensor(ohl[:, 1], o_in, ohl[:, 0], ALU.subtract).then_inc(o_lo, 1)
                if g:
                    k, X = idx(g), xs[g[1]]
                    proj.rebase(PER4 * k)
                    dve.wait_ge(xb_made, GT * k + GT)
                    for s in range(GT + 1):
                        if s < GT:
                            dve.wait_ge(proj_full, GT * k + s + 1)
                            dve.scalar_tensor_tensor(X[:, s, :], bank(4 + s % 2), col(I_O), X[:, s, :],
                                                     ALU.mult, ALU.add).then_inc(x1_made, 1)
                        if s:
                            dve.wait_ge(x1_made, GT * k + s)
                            last = dve.bn_stats(stats[:, s - 1, :], X[:, s - 1, :])
                    proj.mark(last)
                    proj.settle()
                    proj.mark(dve.memset(rs[:], 0.0))
                    for s in range(GT):
                        last = dve.bn_aggr(mv[:, s, :], stats[:, s, :])
                    proj.mark(last)
                    proj.settle()
                    dve.tensor_scalar(mv[:, :, 1], mv[:, :, 1], EPS, None, ALU.add).then_inc(var4_made, 1)
                if d:
                    support_lower(idx(d), 0)
                if g:
                    dve.wait_ge(std4_made, k + 1)
                    proj.mark(dve.reciprocal(rs[:], rs[:]))
                    proj.settle()
                    proj.mark(dve.tensor_scalar(rs[:], rs[:], H_SCALE, None, ALU.mult))
                    proj.settle()
                    dve.wait_ge(x1b_made, GT * k + GT)
                    for s in range(GT):
                        dve.tensor_scalar(X[:, s, :], X[:, s, :], mv[:, s, 0:1], rs[:, s:s + 1],
                                          ALU.subtract, ALU.mult).then_inc(xn4_made, 1)
                    assert proj.k == PER4
                if d:
                    support_lower(idx(d), 1)
                if g:
                    dve.wait_ge(h2_hi, k + 1)
                    dve.scalar_tensor_tensor(h2hl[:, 1].rearrange("p s d -> p (s d)"), X.rearrange("p s d -> p (s d)"), 0.0,
                                             h2hl[:, 0].rearrange("p s d -> p (s d)"), ALU.max, ALU.subtract).then_inc(h2_lo, 1)
                if d:
                    for s in range(2, GT):
                        support_lower(idx(d), s)
            pair = projection_steps(projection_step)
            with dve.Fori(1, NG // 2 - 1) as j:
                pair(j)
            projection_end(projection_step)
            dve.wait_ge(x1b_stored, 16 * NG)

            dve.wait_ge(pT_evacuated, TG * NT)

            def conv_step(j, b):
                t = 2 * j + b
                dve.wait_ge(adj5_in[b], 16 * j + 16)
                if not isinstance(j, int) or t:
                    dve.wait_ge(aT_made, 4 * t - 4)
                wait_from(dve, adj_compared, t)
                dve.tensor_copy(a_bf[:, b, :], tt[b]).then_inc(adj_rounded, 1)
                dve.wait_ge(adj_rounded, t + 1)
                dve.scalar_tensor_tensor(unequal, tt[b], 0.0, a_bf[:, b, :], ALU.add, ALU.not_equal,
                                         accum_out=miss[:, bass.ds(t, 1)]).then_inc(adj_compared, 1)

            def conv_out(j, b):
                t = 2 * j + b
                dve.wait_ge(conv_full, t + 1)
                dve.wait_ge(x1_loaded[b], 16 * j + 16)
                wait_from(dve, out_stored[b], 16 * j)
                dve.scalar_tensor_tensor(o_out[b], bank(6 + b), col(I_S), x1_in[b], ALU.mult, ALU.add).then_inc(out_made, 1)

            def conv_pair(j):
                conv_step(j, 1)
                conv_out(j, 0)
                conv_step(j + 1, 0)
                conv_out(j, 1)
            conv_step(0, 0)
            conv_pair(0)
            with dve.Fori(1, NT // 2 - 1) as j:
                conv_pair(j)
            conv_step(NT // 2 - 1, 1)
            conv_out(NT // 2 - 1, 0)
            conv_out(NT // 2 - 1, 1)

            dve.wait_ge(adj_compared, NT)
            dve.tensor_reduce(miss2[:, 0:1], miss[:], AX_X, ALU.add).then_inc(misses_summed, 1)
            dve.wait_ge(misses_shared, 1)
            dve.tensor_scalar(flag[:], miss2[:, 1:2], 1.0, None, ALU.min).then_inc(flag_made, 1)
            dve.wait_ge(flag_made, 1)
            with dve.If(dve.value_load(flag[0:1, 0:1], min_val=0, max_val=1) > 0):
                dve.tensor_tensor(sup32, SUP[:, :, 0, :], SUP[:, :, 1, :], ALU.add).then_inc(sup32_made, 1)

                def rest_step(t):
                    dve.wait_ge(adj6_in, 16 * t + 16)
                    dve.tensor_copy(a_bf[:, 0, :], tt[0]).then_inc(rounded6, 1)
                    dve.wait_ge(rounded6, t + 1)
                    dve.tensor_tensor(tt[1], tt[0], a_bf[:, 0, :], ALU.subtract).then_inc(rest_made, 1)
                    dve.wait_ge(rest_full, t + 1)
                    dve.wait_ge(fix_loaded, 16 * t + 16)
                    wait_from(dve, fix_stored, 16 * t)
                    dve.scalar_tensor_tensor(fix_out, bank(6), col(I_S), fix_in, ALU.mult, ALU.add).then_inc(fix_made, 1)
                rest_step(0)
                with dve.Fori(1, NT) as t:
                    rest_step(t)


_INS = ["x", "adj", "L0_gnn_key", "L0_gnn_value", "L0_gnn_Wq", "L0_gnn_bq", "L0_gnn_Wk", "L0_gnn_bk",
        "L0_gnn_Wv", "L0_gnn_bv", "L0_gnn_Wm", "L0_gnn_bm", "L1_gnn_weight", "L1_gnn_bias"]


def kernel(**inputs):
    import numpy as _np
    import concourse.bacc as _bacc
    from concourse import mybir as _mybir
    from concourse.bass_utils import run_bass_kernel_spmd as _run

    nc = _bacc.Bacc("TRN2", target_bir_lowering=False, num_devices=1)
    arrays, args = {}, []
    for name in _INS:
        a = _np.ascontiguousarray(inputs[name])
        arrays[f"in_{name}_dram"] = a
        args.append(nc.dram_tensor(f"in_{name}_dram", a.shape, _mybir.dt.from_np(a.dtype), kind="ExternalInput").ap())
    args.append(nc.dram_tensor("out_dram", (N, D), F32, kind="ExternalOutput").ap())
    program(nc, *args)
    r = _run(nc, [arrays], core_ids=[0])
    return r.results[0]["out_dram"]
```

```python
import concourse.bass as bass
from concourse import mybir

F32 = mybir.dt.float32
F16 = mybir.dt.float16
BF16 = mybir.dt.bfloat16
I32 = mybir.dt.int32
ALU = mybir.AluOpType
ACT = mybir.ActivationFunctionType
AX_X = mybir.AxisListType.X
AX_XY = mybir.AxisListType.XY
RMAX = bass.bass_isa.ReduceOp.max
RADD = bass.bass_isa.ReduceOp.add

P = 128
N = 4096
D = 512
DB = D // P
NT = N // P
GT = 4
NG = NT // GT
CH = N // D
HC = CH // 2
SC = N // HC
TG = NT // 4
KB = 1024

EPS = 1e-5
NEAR_ZERO = 1e-5
MASKED = -1e9
H_SCALE = 256.0
P_SHIFT = 9.0
TOP = 2.0 ** 14
SCORE_DIV = float(N) ** 0.5
EXPONENT_BITS = 0x7F800000
SUPPORT_SCALE = 1.0 / (H_SCALE * D)


def wait_from(eng, sem, count):
    if not isinstance(count, int) or count > 0:
        eng.wait_ge(sem, count)


class Chain:

    def __init__(self, eng, sem):
        self.eng, self.sem, self.base, self.k = eng, sem, 0, 0

    def mark(self, ins):
        self.k += 1
        return ins.then_inc(self.sem, 1)

    def settle(self):
        self.eng.wait_ge(self.sem, self.base + self.k)

    def rebase(self, base):
        self.base, self.k = base, 0


def program(nc, x, adj, key, value, wq, bq, wk, bk, wv, bv, wm, bm, w1, b1, out):
    from contextlib import ExitStack
    ctx = ExitStack()
    with ctx:
        def sb(name, shape, dt):
            return ctx.enter_context(nc.sbuf_tensor(name, shape, dt))

        def sem(name):
            return ctx.enter_context(nc.semaphore(name))

        q_scr = nc.dram_tensor("q_scr", (NT, P, 2 * DB * P), F16, kind="Internal").ap()
        w2_scr = nc.dram_tensor("w2_scr", (P, DB * 2 * D), F16, kind="Internal").ap()
        w1_scr = nc.dram_tensor("w1_scr", (P, DB * 2 * D), F16, kind="Internal").ap()
        o_scr = nc.dram_tensor("o_scr", (N, D), F32, kind="Internal").ap()
        x1_scr = nc.dram_tensor("x1_scr", (N, D), F32, kind="Internal").ap()

        KR = sb("key_region", [P, 16 * KB], F32)
        VR = sb("value_region", [P, 16 * KB], F32)
        R = sb("work_region", [P, 18 * KB], F32)

        def view(region, kb, size_kb, dt):
            w = region[:, kb * KB // 4:(kb + size_kb) * KB // 4]
            return w if dt == F32 else w.bitcast(dt)

        KT = view(KR, 0, 64, F16).rearrange("p (h a n) -> p h a n", h=2, a=DB)
        VV = view(VR, 0, 64, F16).rearrange("p (t h d) -> p t h d", h=2, d=D)
        def wview(region, kb):
            return view(region, kb, 8, F32).rearrange("p (a d) -> p a d", a=DB)
        wq_s, wk_s, wv_s, wm_s, wmT, m32 = [wview(KR, 8 * n) for n in range(6)]
        bkb = view(KR, 48, 2, F32).rearrange("p (a n) -> p a n", a=DB)
        bvb = view(KR, 50, 2, F32).rearrange("p (a n) -> p a n", a=DB)
        bm_b = view(KR, 52, 2, F32)
        w232, w1_s = wview(KR, 54), wview(KR, 24)
        key32 = view(VR, 0, 64, F32).rearrange("p (t d) -> p t d", d=D)
        junk = view(R, 60, 4, BF16).rearrange("p (s d) -> p s d", s=GT)
        xg = [view(R, 8 * n, 8, F32).rearrange("p (s d) -> p s d", s=GT) for n in range(2)]
        hT = [view(r, kb, 8, F16).rearrange("p (h a n) -> p h a n", h=2, a=DB) for r, kb in ((KR, 0), (R, 16))]
        mhl = view(R, 24, 8, F16).rearrange("p (a h d) -> p a h d", a=DB, h=2)
        qst = view(R, 32, 8, F16).rearrange("p (s h a n) -> p s h a n", s=GT, h=2, a=DB)
        q32 = view(R, 40, 4, F32).rearrange("p (b n) -> p b n", b=2)
        u_b = view(R, 44, 2, F32)
        value_homes = [view(R, kb, 8, F32).rearrange("p (s d) -> p s d", s=GT) for kb in (48, 56, 32, 40)]
        value_scan = value_homes[0]
        w2hl, w1hl = [view(R, kb, 8, F16).rearrange("p (a h d) -> p a h d", a=DB, h=2) for kb in (64, 56)]
        tt = [view(R, 16 * n, 16, F32) for n in range(2)]
        phl = view(R, 32, 16, F16).rearrange("p (h m) -> p h m", h=2)
        p32 = view(R, 48, 8, F32).rearrange("p (b m) -> p b m", b=2)
        pT = view(R, 56, 4, F16).rearrange("p (b t h n) -> p b t h n", b=2, t=4, h=2)
        qT = [view(R, 64 + 2 * n, 2, F16).rearrange("p (h a n) -> p h a n", h=2, a=DB) for n in range(2)]
        o32 = view(R, 68, 2, F32)
        o_in = view(R, 0, 8, F32).rearrange("p (s d) -> p s d", s=GT)
        xs = [view(r, kb, 8, F32).rearrange("p (s d) -> p s d", s=GT) for r, kb in ((R, 8), (VR, 0))]
        w2p = view(R, 16, 8, F16).rearrange("p (a h d) -> p a h d", a=DB, h=2)
        w1p = view(R, 24, 8, F16).rearrange("p (a h d) -> p a h d", a=DB, h=2)
        oT = view(R, 32, 8, F16).rearrange("p (s h a n) -> p s h a n", s=GT, h=2, a=DB)
        ohl = view(R, 48, 8, F16).rearrange("p (h s d) -> p h s d", h=2, s=GT)
        b1_b = view(R, 60, 2, F32)
        x1b = view(VR, 8, 8, F32).rearrange("p (s d) -> p s d", s=GT)
        h2hl = view(VR, 16, 8, F16).rearrange("p (h s d) -> p h s d", h=2, s=GT)
        h2T = view(VR, 24, 8, F16).rearrange("p (s h a n) -> p s h a n", s=GT, h=2, a=DB)
        SUP = view(KR, 0, 64, F16).rearrange("p (t h d) -> p t h d", h=2, d=D)
        aT = view(R, 48, 4, BF16).rearrange("p (b t n) -> p b t n", b=2, t=8)
        a_bf = view(R, 32, 16, BF16).rearrange("p (b m) -> p b m", b=2)
        unequal = view(R, 52, 8, BF16)
        x1_in = [view(R, 68 + 2 * n, 2, F32) for n in range(2)]
        o_out = [view(R, 64 + 2 * n, 2, F32) for n in range(2)]
        sup32 = view(VR, 0, 64, F32).rearrange("p (t d) -> p t d", d=D)
        restT = view(R, 48, 2, F32)
        fix_in = view(R, 60, 2, F32)
        fix_out = view(R, 64, 2, F32)

        ones = sb("ones", [P, P], F32)
        ident32 = sb("ident32", [P, P], F32)
        ident16 = sb("ident16", [P, P], F16)
        identb = sb("identb", [P, P], BF16)
        b2_b = sb("b2_b", [P, D], F32)
        bcol = sb("bcol", [P, 3, DB], F32)
        cs = sb("cs", [P, DB + 1], F32)
        kmx = sb("kmx", [P, 2, NG], F32)
        mx = sb("mx", [P, 6], F32)
        gmx = sb("gmx", [P, 6], F32)
        fl = sb("fl", [P, 8], F32)
        sc = sb("sc", [P, 16], F32)
        cq = sb("cq", [P, DB], F32)
        r_s = sb("r_s", [P, NT], F32)
        stats = sb("stats", [P, GT, 6], F32)
        mv = sb("mv", [P, GT, 2], F32)
        rs = sb("rs", [P, GT], F32)
        mean_rs = sb("mean_rs", [P, GT], F32)
        rsum = sb("rsum", [P, HC], F32)
        rmax = sb("rmax", [P, HC], F32)
        nbias = sb("nbias", [P, 4], F32)
        linv = sb("linv", [P, 4], F32)
        miss = sb("miss", [P, NT], F32)
        miss2 = sb("miss2", [P, 2], F32)
        flag = sb("flag", [P, 1], I32)

        (G_M, G_Q, G_K, G_V, G_W2, G_W1, S_Q, S_R, G_QK, G_ALL, I_G, THR, BIG, I_O, I_S, R0) = range(16)

        def col(n):
            return sc[:, n:n + 1]

        PS = ctx.enter_context(nc.psum_tensor("ps", [P, 8, D], F32))

        def bank(n):
            return PS[:, n, :]

        def bank16(n, dt=F16):
            return PS[:, n, :].bitcast(dt).rearrange("p (t n) -> p t n", n=P)

        wqk_in = [sem(f"wqk_in{a}") for a in range(DB)]
        wvm_in, w1_in, bias_in = sem("wvm_in"), sem("w1_in"), sem("bias_in")
        ident_zero, ident_made, cols_spread = sem("ident_zero"), sem("ident_made"), sem("cols_spread")
        weight_product, weight_evacuated = sem("weight_product"), sem("weight_evacuated")
        maxima_made, maxima_shared, dve_own, scales_made = sem("maxima_made"), sem("maxima_shared"), sem("dve_own"), sem("scales_made")
        weight_hi, weight_lo, rs_made = sem("weight_hi"), sem("weight_lo"), sem("rs_made")
        w2_stored, w1_stored = sem("w2_stored"), sem("w1_stored")
        x_loaded = [sem(f"x_loaded{b}") for b in range(2)]
        key_loaded = [sem(f"key_loaded{b}") for b in range(2)]
        vscan_in, key_scanned, value_scanned = sem("vscan_in"), sem("key_scanned"), sem("value_scanned")
        var_made, std_made, xn_made, h_hi, h_lo, r_made = [sem(n) for n in (
            "var_made", "std_made", "xn_made", "h_hi", "h_lo", "r_made")]
        hT_made, q_product, q32_made, q_hi, q_lo, q_stored = [sem(n) for n in (
            "hT_made", "q_product", "q32_made", "q_hi", "q_lo", "q_stored")]
        value_loaded = [sem(f"value_loaded{b}") for b in range(4)]
        keyT_made, key_hi, key_lo, value_hi, value_lo = [sem(n) for n in (
            "keyT_made", "key_hi", "key_lo", "value_hi", "value_lo")]
        value_scaled, value_lo_pool = sem("value_scaled"), sem("value_lo_pool")
        adj_in = [sem(f"adj_in{b}") for b in range(2)]
        q_in = [sem(f"q_in{b}") for b in range(2)]
        scores_full, scores_scaled, hidden_found, scores_masked, max_chunk, shift_made = [sem(s) for s in (
            "scores_full", "scores_scaled", "hidden_found", "scores_masked", "max_chunk", "shift_made")]
        exp_made, p_hi, p_lo, pT_made, pT_evacuated = sem("exp_made"), sem("p_hi"), sem("p_lo"), sem("pT_made"), sem("pT_evacuated")
        context_full, context_made, context_stored, dve_att = sem("context_full"), sem("context_made"), sem("context_stored"), sem("dve_att")
        sum_made, inverse_made, abs_made = sem("sum_made"), sem("inverse_made"), sem("abs_made")
        proj_w_in, o_loaded, x4_loaded = sem("proj_w_in"), sem("o_loaded"), [sem(f"x4_loaded{b}") for b in range(2)]
        o_hi, o_lo, oT_made, oT_evacuated, proj_full, xb_made, x1_made = [sem(s) for s in (
            "o_hi", "o_lo", "oT_made", "oT_evacuated", "proj_full", "xb_made", "x1_made")]
        var4_made, std4_made, xn4_made, h2_hi, h2_lo, h2T_made, h2T_evacuated = [sem(s) for s in (
            "var4_made", "std4_made", "xn4_made", "h2_hi", "h2_lo", "h2T_made", "h2T_evacuated")]
        support_full, support_hi, support_lo = sem("support_full"), sem("support_hi"), sem("support_lo")
        x1b_made, x1b_stored, dve_proj = sem("x1b_made"), sem("x1b_stored"), sem("dve_proj")
        adj5_in = [sem(f"adj5_in{b}") for b in range(2)]
        x1_loaded = [sem(f"x1_loaded{b}") for b in range(2)]
        adj_rounded, adj_compared, aT_made, aT_evacuated, conv_full, out_made = [sem(s) for s in (
            "adj_rounded", "adj_compared", "aT_made", "aT_evacuated", "conv_full", "out_made")]
        out_stored = [sem(f"out_stored{b}") for b in range(2)]
        misses_summed, misses_shared, flag_made = sem("misses_summed"), sem("misses_shared"), sem("flag_made")
        sup32_made, adj6_in, rest_made, restT_made, restT_evacuated, rest_full = [sem(s) for s in (
            "sup32_made", "adj6_in", "rest_made", "restT_made", "restT_evacuated", "rest_full")]
        fix_loaded, fix_made, fix_stored, rounded6 = sem("fix_loaded"), sem("fix_made"), sem("fix_stored"), sem("rounded6")

        block = ctx.enter_context(nc.Block())

        def rows(t, n=1):
            return bass.ds(t * P, n * P)

        def group_rows(t, g):
            return t[bass.ds(g * (GT * P), GT * P), :].rearrange("(s p) d -> p s d", p=P)

        def idx(tile):
            return 2 * tile[0] + tile[1]

        def value_home(g):
            return 1 + (g - 1) % 3 if g else 0

        def key_bank(t):
            return bank(t % GT + (GT if t >= GT else 0))

        VALUES_AFTER = {(0, n): n for n in range(NG - 1)}
        VALUES_AFTER[1, 0] = NG - 1
        POOL_VALUES = (2, 4)

        def wait_values_lower(eng, n):
            by_pool = sum(g < n for g in POOL_VALUES)
            eng.wait_ge(value_lo, n - by_pool)
            wait_from(eng, value_lo_pool, by_pool)

        def attention_steps(eng, step):
            step((0, 0), None)
            step((0, 1), (0, 0))
            step((1, 0), (0, 1))
            with eng.Fori(1, NT // 2 - 1) as j:
                step((j, 1), (j, 0))
                step((j + 1, 0), (j, 1))
            last = NT // 2 - 1
            step((last, 1), (last, 0))
            step(None, (last, 1))

        def group_steps(step):
            step((0, 0), None, None)
            step((0, 1), (0, 0), None)
            step((1, 0), (0, 1), (0, 0))

            def pair(j):
                step((j, 1), (j, 0), (j - 1, 1))
                step((j + 1, 0), (j, 1), (j, 0))
            return pair

        def group_end(step):
            last = NG // 2 - 1
            step((last, 1), (last, 0), (last - 1, 1))
            step(None, (last, 1), (last, 0))
            step(None, None, (last, 1))

        def projection_steps(eng, step):
            def group(k):
                return (k // 2, k % 2) if 0 <= k < NG else None

            def plain(k):
                step(group(k + 1), group(k), group(k - 1), group(k - 2))
            for k in range(-1, 3):
                plain(k)
            with eng.Fori(1, NG // 2 - 1) as j:
                step((j + 1, 0), (j, 1), (j, 0), (j - 1, 1))
                step((j + 1, 1), (j + 1, 0), (j, 1), (j, 0))
            for k in range(NG - 1, NG + 1):
                plain(k)

        @block.sync
        def _(sp):
            for a in range(DB):
                sp.dma_start(wq_s[:, a, :], wq[a * P:(a + 1) * P, :]).then_inc(wqk_in[a], 16)
                sp.dma_start(wk_s[:, a, :], wk[a * P:(a + 1) * P, :]).then_inc(wqk_in[a], 16)
            with nc.allow_non_contiguous_dma(reason="three vectors of 512, once"):
                for n, v in enumerate((bq, bk, bv)):
                    sp.dma_start(bcol[:, n, :], v.rearrange("(a p) -> p a", p=P)).then_inc(bias_in, 16)
            sp.dma_start(xg[0], group_rows(x, 0)).then_inc(x_loaded[0], 16)
            sp.dma_start(wm_s, wm.rearrange("(a p) d -> p a d", p=P)).then_inc(wvm_in, 16)
            sp.dma_start(wv_s, wv.rearrange("(a p) d -> p a d", p=P)).then_inc(wvm_in, 16)
            sp.dma_start(bm_b, bm.rearrange("(a d) -> a d", a=1).to_broadcast([P, D])).then_inc(wvm_in, 16)

            def group_loads(k, b):
                if not isinstance(k, int) or k >= 2:
                    sp.wait_ge(hT_made, GT * (k - 1))
                    sp.wait_ge(r_made, k - 1)
                if not isinstance(k, int) or k:
                    sp.dma_start(xg[b], group_rows(x, k)).then_inc(x_loaded[b], 16)
                if not isinstance(k, int) or k >= 2:
                    sp.wait_ge(key_scanned, k - 1)
                sp.dma_start(key32[:, bass.ds(k * GT, GT), :], group_rows(key, k)).then_inc(key_loaded[b], 16)
                wait_from(sp, value_scanned, k)
                sp.dma_start(value_scan, group_rows(value, k)).then_inc(vscan_in, 16)

            def store_queries(k):
                sp.wait_ge(q_hi, DB * (k + 1))
                sp.wait_ge(q_lo, DB * (k + 1))
                sp.dma_start(q_scr[bass.ds(k * GT, GT)].rearrange("s p m -> p s m"),
                             qst.rearrange("p s h a n -> p s (h a n)")).then_inc(q_stored, 16)
            group_loads(0, 0)
            group_loads(1, 1)
            sp.wait_ge(weight_product, 2 * DB + 2)
            sp.dma_start(w1_s, w1.rearrange("(a p) d -> p a d", p=P)).then_inc(w1_in, 16)
            group_loads(2, 0)
            with sp.Fori(1, NG // 2 - 1) as j:
                group_loads(2 * j + 1, 1)
                store_queries(2 * j - 2)
                group_loads(2 * j + 2, 0)
                store_queries(2 * j - 1)
            group_loads(NG - 1, 1)
            store_queries(NG - 4)
            store_queries(NG - 3)

            def load_values(g):
                sp.dma_start(value_homes[value_home(g)], group_rows(value, g)).then_inc(value_loaded[value_home(g)], 16)
            sp.wait_ge(value_scanned, NG)
            load_values(0)
            sp.wait_ge(hT_made, NG * GT)
            sp.wait_ge(r_made, NG)
            sp.dma_start(tt[0], adj[rows(0), :]).then_inc(adj_in[0], 16)
            store_queries(NG - 2)
            for n, (home, staged, stored) in enumerate(((w2_scr, w2hl, w2_stored), (w1_scr, w1hl, w1_stored))):
                sp.wait_ge(weight_hi, n + 2)
                sp.wait_ge(weight_lo, n + 2)
                sp.dma_start(home, staged.rearrange("p a h d -> p (a h d)")).then_inc(stored, 16)
            sp.wait_ge(w2_stored, 16)
            sp.wait_ge(q_stored, 16 * (NG - 1))
            sp.dma_start(qT[0], q_scr[0].rearrange("p (h a n) -> p h a n", h=2, a=DB)).then_inc(q_in[0], 16)
            sp.wait_ge(w1_stored, 16)
            load_values(1)
            store_queries(NG - 1)
            sp.wait_ge(q_stored, 16 * NG)
            for g in range(2, NG):
                if g >= 4:
                    sp.wait_ge(value_hi, g - 2)
                    wait_values_lower(sp, g - 2)
                load_values(g)
                if g == 3:
                    sp.wait_ge(q_product, NG * DB)
                    sp.dma_start(tt[1], adj[rows(1), :]).then_inc(adj_in[1], 16)
                    sp.dma_start(qT[1], q_scr[1].rearrange("p (h a n) -> p h a n", h=2, a=DB)).then_inc(q_in[1], 16)

            def store_context(t):
                sp.wait_ge(context_made, t + 1)
                sp.dma_start(o_scr[rows(t), :], o32).then_inc(context_stored, 16)

            def attention_loads(j, b):
                t = 2 * j + b
                sp.wait_ge(exp_made, HC * (t - 1))
                sp.dma_start(tt[b], adj[rows(t), :]).then_inc(adj_in[b], 16)
                sp.wait_ge(scores_full, CH * (t - 1))
                sp.dma_start(qT[b], q_scr[bass.ds(t, 1)].rearrange("o p (h a n) -> p (o h) a n", h=2, a=DB)).then_inc(q_in[b], 16)
            attention_loads(1, 0)
            with sp.Fori(1, NT // 2 - 1) as j:
                attention_loads(j, 1)
                store_context(2 * j - 2)
                attention_loads(j + 1, 0)
                store_context(2 * j - 1)
            attention_loads(NT // 2 - 1, 1)
            store_context(NT - 4)
            store_context(NT - 3)

            def load_context(g):
                wait_from(sp, o_hi, g)
                wait_from(sp, o_lo, g)
                sp.dma_start(o_in, group_rows(o_scr, g)).then_inc(o_loaded, 16)
            sp.wait_ge(exp_made, HC * (NT - 1))
            sp.wait_ge(context_stored, 16 * (NT - 2))
            load_context(0)
            sp.dma_start(xs[0], group_rows(x, 0)).then_inc(x4_loaded[0], 16)
            sp.wait_ge(exp_made, HC * NT)
            sp.wait_ge(w2_stored, 16)
            sp.wait_ge(w1_stored, 16)
            sp.dma_start(w2p.rearrange("p a h d -> p (a h d)"), w2_scr).then_inc(proj_w_in, 16)
            sp.dma_start(w1p.rearrange("p a h d -> p (a h d)"), w1_scr).then_inc(proj_w_in, 16)
            sp.dma_start(b1_b, b1.rearrange("(a d) -> a d", a=1).to_broadcast([P, D])).then_inc(proj_w_in, 16)
            store_context(NT - 2)
            load_context(1)
            sp.wait_ge(context_full, NT)
            sp.dma_start(xs[1], group_rows(x, 1)).then_inc(x4_loaded[1], 16)
            store_context(NT - 1)
            sp.wait_ge(context_stored, 16 * NT)
            load_context(2)

            def load_x(g, b):
                sp.wait_ge(h2_hi, g - 1)
                sp.wait_ge(h2_lo, g - 1)
                sp.dma_start(xs[b], group_rows(x, g)).then_inc(x4_loaded[b], 16)

            def store_x1(g):
                sp.wait_ge(x1b_made, GT * g + GT)
                sp.dma_start(group_rows(x1_scr, g), x1b).then_inc(x1b_stored, 16)
            store_x1(0)
            load_context(3)
            load_x(2, 0)
            store_x1(1)
            with sp.Fori(1, NG // 2 - 1) as j:
                for b in range(2):
                    load_context(2 * j + b + 2)
                    load_x(2 * j + b + 1, 1 - b)
                    store_x1(2 * j + b)
            load_x(NG - 1, 1)
            store_x1(NG - 2)
            sp.wait_ge(o_hi, NG)
            sp.wait_ge(o_lo, NG)
            sp.wait_ge(h2_hi, NG - 1)
            sp.wait_ge(h2_lo, NG - 1)
            sp.dma_start(tt[0], adj[rows(0), :]).then_inc(adj5_in[0], 16)
            store_x1(NG - 1)
            sp.wait_ge(support_full, NT)
            sp.dma_start(tt[1], adj[rows(1), :]).then_inc(adj5_in[1], 16)

            sp.wait_ge(x1b_stored, 16 * NG)
            for b in range(2):
                sp.dma_start(x1_in[b], x1_scr[rows(b), :]).then_inc(x1_loaded[b], 16)

            def store_out(t, b):
                sp.wait_ge(out_made, t + 1)
                sp.dma_start(out[rows(t), :], o_out[b]).then_inc(out_stored[b], 16)
            with sp.Fori(1, NT // 2) as j:
                for b in range(2):
                    t = 2 * j + b
                    sp.wait_ge(adj_rounded, t - 1)
                    sp.wait_ge(adj_compared, t - 1)
                    sp.dma_start(tt[b], adj[rows(t), :]).then_inc(adj5_in[b], 16)
                    store_out(t - 2, b)
                    sp.dma_start(x1_in[b], x1_scr[rows(t), :]).then_inc(x1_loaded[b], 16)
            for b in range(2):
                store_out(NT - 2 + b, b)
            for b in range(2):
                sp.wait_ge(out_stored[b], 16 * NT // 2)

            sp.wait_ge(flag_made, 1)
            with sp.If(sp.value_load(flag[0:1, 0:1], min_val=0, max_val=1) > 0):
                def rest_traffic(t):
                    wait_from(sp, fix_stored, 16 * t)
                    sp.dma_start(tt[0], adj[rows(t), :]).then_inc(adj6_in, 16)
                    sp.dma_start(fix_in, out[rows(t), :]).then_inc(fix_loaded, 16)
                    sp.wait_ge(fix_made, t + 1)
                    sp.dma_start(out[rows(t), :], fix_out).then_inc(fix_stored, 16)
                rest_traffic(0)
                with sp.Fori(1, NT) as t:
                    rest_traffic(t)
                sp.wait_ge(fix_stored, 16 * NT)

        @block.gpsimd
        def _(pool):
            pool.memset(ident32[:], 0.0).then_inc(ident_zero, 1)
            pool.memset(ident16[:], 0.0).then_inc(ident_zero, 1)
            pool.memset(identb[:], 0.0).then_inc(ident_zero, 1)
            pool.wait_ge(ident_zero, 3)
            for m in (ident32, ident16, identb):
                pool.affine_select(out=m[:], in_=m[:], compare_op=ALU.not_equal, fill=1.0, base=0,
                                   pattern=[[-1, P]], channel_multiplier=1).then_inc(ident_made, 1)
            pool.wait_ge(maxima_made, 1)
            pool.partition_all_reduce(gmx[:, 0:2], mx[:, 0:2], P, RMAX).then_inc(maxima_shared, 1)

            def query_step(a, g, d):
                if d and not a and g:
                    pool.wait_ge(maxima_made, 2)
                    pool.partition_all_reduce(gmx[:, 2:6], mx[:, 2:6], P, RMAX).then_inc(maxima_shared, 1)
                if d:
                    for o in range(DB):
                        pool.wait_ge(q_hi, DB * idx(d) + o + 1)
                        pool.tensor_tensor(qst[:, :, 1, o, :], q32[:, o % 2, :].rearrange("p (s n) -> p s n", s=GT),
                                           qst[:, :, 0, o, :], ALU.subtract).then_inc(q_lo, 1)
            pair = group_steps(query_step)
            with pool.Fori(1, NG // 2 - 1) as j:
                pair(j)
            group_end(query_step)
            for g in POOL_VALUES:
                pool.wait_ge(value_hi, g + 1)
                pool.tensor_tensor(VV[:, g * GT:(g + 1) * GT, 1, :], value_homes[value_home(g)],
                                   VV[:, g * GT:(g + 1) * GT, 0, :], ALU.subtract).then_inc(value_lo_pool, 1)

            pool.wait_ge(proj_w_in, 48)

            def projection_step(a, g, d, e):
                if g:
                    k = idx(g)
                    if isinstance(k, int) and k == 0:
                        pool.wait_ge(context_full, NT)
                    wait_from(pool, x1b_stored, 16 * k)
                    for s in range(GT):
                        pool.wait_ge(x1_made, GT * k + s + 1)
                        pool.tensor_tensor(x1b[:, s, :], xs[g[1]][:, s, :], b1_b, ALU.add).then_inc(x1b_made, 1)
                if a:
                    pool.wait_ge(x4_loaded[a[1]], 16 * a[0] + 16)
                    for s in range(GT):
                        pool.tensor_tensor(xs[a[1]][:, s, :], xs[a[1]][:, s, :], b2_b[:], ALU.add).then_inc(xb_made, 1)
            projection_steps(pool, projection_step)

            pool.wait_ge(misses_summed, 1)
            pool.partition_all_reduce(miss2[:, 1:2], miss2[:, 0:1], P, RADD).then_inc(misses_shared, 1)

        @block.tensor
        def _(pe):
            item = [0]

            def weight_item(emit):
                n = item[0]
                if n >= 8:
                    pe.wait_ge(weight_evacuated, n - 7)
                emit(bank(n % 8)).then_inc(weight_product, 1)
                item[0] += 1

            def product(lhs, rhs):
                def emit(to):
                    for a in range(DB):
                        last = pe.matmul(to[:, 0:rhs(a).shape[1]], lhs(a), rhs(a), start=(a == 0), stop=(a == DB - 1))
                    return last
                return emit

            for a in range(DB):
                pe.wait_ge(wqk_in[a], 32)
                for d in range(DB):
                    last = pe.matmul(bank(d), wq_s[:, a, d * P:(d + 1) * P], wk_s[:, a, :], start=(a == 0), stop=(a == DB - 1))
                    if a == DB - 1:
                        last.then_inc(weight_product, 1)
            item[0] = DB
            pe.wait_ge(bias_in, 48)
            pe.wait_ge(cols_spread, 2)
            weight_item(product(lambda a: bkb[:, a, :], lambda a: wq_s[:, a, :]))

            def columns(to):
                for d in range(DB):
                    for a in range(DB):
                        pe.matmul(to[:, d:d + 1], wk_s[:, a, d * P:(d + 1) * P], bcol[:, 0, a:a + 1],
                                  start=(a == 0), stop=(a == DB - 1))
                for a in range(DB):
                    last = pe.matmul(to[:, DB:DB + 1], bkb[:, a, :], bcol[:, 0, a:a + 1],
                                     start=(a == 0), stop=(a == DB - 1))
                return last
            weight_item(columns)
            pe.wait_ge(wvm_in, 48)
            pe.wait_ge(ident_made, 3)
            for a in range(DB):
                def turned(to, a=a):
                    for e in range(DB):
                        last = pe.transpose(to[:, e * P:(e + 1) * P], wm_s[:, e, a * P:(a + 1) * P], ident32[:])
                    return last
                weight_item(turned)
            pe.wait_ge(weight_evacuated, item[0])
            for d in range(DB):
                weight_item(product(lambda a: wv_s[:, a, d * P:(d + 1) * P], lambda a: wmT[:, a, :]))
            weight_item(product(lambda a: bvb[:, a, :], lambda a: wmT[:, a, :]))

            pe.wait_ge(weight_evacuated, item[0])

            def query_products(d):
                k = idx(d)
                pe.wait_ge(h_hi, GT * (k + 1))
                pe.wait_ge(h_lo, GT * (k + 1))
                if isinstance(k, int) and k == 0:
                    pe.wait_ge(weight_hi, 1)
                    pe.wait_ge(weight_lo, 1)
                for o in range(DB):
                    if not isinstance(k, int) or k:
                        pe.wait_ge(q32_made, DB * k + o - 3)
                    n = 0
                    for lh, rh in ((0, 0), (0, 1), (1, 0)):
                        for a in range(DB):
                            last = pe.matmul(bank(4 + o), mhl[:, a, lh, o * P:(o + 1) * P], hT[d[1]][:, rh, a, :],
                                             start=(n == 0), stop=(n == 3 * DB - 1))
                            n += 1
                    last.then_inc(q_product, 1)

            def turn_x(g):
                k = idx(g)
                if not isinstance(k, int) or k:
                    pe.wait_ge(h_hi, GT * k)
                    pe.wait_ge(h_lo, GT * k)
                for s in range(GT):
                    pe.wait_ge(xn_made, GT * k + s + 1)
                    for a in range(DB):
                        last = pe.transpose(bank(s)[:, a * P:(a + 1) * P], xg[g[1]][:, s, a * P:(a + 1) * P], ident32[:])
                    last.then_inc(hT_made, 1)

            def query_step(a, g, d):
                if g:
                    turn_x(g)
                if d:
                    query_products(d)
            pair = group_steps(query_step)
            with pe.Fori(1, NG // 2 - 1) as j:
                pair(j)
            last_pair = NG // 2 - 1
            query_step((last_pair, 1), (last_pair, 0), (last_pair - 1, 1))
            query_step(None, (last_pair, 1), (last_pair, 0))

            def turn_keys(g):
                for t in range(GT * g, GT * g + GT):
                    if g == 1:
                        pe.wait_ge(q32_made, (NG - 1) * DB + t - GT + 1)
                    if g >= 2:
                        pe.wait_ge(key_hi, t - 3)
                        pe.wait_ge(key_lo, t - 3)
                    for a in range(DB):
                        last = pe.transpose(key_bank(t)[:, a * P:(a + 1) * P], key32[:, t, a * P:(a + 1) * P], ident32[:])
                    last.then_inc(keyT_made, 1)
            pe.wait_ge(key_scanned, NG)
            pe.wait_ge(h_hi, NG * GT)
            pe.wait_ge(h_lo, NG * GT)
            turn_keys(0)
            query_products((last_pair, 1))
            turn_keys(1)

            def p_transposes(t, g):
                pe.wait_ge(p_hi, HC * t + g // 2 + 1)
                pe.wait_ge(p_lo, HC * t + g // 2 + 1)
                if g >= 2 or not isinstance(t, int) or t:
                    pe.wait_ge(pT_evacuated, TG * t + g)
                to = bank16(4 + g % 2)
                for m in range(4):
                    for h in range(2):
                        last = pe.transpose(to[:, 2 * m + h, :], phl[:, h, (4 * g + m) * P:(4 * g + m + 1) * P], ident16[:])
                last.then_inc(pT_made, 1)

            def context_products(t, g):
                pe.wait_ge(pT_evacuated, TG * t + g + 1)
                for m in range(4):
                    for i, (lh, rh) in enumerate(((0, 0), (0, 1), (1, 0))):
                        last = pe.matmul(bank(6), pT[:, g % 2, m, lh, :], VV[:, 4 * g + m, rh, :],
                                         start=(g == 0 and m == 0 and i == 0), stop=(g == TG - 1 and m == 3 and i == 2))
                return last

            def attention_step(s, c):
                if s:
                    t = idx(s)
                    pe.wait_ge(q_in[s[1]], 16 * s[0] + 16)
                    for n in range(CH):
                        if not c:
                            if n + 2 < NG:
                                turn_keys(n + 2)
                            pe.wait_ge(key_hi, GT * (n + 1))
                            pe.wait_ge(key_lo, GT * (n + 1))
                        if c and n == CH - 1:
                            p_transposes(idx(c), 0)
                        if n >= 4 or c:
                            pe.wait_ge(scores_scaled, CH * t + n - 3)
                        i = 0
                        for lh, rh in ((0, 0), (0, 1), (1, 0)):
                            for a in range(DB):
                                last = pe.matmul(bank(n % 4), qT[s[1]][:, lh, a, :], KT[:, rh, a, n * D:(n + 1) * D],
                                                 start=(i == 0), stop=(i == 3 * DB - 1))
                                i += 1
                        last.then_inc(scores_full, 1)
                elif c:
                    p_transposes(idx(c), 0)
                if c:
                    t = idx(c)
                    wait_from(pe, context_made, t)
                    if isinstance(t, int) and t == 0:
                        pe.wait_ge(value_hi, NG)
                        wait_values_lower(pe, NG)
                    for g in range(TG):
                        if g + 1 < TG:
                            p_transposes(t, g + 1)
                        last = context_products(t, g)
                    last.then_inc(context_full, 1)
            attention_steps(pe, attention_step)

            pe.wait_ge(proj_w_in, 48)

            def turn(first, src, g, s, evacuated, made):
                if s >= 2 or not isinstance(g, int) or g:
                    pe.wait_ge(evacuated, GT * g + s - 1)
                to = bank16(first + s % 2)
                for h in range(2):
                    for a in range(DB):
                        last = pe.transpose(to[:, h * DB + a, :], src[:, h, s, a * P:(a + 1) * P], ident16[:])
                last.then_inc(made, 1)

            def group_product(first, left, w, g, s, taken, full):
                if s >= 2 or not isinstance(g, int) or g:
                    for t in taken:
                        pe.wait_ge(t, GT * g + s - 1)
                n = 0
                for lh, rh in ((0, 0), (0, 1), (1, 0)):
                    for a in range(DB):
                        last = pe.matmul(bank(first + s % 2), left[:, s, lh, a, :], w[:, a, rh, :],
                                         start=(n == 0), stop=(n == 3 * DB - 1))
                        n += 1
                last.then_inc(full, 1)

            def projection_step(a, g, d, e):
                def turn_o(s):
                    if a and s == 0:
                        pe.wait_ge(o_hi, idx(a) + 1)
                        pe.wait_ge(o_lo, idx(a) + 1)
                    if a:
                        turn(0, ohl, idx(a), s, oT_evacuated, oT_made)

                def turn_h2(s):
                    if d and s == 0:
                        pe.wait_ge(h2_hi, idx(d) + 1)
                        pe.wait_ge(h2_lo, idx(d) + 1)
                    if d:
                        turn(2, h2hl, idx(d), s, h2T_evacuated, h2T_made)

                def project(s):
                    if g and s == 0:
                        pe.wait_ge(oT_evacuated, GT * idx(g) + GT)
                    if g:
                        group_product(4, oT, w2p, idx(g), s, (x1_made,), proj_full)

                def support(s):
                    if e and s == 0:
                        pe.wait_ge(h2T_evacuated, GT * idx(e) + GT)
                    if e:
                        group_product(6, h2T, w1p, idx(e), s, (support_hi, support_lo), support_full)
                project(0)
                project(1)
                turn_o(0)
                project(2)
                turn_o(1)
                project(3)
                turn_o(2)
                support(0)
                turn_o(3)
                support(1)
                turn_h2(0)
                support(2)
                turn_h2(1)
                support(3)
                turn_h2(2)
                turn_h2(3)
            projection_steps(pe, projection_step)

            pe.wait_ge(x1_made, NT)

            def adj_transposes(t, b, g):
                if g == 0:
                    pe.wait_ge(adj_rounded, t + 1)
                if g >= 2 or not isinstance(t, int) or t:
                    pe.wait_ge(aT_evacuated, 4 * t + g - 1)
                for m in range(8):
                    last = pe.transpose(bank16(4 + g % 2, BF16)[:, m, :],
                                        a_bf[:, b, (8 * g + m) * P:(8 * g + m + 1) * P], identb[:])
                last.then_inc(aT_made, 1)

            def conv_products(t, b, g):
                pe.wait_ge(aT_evacuated, 4 * t + g + 1)
                for m in range(8):
                    for h in range(2):
                        last = pe.matmul(bank(6 + b), aT[:, g % 2, m, :], SUP[:, 8 * g + m, h, :],
                                         start=(g == 0 and m == 0 and h == 0), stop=(g == 3 and m == 7 and h == 1))
                return last

            def conv_tile(t, b, last_tile=False):
                if not isinstance(t, int) or t > 1:
                    pe.wait_ge(out_made, t - 1)
                for g in range(4):
                    if g + 1 < 4:
                        adj_transposes(t, b, g + 1)
                    elif not last_tile:
                        adj_transposes(t + 1, 1 - b, 0)
                    last = conv_products(t, b, g)
                last.then_inc(conv_full, 1)

            def conv_pair(j):
                for b in range(2):
                    conv_tile(2 * j + b, b)

            adj_transposes(0, 0, 0)
            projection_step(None, None, None, (NG // 2 - 1, 1))
            pe.wait_ge(support_hi, NT)
            pe.wait_ge(support_lo, NT)
            conv_pair(0)
            with pe.Fori(1, NT // 2 - 1) as j:
                conv_pair(j)
            conv_tile(NT - 2, 0)
            conv_tile(NT - 1, 1, last_tile=True)

            pe.wait_ge(flag_made, 1)
            with pe.If(pe.value_load(flag[0:1, 0:1], min_val=0, max_val=1) > 0):
                pe.wait_ge(sup32_made, 1)
                pe.wait_ge(out_made, NT)

                def rest_tile(t):
                    pe.wait_ge(rest_made, t + 1)
                    wait_from(pe, fix_made, t)
                    for q in range(8):
                        wait_from(pe, restT_evacuated, 8 * t + q)
                        for m in range(4):
                            last = pe.transpose(bank(4)[:, m * P:(m + 1) * P], tt[1][:, (4 * q + m) * P:(4 * q + m + 1) * P], ident32[:])
                        last.then_inc(restT_made, 1)
                        pe.wait_ge(restT_evacuated, 8 * t + q + 1)
                        for m in range(4):
                            last = pe.matmul(bank(6), restT[:, m * P:(m + 1) * P], sup32[:, 4 * q + m, :],
                                             start=(q == 0 and m == 0), stop=(q == 7 and m == 3))
                    last.then_inc(rest_full, 1)
                rest_tile(0)
                with pe.Fori(1, NT) as t:
                    rest_tile(t)

        @block.scalar
        def _(act):
            homes = [m32[:, d, :] for d in range(DB)] + [u_b, cs[:]] + [wmT[:, a, :] for a in range(DB)] \
                + [w232[:, d, :] for d in range(DB)] + [b2_b[:]]

            def root(a):
                act.wait_ge(var_made, idx(a) + 1)
                act.activation(rs[:], mv[:, :, 1], ACT.Sqrt).then_inc(std_made, 1)

            def normalise(a):
                act.wait_ge(rs_made, idx(a) + 1)
                for s in range(GT):
                    act.activation(xg[a[1]][:, s, :], xg[a[1]][:, s, :], ACT.Identity, bias=mean_rs[:, s:s + 1],
                                   scale=rs[:, s:s + 1]).then_inc(xn_made, 1)
            early = {1: (0, 0), 3 * DB: (0, 1)}
            for n, home in enumerate(homes):
                if n in early:
                    root(early[n])
                    normalise(early[n])
                act.wait_ge(weight_product, n + 1)
                act.copy(home, bank(n % 8)[:, 0:home.shape[1]]).then_inc(weight_evacuated, 1)
                if n == 2 * DB + 1:
                    act.wait_ge(scales_made, 1)
                    act.wait_ge(weight_evacuated, n + 1)
                    act.activation(mhl[:, :, 0, :], m32, ACT.Copy, scale=col(G_M)).then_inc(weight_hi, 1)

            def upper_h(g):
                for s in range(GT):
                    act.wait_ge(hT_made, GT * idx(g) + s + 1)
                    act.activation(hT[g[1]][:, 0, :, s * P:(s + 1) * P], bank(s).rearrange("p (a n) -> p a n", a=DB),
                                   ACT.Relu).then_inc(h_hi, 1)

            def query(d, o):
                k = idx(d)
                act.wait_ge(q_product, DB * k + o + 1)
                if o >= 2 or not isinstance(k, int) or k:
                    act.wait_ge(q_hi, DB * k + o - 1)
                    act.wait_ge(q_lo, DB * k + o - 1)
                act.activation(q32[:, o % 2, :], bank(4 + o), ACT.Identity, bias=cq[:, o:o + 1],
                               scale=col(S_Q)).then_inc(q32_made, 1)
                act.wait_ge(q32_made, DB * k + o + 1)
                if o == 0:
                    wait_from(act, q_stored, 16 * k)
                act.copy(qst[:, :, 0, o, :], q32[:, o % 2, :].rearrange("p (s n) -> p s n", s=GT)).then_inc(q_hi, 1)

            def ahead_in_loop(a):
                return not isinstance(a[0], int) or a[0] > 0

            def query_step(a, g, d):
                if g:
                    upper_h(g)
                if d:
                    query(d, 0)
                if a and ahead_in_loop(a):
                    root(a)
                if d:
                    query(d, 1)
                if a and ahead_in_loop(a):
                    normalise(a)
                if d:
                    query(d, 2)
                    query(d, 3)
            pair = group_steps(query_step)
            with act.Fori(1, NG // 2 - 1) as j:
                pair(j)
            last_pair = NG // 2 - 1
            query_step((last_pair, 1), (last_pair, 0), (last_pair - 1, 1))
            query_step(None, (last_pair, 1), (last_pair, 0))

            act.wait_ge(scales_made, 2)
            for w, g, staged in ((w232, G_W2, w2hl), (w1_s, G_W1, w1hl)):
                act.activation(staged[:, :, 0, :], w, ACT.Copy, scale=col(g)).then_inc(weight_hi, 1)

            def upper_keys(g):
                for t in range(GT * g, GT * g + GT):
                    act.wait_ge(keyT_made, t + 1)
                    act.activation(KT[:, 0, :, t * P:(t + 1) * P], key_bank(t).rearrange("p (a n) -> p a n", a=DB),
                                   ACT.Copy, scale=col(G_K)).then_inc(key_hi, 1)

            def upper_values(g):
                home = value_home(g)
                act.wait_ge(value_loaded[home], 16 * ((g - 1) // 3 if g else 0) + 16)
                if g in POOL_VALUES:
                    act.activation(value_homes[home], value_homes[home], ACT.Copy, scale=col(G_V)).then_inc(value_scaled, 1)
                    act.wait_ge(value_scaled, POOL_VALUES.index(g) + 1)
                    act.copy(VV[:, g * GT:(g + 1) * GT, 0, :], value_homes[home]).then_inc(value_hi, 1)
                else:
                    act.activation(VV[:, g * GT:(g + 1) * GT, 0, :], value_homes[home], ACT.Copy, scale=col(G_V)).then_inc(value_hi, 1)
            query((last_pair, 1), 0)
            query((last_pair, 1), 1)
            act.wait_ge(weight_hi, 3)
            act.wait_ge(weight_lo, 3)
            act.wait_ge(q_product, DB * (NG - 1))
            upper_keys(0)
            query((last_pair, 1), 2)
            query((last_pair, 1), 3)
            upper_keys(1)


            def take_pT(t, g):
                act.wait_ge(pT_made, TG * t + g + 1)
                act.copy(pT[:, g % 2], bank16(4 + g % 2).rearrange("p (t h) n -> p t h n", h=2)).then_inc(pT_evacuated, 1)

            def upper_context(a):
                act.wait_ge(o_loaded, 16 * idx(a) + 16)
                wait_from(act, oT_made, GT * idx(a))
                act.copy(ohl[:, 0], o_in).then_inc(o_hi, 1)

            def attention_step(s, c):
                def magnitudes(n):
                    t = idx(s)
                    act.wait_ge(scores_scaled, CH * t + 2 * n + 2)
                    if n >= 2:
                        act.wait_ge(scores_masked, HC * t + n - 1)
                    elif c:
                        act.wait_ge(p_lo, HC * t)
                    else:
                        wait_values_lower(act, 1)
                    act.activation(p32[:, n % 2, :], tt[s[1]][:, n * SC:(n + 1) * SC], ACT.Abs).then_inc(abs_made, 1)

                def exponentials(n):
                    t = idx(s)
                    if n == 0:
                        act.wait_ge(shift_made, t + 1)
                    if n >= 2:
                        act.wait_ge(p_lo, HC * t + n - 1)
                    act.activation(p32[:, n % 2, :], tt[s[1]][:, n * SC:(n + 1) * SC], ACT.Exp,
                                   bias=nbias[:, 2:3], scale=col(I_G), accum_out=rsum[:, n:n + 1]).then_inc(exp_made, 1)

                def upper_parts(n):
                    t = idx(s)
                    act.wait_ge(exp_made, HC * t + n + 1)
                    if not c:
                        wait_values_lower(act, NG - 1)
                    if c:
                        act.wait_ge(pT_made, TG * idx(c) + 2 * n + 2)
                    act.copy(phl[:, 0, n * SC:(n + 1) * SC], p32[:, n % 2, :]).then_inc(p_hi, 1)

                second = s and isinstance(s[0], int) and idx(s) == 1
                if s and not c:
                    for n in range(CH):
                        if n + 2 < NG:
                            upper_keys(n + 2)
                        if (0, n) in VALUES_AFTER:
                            upper_values(VALUES_AFTER[0, n])
                        if n % 2 and n < CH - 1:
                            magnitudes(n // 2)
                elif second:
                    wait_values_lower(act, NG)
                    take_pT(0, 0)
                    for g in range(1, TG):
                        take_pT(0, g)
                        if g > TG - 1 - HC:
                            magnitudes(g - (TG - HC))
                    for n in range(HC):
                        exponentials(n)
                        upper_parts(n)
                    return
                elif s:
                    for n in range(HC - 1):
                        magnitudes(n)
                if c:
                    take_pT(idx(c), 0)
                    take_pT(idx(c), 1)
                if s:
                    magnitudes(HC - 1)
                if s and not c:
                    upper_values(VALUES_AFTER[1, 0])
                if not s:
                    act.wait_ge(p_lo, HC * NT)
                    upper_context((0, 0))
                for g in range(2, TG):
                    if c:
                        take_pT(idx(c), g)
                    if s and g % 2 == 0:
                        exponentials(g // 2 - 1)
                    if s and g % 2:
                        upper_parts(g // 2 - 1)
                if s:
                    exponentials(HC - 1)
                    upper_parts(HC - 1)
            attention_steps(act, attention_step)

            def take_turned(to, g, s, bank0, made, evacuated):
                act.wait_ge(made, GT * g + s + 1)
                act.copy(to[:, s], bank16(bank0 + s % 2).rearrange("p (h a) n -> p h a n", h=2)).then_inc(evacuated, 1)

            def support_upper(e, s):
                t = GT * idx(e) + s
                act.wait_ge(support_full, t + 1)
                act.activation(SUP[:, bass.ds(t, 1), 0, :].rearrange("p t d -> p (t d)"), bank(6 + s % 2), ACT.Copy,
                               scale=SUPPORT_SCALE).then_inc(support_hi, 1)

            def projection_step(a, g, d, e):
                def take_o(s):
                    if a:
                        take_turned(oT, idx(a), s, 0, oT_made, oT_evacuated)

                def take_h2(s):
                    if d:
                        take_turned(h2T, idx(d), s, 2, h2T_made, h2T_evacuated)
                if a and g:
                    upper_context(a)
                if d:
                    act.wait_ge(xn4_made, GT * idx(d) + GT)
                    wait_from(act, h2T_made, GT * idx(d))
                    act.activation(h2hl[:, 0], xs[d[1]], ACT.Relu).then_inc(h2_hi, 1)
                for s in range(3):
                    take_o(s)
                if g:
                    act.wait_ge(var4_made, idx(g) + 1)
                    act.activation(rs[:], mv[:, :, 1], ACT.Sqrt).then_inc(std4_made, 1)
                if e:
                    support_upper(e, 0)
                take_o(3)
                for s in range(3):
                    if e:
                        support_upper(e, s + 1)
                    take_h2(s)
                take_h2(3)
            projection_steps(act, projection_step)

            def take_aT(t, g):
                act.wait_ge(aT_made, 4 * t + g + 1)
                act.copy(aT[:, g % 2], bank16(4 + g % 2, BF16)).then_inc(aT_evacuated, 1)
            take_aT(0, 0)
            projection_step(None, None, None, (NG // 2 - 1, 1))
            for g in range(1, 4):
                take_aT(0, g)
            with act.Fori(1, NT) as t:
                for g in range(4):
                    take_aT(t, g)

            act.wait_ge(flag_made, 1)
            with act.If(act.value_load(flag[0:1, 0:1], min_val=0, max_val=1) > 0):
                with act.Fori(0, NT) as t:
                    for q in range(8):
                        act.wait_ge(restT_made, 8 * t + q + 1)
                        act.copy(restT, bank(4)).then_inc(restT_evacuated, 1)

        @block.vector
        def _(dve):
            own = Chain(dve, dve_own)
            own.mark(dve.memset(ones[:], 1.0))
            own.settle()
            dve.wait_ge(bias_in, 48)
            for n, spread in ((1, bkb), (2, bvb)):
                for a in range(DB):
                    last = dve.tensor_scalar(spread[:, a, :], ones[:], bcol[:, n, a:a + 1], None, ALU.mult)
                last.then_inc(cols_spread, 1)

            def powers_below(first, last, scales):
                own.mark(dve.tensor_scalar(gmx[:, first:last], gmx[:, first:last], 2.0 ** -20, None, ALU.max))
                own.settle()
                own.mark(dve.tensor_scalar(fl[:, first:last].bitcast(I32), gmx[:, first:last].bitcast(I32),
                                           EXPONENT_BITS, None, ALU.bitwise_and))
                own.settle()
                own.mark(dve.reciprocal(gmx[:, first:last], fl[:, first:last]))
                own.settle()
                own.mark(dve.tensor_scalar(sc[:, scales:scales + last - first], gmx[:, first:last], TOP, None, ALU.mult))
                own.settle()

            PER2 = 5

            def layernorm(a, base):
                X = xg[a[1]]
                own.rebase(base + PER2 * idx(a))
                dve.wait_ge(x_loaded[a[1]], 16 * a[0] + 16)
                for s in range(GT):
                    last = dve.bn_stats(stats[:, s, :], X[:, s, :])
                own.mark(last)
                own.settle()
                own.mark(dve.memset(nbias[:, 0:1], 0.0))
                for s in range(GT):
                    last = dve.bn_aggr(mv[:, s, :], stats[:, s, :])
                own.mark(last)
                own.settle()
                dve.tensor_scalar(mv[:, :, 1], mv[:, :, 1], EPS, None, ALU.add).then_inc(var_made, 1)

            def norm_scales(a):
                dve.wait_ge(std_made, idx(a) + 1)
                own.mark(dve.reciprocal(rs[:], rs[:]))
                own.settle()
                own.mark(dve.tensor_scalar(rs[:], rs[:], H_SCALE, None, ALU.mult))
                own.settle()
                dve.scalar_tensor_tensor(mean_rs[:], mv[:, :, 0], -1.0, rs[:], ALU.mult, ALU.mult).then_inc(rs_made, 1)

            def scans(a):
                k = idx(a)
                dve.wait_ge(key_loaded[a[1]], 16 * a[0] + 16)
                dve.tensor_reduce(kmx[:, 0, bass.ds(k, 1)], key32[:, bass.ds(k * GT, GT), :], AX_XY, ALU.max,
                                  apply_absolute_value=True).then_inc(key_scanned, 1)
                dve.wait_ge(vscan_in, 16 * k + 16)
                dve.tensor_reduce(kmx[:, 1, bass.ds(k, 1)], value_scan, AX_XY, ALU.max,
                                  apply_absolute_value=True).then_inc(value_scanned, 1)

            def row_terms(g):
                k = idx(g)
                dve.wait_ge(xn_made, GT * k + GT)
                for s in range(GT):
                    last = dve.scalar_tensor_tensor(junk[:, s, :], xg[g[1]][:, s, :], 0.0, u_b, ALU.max, ALU.mult,
                                                    accum_out=r_s[:, bass.ds(k * GT + s, 1)])
                last.then_inc(r_made, 1)

            def lower_h(g):
                for s in range(GT):
                    dve.wait_ge(h_hi, GT * idx(g) + s + 1)
                    dve.scalar_tensor_tensor(hT[g[1]][:, 1, :, s * P:(s + 1) * P], bank(s).rearrange("p (a n) -> p a n", a=DB), 0.0,
                                             hT[g[1]][:, 0, :, s * P:(s + 1) * P], ALU.max, ALU.subtract).then_inc(h_lo, 1)

            layernorm((0, 0), own.base + own.k)
            norm_scales((0, 0))
            scans((0, 0))

            dve.wait_ge(weight_evacuated, DB + 2)
            own.mark(dve.tensor_reduce(mx[:, 0:1], m32, AX_XY, ALU.max, apply_absolute_value=True))
            dve.tensor_reduce(mx[:, 1:2], cs[:, 0:DB], AX_X, ALU.max, apply_absolute_value=True).then_inc(maxima_made, 1)
            dve.wait_ge(maxima_shared, 1)
            own.mark(dve.tensor_scalar(sc[:, R0:R0 + 1], gmx[:, 0:1], float(D), gmx[:, 1:2], ALU.mult, ALU.add))
            own.settle()
            own.mark(dve.tensor_copy(gmx[:, 1:2], sc[:, R0:R0 + 1]))
            own.settle()
            powers_below(0, 2, G_M)
            own.mark(dve.tensor_scalar(col(S_Q), fl[:, 0:1], 1.0 / (H_SCALE * TOP), col(G_Q), ALU.mult, ALU.mult))
            own.mark(dve.tensor_scalar(cq[:], cs[:, 0:DB], col(G_Q), None, ALU.mult))
            own.settle()
            dve.tensor_copy(fl[:, 6:7], fl[:, 0:1]).then_inc(scales_made, 1)
            dve.wait_ge(weight_hi, 1)
            for a in range(DB):
                last = dve.scalar_tensor_tensor(mhl[:, a, 1, :], m32[:, a, :], col(G_M), mhl[:, a, 0, :], ALU.mult, ALU.subtract)
            last.then_inc(weight_lo, 1)
            dve.wait_ge(weight_lo, 1)

            BASE2 = own.base + own.k - PER2
            dve.wait_ge(weight_evacuated, DB + 1)

            def query_step(a, g, d):
                if g:
                    row_terms(g)
                if a:
                    layernorm(a, BASE2)
                if g:
                    lower_h(g)
                if a:
                    norm_scales(a)
                    scans(a)
            row_terms((0, 0))
            layernorm((0, 1), BASE2)
            norm_scales((0, 1))
            lower_h((0, 0))
            scans((0, 1))
            query_step((1, 0), (0, 1), (0, 0))
            with dve.Fori(1, NG // 2 - 1) as j:
                query_step((j, 1), (j, 0), (j - 1, 1))
                query_step((j + 1, 0), (j, 1), (j, 0))
            last_pair = NG // 2 - 1
            query_step((last_pair, 1), (last_pair, 0), (last_pair - 1, 1))
            own.rebase(BASE2 + PER2 * NG)
            row_terms((last_pair, 1))

            dve.wait_ge(key_scanned, NG)
            dve.wait_ge(value_scanned, NG)
            dve.wait_ge(weight_evacuated, 15)
            dve.wait_ge(w1_in, 16)
            dve.wait_ge(wvm_in, 48)
            own.mark(dve.tensor_tensor(b2_b[:], b2_b[:], bm_b, ALU.add))
            for n, w in ((4, w232), (5, w1_s)):
                own.mark(dve.tensor_reduce(mx[:, n:n + 1], w, AX_XY, ALU.max, apply_absolute_value=True))
            dve.tensor_reduce(mx[:, 2:4], kmx[:], AX_X, ALU.max).then_inc(maxima_made, 1)
            lower_h((last_pair, 1))
            dve.wait_ge(maxima_shared, 2)
            powers_below(2, 6, G_K)
            own.mark(dve.tensor_scalar(col(G_QK), col(G_Q), col(G_K), None, ALU.mult))
            own.settle()
            own.mark(dve.tensor_scalar(col(S_R), col(G_QK), 1.0 / H_SCALE, None, ALU.mult))
            own.mark(dve.tensor_scalar(col(R0), cs[:, DB:DB + 1], col(G_QK), None, ALU.mult))
            own.mark(dve.tensor_scalar(col(G_ALL), col(G_QK), SCORE_DIV, None, ALU.mult))
            own.settle()
            own.mark(dve.reciprocal(col(I_G), col(G_ALL)))
            own.mark(dve.tensor_scalar(col(THR), col(G_ALL), NEAR_ZERO, None, ALU.mult))
            own.mark(dve.tensor_scalar(col(BIG), col(G_ALL), MASKED, None, ALU.mult))
            own.mark(dve.tensor_scalar(col(I_O), fl[:, 3:4], TOP ** -2, fl[:, 4:5], ALU.mult, ALU.mult))
            own.mark(dve.tensor_scalar(col(I_S), fl[:, 5:6], D / TOP, None, ALU.mult))
            own.settle()
            dve.wait_ge(r_made, NG)
            dve.tensor_scalar(r_s[:], r_s[:], col(S_R), col(R0), ALU.mult, ALU.add).then_inc(scales_made, 1)

            dve.wait_ge(scales_made, 2)
            for n, (w, g, staged) in enumerate(((w232, G_W2, w2hl), (w1_s, G_W1, w1hl))):
                dve.wait_ge(weight_hi, n + 2)
                dve.scalar_tensor_tensor(staged[:, :, 1, :], w, col(g), staged[:, :, 0, :], ALU.mult, ALU.subtract).then_inc(weight_lo, 1)

            def lower_keys(g):
                for t in range(GT * g, GT * g + GT):
                    dve.wait_ge(key_hi, t + 1)
                    dve.scalar_tensor_tensor(KT[:, 1, :, t * P:(t + 1) * P], key_bank(t).rearrange("p (a n) -> p a n", a=DB),
                                             col(G_K), KT[:, 0, :, t * P:(t + 1) * P], ALU.mult, ALU.subtract).then_inc(key_lo, 1)

            def lower_values(g):
                dve.wait_ge(value_hi, g + 1)
                dve.scalar_tensor_tensor(VV[:, g * GT:(g + 1) * GT, 1, :], value_homes[value_home(g)], col(G_V),
                                         VV[:, g * GT:(g + 1) * GT, 0, :], ALU.mult, ALU.subtract).then_inc(value_lo, 1)
            lower_keys(0)
            lower_keys(1)

            att = Chain(dve, dve_att)

            def mask_chunk(t, T, m):
                wide = T[:, m * SC:(m + 1) * SC]
                dve.wait_ge(abs_made, HC * t + m + 1)
                dve.tensor_scalar(p32[:, m % 2, :], p32[:, m % 2, :], col(THR), col(BIG),
                                  ALU.is_lt, ALU.mult).then_inc(hidden_found, 1)
                dve.wait_ge(hidden_found, HC * t + m + 1)
                dve.tensor_tensor(wide, wide, p32[:, m % 2, :], ALU.add).then_inc(scores_masked, 1)
                dve.wait_ge(scores_masked, HC * t + m + 1)
                dve.tensor_reduce(rmax[:, m:m + 1], wide, AX_X, ALU.max).then_inc(max_chunk, 1)

            def lower_probs(t, m):
                dve.wait_ge(p_hi, HC * t + m + 1)
                dve.tensor_tensor(phl[:, 1, m * SC:(m + 1) * SC], p32[:, m % 2, :],
                                  phl[:, 0, m * SC:(m + 1) * SC], ALU.subtract).then_inc(p_lo, 1)

            FIRST_SPLIT_AFTER = {2: 0, 3: 1, 5: 2, 6: 3}

            def lower_context(a):
                dve.wait_ge(o_hi, idx(a) + 1)
                dve.tensor_tensor(ohl[:, 1], o_in, ohl[:, 0], ALU.subtract).then_inc(o_lo, 1)

            def inverse_of_sum(t):
                dve.wait_ge(exp_made, HC * t + HC)
                dve.tensor_reduce(linv[:, 0:1], rsum[:], AX_X, ALU.add).then_inc(sum_made, 1)
                dve.wait_ge(sum_made, t + 1)
                dve.reciprocal(linv[:, 1:2], linv[:, 0:1]).then_inc(inverse_made, 1)
                dve.wait_ge(inverse_made, t + 1)

            def attention_step(s, c):
                if s:
                    t = idx(s)
                    T = tt[s[1]]
                    second = isinstance(t, int) and t == 1
                    dve.wait_ge(adj_in[s[1]], 16 * s[0] + 16)
                    for n in range(CH):
                        if not c and n + 2 < NG:
                            lower_keys(n + 2)
                        dve.wait_ge(scores_full, CH * t + n + 1)
                        chunk = T[:, n * D:(n + 1) * D]
                        dve.scalar_tensor_tensor(chunk, bank(n % 4), r_s[:, bass.ds(t, 1)], chunk,
                                                 ALU.add, ALU.mult).then_inc(scores_scaled, 1)
                        if isinstance(t, int) and (t, n) in VALUES_AFTER:
                            if VALUES_AFTER[t, n] not in POOL_VALUES:
                                lower_values(VALUES_AFTER[t, n])
                        if second and n in FIRST_SPLIT_AFTER:
                            lower_probs(0, FIRST_SPLIT_AFTER[n])
                        if n % 2 == 0 and n and not second:
                            mask_chunk(t, T, n // 2 - 1)
                    if second:
                        inverse_of_sum(0)
                    for m in range(0 if second else HC - 1, HC):
                        mask_chunk(t, T, m)
                    dve.wait_ge(max_chunk, HC * t + HC)
                    att.rebase(2 * t)
                    att.mark(dve.tensor_reduce(nbias[:, 0:1], rmax[:], AX_X, ALU.max))
                    att.settle()
                    att.mark(dve.tensor_scalar(nbias[:, 1:2], nbias[:, 0:1], col(I_G), -1.0, ALU.mult, ALU.mult))
                    att.settle()
                    dve.tensor_scalar(nbias[:, 2:3], nbias[:, 1:2], P_SHIFT, None, ALU.add).then_inc(shift_made, 1)
                if s and c:
                    for m in range(HC):
                        lower_probs(idx(s), m)
                if not s:
                    lower_context((0, 0))
                if c:
                    dve.wait_ge(context_full, idx(c) + 1)
                    wait_from(dve, context_stored, 16 * idx(c))
                    dve.tensor_scalar(o32, bank(6), linv[:, 1:2], None, ALU.mult).then_inc(context_made, 1)
                if s and c:
                    inverse_of_sum(idx(s))
            attention_steps(dve, attention_step)

            dve.wait_ge(proj_w_in, 48)
            proj = Chain(dve, dve_proj)
            PER4 = 5

            def support_lower(e, s):
                t = GT * idx(e) + s
                dve.wait_ge(support_hi, t + 1)
                home = SUP[:, bass.ds(t, 1)]
                dve.scalar_tensor_tensor(home[:, :, 1, :].rearrange("p t d -> p (t d)"), bank(6 + s % 2), SUPPORT_SCALE,
                                         home[:, :, 0, :].rearrange("p t d -> p (t d)"), ALU.mult, ALU.subtract).then_inc(support_lo, 1)

            def projection_step(a, g, d, e):
                def first_x1(s):
                    k, X = idx(g), xs[g[1]]
                    if s == 0:
                        dve.wait_ge(xb_made, GT * k + GT)
                    dve.wait_ge(proj_full, GT * k + s + 1)
                    dve.scalar_tensor_tensor(X[:, s, :], bank(4 + s % 2), col(I_O), X[:, s, :],
                                             ALU.mult, ALU.add).then_inc(x1_made, 1)

                def statistics(s):
                    dve.wait_ge(x1_made, GT * idx(g) + s + 1)
                    return dve.bn_stats(stats[:, s, :], xs[g[1]][:, s, :])
                if a and g:
                    lower_context(a)
                if g:
                    first_x1(0)
                    first_x1(1)
                    statistics(0)
                if d:
                    dve.wait_ge(h2_hi, idx(d) + 1)
                    dve.scalar_tensor_tensor(h2hl[:, 1].rearrange("p s d -> p (s d)"), xs[d[1]].rearrange("p s d -> p (s d)"), 0.0,
                                             h2hl[:, 0].rearrange("p s d -> p (s d)"), ALU.max, ALU.subtract).then_inc(h2_lo, 1)
                if g:
                    k, X = idx(g), xs[g[1]]
                    proj.rebase(PER4 * k)
                    first_x1(2)
                    statistics(1)
                    statistics(2)
                    first_x1(3)
                    proj.mark(statistics(3))
                    proj.settle()
                    proj.mark(dve.memset(rs[:], 0.0))
                    for s in range(GT):
                        last = dve.bn_aggr(mv[:, s, :], stats[:, s, :])
                    proj.mark(last)
                    proj.settle()
                    dve.tensor_scalar(mv[:, :, 1], mv[:, :, 1], EPS, None, ALU.add).then_inc(var4_made, 1)
                    dve.wait_ge(std4_made, k + 1)
                    proj.mark(dve.reciprocal(rs[:], rs[:]))
                    proj.settle()
                    proj.mark(dve.tensor_scalar(rs[:], rs[:], H_SCALE, None, ALU.mult))
                    proj.settle()
                    dve.wait_ge(x1b_made, GT * k + GT)
                    for s in range(GT):
                        dve.tensor_scalar(X[:, s, :], X[:, s, :], mv[:, s, 0:1], rs[:, s:s + 1],
                                          ALU.subtract, ALU.mult).then_inc(xn4_made, 1)
                    assert proj.k == PER4
                if e:
                    for s in range(GT):
                        support_lower(e, s)
            projection_steps(dve, projection_step)

            def conv_round(j, b):
                t = 2 * j + b
                dve.wait_ge(adj5_in[b], 16 * j + 16)
                if not isinstance(j, int) or t:
                    dve.wait_ge(aT_made, 4 * t - 4)
                wait_from(dve, adj_compared, t)
                dve.tensor_copy(a_bf[:, b, :], tt[b]).then_inc(adj_rounded, 1)

            def conv_compare(j, b):
                t = 2 * j + b
                dve.wait_ge(adj_rounded, t + 1)
                dve.scalar_tensor_tensor(unequal, tt[b], 0.0, a_bf[:, b, :], ALU.add, ALU.not_equal,
                                         accum_out=miss[:, bass.ds(t, 1)]).then_inc(adj_compared, 1)

            def conv_step(j, b):
                conv_round(j, b)
                conv_compare(j, b)

            def conv_out(j, b):
                t = 2 * j + b
                dve.wait_ge(conv_full, t + 1)
                dve.wait_ge(x1_loaded[b], 16 * j + 16)
                wait_from(dve, out_stored[b], 16 * j)
                dve.scalar_tensor_tensor(o_out[b], bank(6 + b), col(I_S), x1_in[b], ALU.mult, ALU.add).then_inc(out_made, 1)

            def conv_pair(j):
                conv_step(j, 1)
                conv_out(j, 0)
                conv_step(j + 1, 0)
                conv_out(j, 1)
            dve.wait_ge(proj_full, NT)
            dve.wait_ge(oT_made, NT)
            conv_round(0, 0)
            projection_step(None, None, None, (NG // 2 - 1, 1))
            conv_compare(0, 0)
            conv_pair(0)
            with dve.Fori(1, NT // 2 - 1) as j:
                conv_pair(j)
            conv_step(NT // 2 - 1, 1)
            conv_out(NT // 2 - 1, 0)
            conv_out(NT // 2 - 1, 1)

            dve.wait_ge(adj_compared, NT)
            dve.tensor_reduce(miss2[:, 0:1], miss[:], AX_X, ALU.add).then_inc(misses_summed, 1)
            dve.wait_ge(misses_shared, 1)
            dve.tensor_scalar(flag[:], miss2[:, 1:2], 1.0, None, ALU.min).then_inc(flag_made, 1)
            dve.wait_ge(flag_made, 1)
            with dve.If(dve.value_load(flag[0:1, 0:1], min_val=0, max_val=1) > 0):
                dve.tensor_tensor(sup32, SUP[:, :, 0, :], SUP[:, :, 1, :], ALU.add).then_inc(sup32_made, 1)

                def rest_step(t):
                    dve.wait_ge(adj6_in, 16 * t + 16)
                    dve.tensor_copy(a_bf[:, 0, :], tt[0]).then_inc(rounded6, 1)
                    dve.wait_ge(rounded6, t + 1)
                    dve.tensor_tensor(tt[1], tt[0], a_bf[:, 0, :], ALU.subtract).then_inc(rest_made, 1)
                    dve.wait_ge(rest_full, t + 1)
                    dve.wait_ge(fix_loaded, 16 * t + 16)
                    wait_from(dve, fix_stored, 16 * t)
                    dve.scalar_tensor_tensor(fix_out, bank(6), col(I_S), fix_in, ALU.mult, ALU.add).then_inc(fix_made, 1)
                rest_step(0)
                with dve.Fori(1, NT) as t:
                    rest_step(t)


_INS = ["x", "adj", "L0_gnn_key", "L0_gnn_value", "L0_gnn_Wq", "L0_gnn_bq", "L0_gnn_Wk", "L0_gnn_bk",
        "L0_gnn_Wv", "L0_gnn_bv", "L0_gnn_Wm", "L0_gnn_bm", "L1_gnn_weight", "L1_gnn_bias"]


def kernel(**inputs):
    import numpy as _np
    import concourse.bacc as _bacc
    from concourse import mybir as _mybir
    from concourse.bass_utils import run_bass_kernel_spmd as _run

    nc = _bacc.Bacc("TRN2", target_bir_lowering=False, num_devices=1)
    arrays, args = {}, []
    for name in _INS:
        a = _np.ascontiguousarray(inputs[name])
        arrays[f"in_{name}_dram"] = a
        args.append(nc.dram_tensor(f"in_{name}_dram", a.shape, _mybir.dt.from_np(a.dtype), kind="ExternalInput").ap())
    args.append(nc.dram_tensor("out_dram", (N, D), F32, kind="ExternalOutput").ap())
    program(nc, *args)
    r = _run(nc, [arrays], core_ids=[0])
    return r.results[0]["out_dram"]
```
